# Optimizing a Trainium2 kernel written in Bass

```python
import numpy as np
import jax
import jax.numpy as jnp

def _softmax(x, axis=-1):
    return jax.nn.softmax(x, axis=axis)

def _gelu(x):
    return jax.nn.gelu(x, approximate=True)

def _silu(x):
    return jax.nn.silu(x)

def _sigmoid(x):
    return jax.nn.sigmoid(x)

def _layernorm(x, axis=-1, eps=1e-05):
    m = jnp.mean(x, axis=axis, keepdims=True)
    v = jnp.var(x, axis=axis, keepdims=True)
    return (x - m) / jnp.sqrt(v + eps)

def _scatter_add(tgt, idx, src, axis=0):
    return tgt.at[idx].add(src)

def _segment_sum(src, seg, n):
    return jax.ops.segment_sum(src, seg, n)
kernel_name = 'mk_vit_tower_d1_tok_img1024_r4_32e8fe'

def setup_inputs(seed: int=0):
    np.random.seed(seed)
    _w = jnp.asarray

    def _rec_inputs():
        import jax
        import jax.numpy as jnp
        _rk = jax.random.key(seed)
        x = -0.00016672 + 0.999947 * jax.random.normal(jax.random.fold_in(_rk, 1), (32, 3, 112, 112), jnp.float32)
        return x
    x = _rec_inputs()

    def _L0_tok_setup():
        import jax, jax.numpy as jnp
        import numpy as np
        PATCH = 16
        D_MODEL = 256

        def patchify(imgs, p):
            n, c, H, W = imgs.shape
            h, w = (H // p, W // p)
            x = imgs.reshape(n, c, h, p, w, p)
            x = jnp.einsum('nchpwq->nhwpqc', x)
            return x.reshape(n, h * w, p * p * c)
        key = jax.random.key(seed)
        k1, k2, k3 = jax.random.split(key, 3)
        val = jax.random.normal(k1, (64, 3, 96, 96), dtype=jnp.float32)
        in_dim = PATCH * PATCH * 3
        bound = 1.0 / np.sqrt(in_dim)
        W = jax.random.uniform(k2, (D_MODEL, in_dim), dtype=jnp.float32, minval=-bound, maxval=bound)
        b = jax.random.uniform(k3, (D_MODEL,), dtype=jnp.float32, minval=-bound, maxval=bound)
        return {'val': val, 'W': W, 'b': b}
    _L0_tok_all = _L0_tok_setup()
    _L0_tok_in = {k: v for k, v in _L0_tok_all.items() if k in ('W', 'b')}
    del _L0_tok_all

    def _L0_attn_setup():
        import jax, jax.numpy as jnp
        import numpy as np
        import math
        B, L, D, MAXL = (4, 1024, 256, 4096)

        def _shift1(a):
            return jnp.concatenate([jnp.zeros_like(a[:, :1]), a[:, :-1]], axis=1)
        key = jax.random.key(seed)
        ks = jax.random.split(key, 12)
        s = 0.02

        def w(k, shape):
            return jax.random.normal(k, shape, jnp.float32) * s
        return {'x': jax.random.normal(ks[0], (B, L, D), jnp.float32), 'pos_phases': jax.random.normal(ks[1], (MAXL, D), jnp.float32) * math.pi, 'Wpv': w(ks[2], (D, D)), 'bpv': jnp.zeros((D,), jnp.float32), 'Wk': w(ks[3], (D, D)), 'bk': jnp.zeros((D,), jnp.float32), 'Wkv': w(ks[4], (D, D)), 'bkv': jnp.zeros((D,), jnp.float32), 'Wg1': w(ks[5], (2 * D, D)), 'bg1': jnp.zeros((D,), jnp.float32), 'Wg2': w(ks[6], (D, 1)), 'bg2': jnp.zeros((1,), jnp.float32), 'Wb1': w(ks[7], (D, D // 2)), 'bb1': jnp.zeros((D // 2,), jnp.float32), 'Wb2': w(ks[8], (D // 2, 2)), 'bb2': jnp.zeros((2,), jnp.float32), 'ln_g': jnp.ones((D,), jnp.float32), 'ln_b': jnp.zeros((D,), jnp.float32), 'Wo': w(ks[9], (D, D)), 'bo': jnp.zeros((D,), jnp.float32)}
    _L0_attn_all = _L0_attn_setup()
    _L0_attn_in = {k: v for k, v in _L0_attn_all.items() if k in ('pos_phases', 'Wpv', 'bpv', 'Wk', 'bk', 'Wkv', 'bkv', 'Wg1', 'bg1', 'Wg2', 'bg2', 'Wb1', 'bb1', 'Wb2', 'bb2', 'ln_g', 'ln_b', 'Wo', 'bo')}
    del _L0_attn_all

    def _L0_ffn_setup():
        import jax, jax.numpy as jnp
        import numpy as np
        EPS = 1e-08

        def _ternary_linear(x, w):
            alpha = jnp.mean(jnp.abs(w))
            w_t = jnp.sign(w) * (jnp.abs(w) > 0.5 * alpha).astype(w.dtype)
            w_q = w + jax.lax.stop_gradient(w_t - w)
            d = x.shape[-1]
            rms = jnp.sqrt(jnp.sum(x * x, axis=-1, keepdims=True)) / jnp.sqrt(jnp.asarray(d, x.dtype))
            x_norm = x / (rms + EPS)
            return jnp.einsum('bsd,fd->bsf', x_norm, w_q)
        key = jax.random.key(seed)
        k1, k2, k3 = jax.random.split(key, 3)
        d_model, d_ff = (256, 1024)
        B, S = (4, 1024)
        x = jax.random.normal(k1, (B, S, d_model), dtype=jnp.float32)
        w_up = jax.random.normal(k2, (d_ff, d_model), dtype=jnp.float32) * 0.02
        w_down = jax.random.normal(k3, (d_model, d_ff), dtype=jnp.float32) * 0.02
        return {'x': x, 'w_up': w_up, 'w_down': w_down}
    _L0_ffn_all = _L0_ffn_setup()
    _L0_ffn_in = {k: v for k, v in _L0_ffn_all.items() if k in ('w_up', 'w_down')}
    del _L0_ffn_all
    return {'x': x, 'L0_tok_W': _L0_tok_in['W'], 'L0_tok_b': _L0_tok_in['b'], 'L0_attn_pos_phases': _L0_attn_in['pos_phases'], 'L0_attn_Wpv': _L0_attn_in['Wpv'], 'L0_attn_bpv': _L0_attn_in['bpv'], 'L0_attn_Wk': _L0_attn_in['Wk'], 'L0_attn_bk': _L0_attn_in['bk'], 'L0_attn_Wkv': _L0_attn_in['Wkv'], 'L0_attn_bkv': _L0_attn_in['bkv'], 'L0_attn_Wg1': _L0_attn_in['Wg1'], 'L0_attn_bg1': _L0_attn_in['bg1'], 'L0_attn_Wg2': _L0_attn_in['Wg2'], 'L0_attn_bg2': _L0_attn_in['bg2'], 'L0_attn_Wb1': _L0_attn_in['Wb1'], 'L0_attn_bb1': _L0_attn_in['bb1'], 'L0_attn_Wb2': _L0_attn_in['Wb2'], 'L0_attn_bb2': _L0_attn_in['bb2'], 'L0_attn_ln_g': _L0_attn_in['ln_g'], 'L0_attn_ln_b': _L0_attn_in['ln_b'], 'L0_attn_Wo': _L0_attn_in['Wo'], 'L0_attn_bo': _L0_attn_in['bo'], 'L0_ffn_w_up': _L0_ffn_in['w_up'], 'L0_ffn_w_down': _L0_ffn_in['w_down']}

def reference(x, L0_tok_W, L0_tok_b, L0_attn_pos_phases, L0_attn_Wpv, L0_attn_bpv, L0_attn_Wk, L0_attn_bk, L0_attn_Wkv, L0_attn_bkv, L0_attn_Wg1, L0_attn_bg1, L0_attn_Wg2, L0_attn_bg2, L0_attn_Wb1, L0_attn_bb1, L0_attn_Wb2, L0_attn_bb2, L0_attn_ln_g, L0_attn_ln_b, L0_attn_Wo, L0_attn_bo, L0_ffn_w_up, L0_ffn_w_down):
    import jax
    import jax.numpy as jnp

    def _L0_tok_ref(val, W, b):
        import jax, jax.numpy as jnp
        import numpy as np
        PATCH = 16
        D_MODEL = 256

        def patchify(imgs, p):
            n, c, H, W = imgs.shape
            h, w = (H // p, W // p)
            x = imgs.reshape(n, c, h, p, w, p)
            x = jnp.einsum('nchpwq->nhwpqc', x)
            return x.reshape(n, h * w, p * p * c)
        patches = patchify(val, PATCH)
        return jnp.einsum('nld,md->nlm', patches, W) + b

    def _L0_attn_ref(x, pos_phases, Wpv, bpv, Wk, bk, Wkv, bkv, Wg1, bg1, Wg2, bg2, Wb1, bb1, Wb2, bb2, ln_g, ln_b, Wo, bo):
        import jax, jax.numpy as jnp
        import numpy as np
        import math
        B, L, D, MAXL = (4, 1024, 256, 4096)

        def _shift1(a):
            return jnp.concatenate([jnp.zeros_like(a[:, :1]), a[:, :-1]], axis=1)
        Bq, Lq, Dq = x.shape
        sqrtD = jnp.sqrt(jnp.float32(Dq))
        pp = pos_phases[:Lq]
        pos_cos, pos_sin = (jnp.cos(pp), jnp.sin(pp))
        pos_values = x @ Wpv + bpv
        pos_mem_cos = jnp.cumsum(pos_cos * pos_values, axis=1)
        pos_mem_sin = jnp.cumsum(pos_sin * pos_values, axis=1)
        pos_ret = (pos_cos * pos_mem_cos + pos_sin * pos_mem_sin) / sqrtD
        key_ph = jnp.tanh(x @ Wk + bk) * jnp.pi
        key_cos, key_sin = (jnp.cos(key_ph), jnp.sin(key_ph))
        kv_values = x @ Wkv + bkv
        x_shifted = _shift1(x)
        gate_in = jnp.concatenate([x, x_shifted], axis=-1)
        gh = jax.nn.gelu(gate_in @ Wg1 + bg1, approximate=False)
        value_gates = jax.nn.sigmoid(gh @ Wg2 + bg2)
        kc_s = _shift1(key_cos)
        ks_s = _shift1(key_sin)
        kv_mem_cos = jnp.cumsum(kc_s * kv_values * value_gates, axis=1)
        kv_mem_sin = jnp.cumsum(ks_s * kv_values * value_gates, axis=1)
        gate_cumsum = jnp.maximum(jnp.cumsum(value_gates, axis=1), 1.0)
        kv_ret = (key_cos * kv_mem_cos + key_sin * kv_mem_sin) / (jnp.sqrt(gate_cumsum) * sqrtD)
        bh = jax.nn.gelu(x @ Wb1 + bb1, approximate=False)
        bw = jax.nn.softmax(bh @ Wb2 + bb2, axis=-1)
        blended = bw[..., 0:1] * pos_ret + bw[..., 1:2] * kv_ret
        mu = jnp.mean(blended, axis=-1, keepdims=True)
        var = jnp.var(blended, axis=-1, keepdims=True)
        ln = (blended - mu) / jnp.sqrt(var + 1e-05) * ln_g + ln_b
        return x + ln @ Wo + bo

    def _L0_ffn_ref(x, w_up, w_down):
        import jax, jax.numpy as jnp
        import numpy as np
        EPS = 1e-08

        def _ternary_linear(x, w):
            alpha = jnp.mean(jnp.abs(w))
            w_t = jnp.sign(w) * (jnp.abs(w) > 0.5 * alpha).astype(w.dtype)
            w_q = w + jax.lax.stop_gradient(w_t - w)
            d = x.shape[-1]
            rms = jnp.sqrt(jnp.sum(x * x, axis=-1, keepdims=True)) / jnp.sqrt(jnp.asarray(d, x.dtype))
            x_norm = x / (rms + EPS)
            return jnp.einsum('bsd,fd->bsf', x_norm, w_q)
        h = jax.nn.gelu(_ternary_linear(x, w_up), approximate=False)
        return _ternary_linear(h, w_down)
    h = _L0_tok_ref(x, L0_tok_W, L0_tok_b)
    h = h + _L0_attn_ref(_layernorm(h, axis=-1), L0_attn_pos_phases, L0_attn_Wpv, L0_attn_bpv, L0_attn_Wk, L0_attn_bk, L0_attn_Wkv, L0_attn_bkv, L0_attn_Wg1, L0_attn_bg1, L0_attn_Wg2, L0_attn_bg2, L0_attn_Wb1, L0_attn_bb1, L0_attn_Wb2, L0_attn_bb2, L0_attn_ln_g, L0_attn_ln_b, L0_attn_Wo, L0_attn_bo)
    h = h + _L0_ffn_ref(_layernorm(h, axis=-1), L0_ffn_w_up, L0_ffn_w_down)
    return h

_drawn_inputs = setup_inputs


def setup_inputs(seed=0):
    import zlib

    import numpy as np

    out = dict(_drawn_inputs(seed))
    spreads = {'L0_attn_bpv': (0.0, 0.1),
     'L0_attn_bk': (0.0, 0.8),
     'L0_attn_bkv': (0.0, 0.1),
     'L0_attn_bg1': (0.0, 0.8),
     'L0_attn_bb1': (0.0, 0.8),
     'L0_attn_bb2': (0.0, 0.797),
     'L0_attn_ln_g': (1.0, 0.2),
     'L0_attn_ln_b': (0.0, 0.432),
     'L0_attn_bo': (0.0, 0.1)}
    factors = {'L0_attn_Wg1': 8.0, 'L0_attn_Wg2': 8.0, 'L0_attn_Wb1': 8.0, 'L0_attn_Wb2': 8.0}
    for name, (base, spread) in spreads.items():
        noise = np.random.default_rng([zlib.crc32(name.encode()), seed]).standard_normal(out[name].shape)
        drawn = base * np.exp(spread * noise) if base else spread * noise
        out[name] = jnp.asarray(drawn.astype(out[name].dtype))
    for name, factor in factors.items():
        out[name] = (out[name] * factor).astype(out[name].dtype)
    return out
```

```python
from contextlib import ExitStack

import concourse.bass as bass
from concourse import mybir

ALU = mybir.AluOpType
ACT = mybir.ActivationFunctionType
F32 = mybir.dt.float32
F16 = mybir.dt.float16

PI = 3.14159265358979
WSCALE = 256.0
TWO_PI_PARTS = (6.28125, 0.0019350051879882812, 3.0199160514e-07)
ROUND_MAGIC = 12582912.0
PI_BELOW = 3.1415925
LN_EPS = 1e-5
RMS_EPS = 1e-8


def vit_block_program(nc, x, tok_W, tok_b, phases, Wpv, bpv, Wk, bk, Wkv, bkv, Wg1, bg1, Wg2, bg2,
                      Wb1, bb1, Wb2, bb2, ln_g, ln_b, Wo, bo, w_up, w_down, out):
    NIMG, C, HW, _ = x.shape
    PATCH = 16
    SIDE = HW // PATCH
    L = SIDE * SIDE
    D = tok_W.shape[0]
    DH = D // 128
    F = w_up.shape[0]
    FC = F // 128
    IPG = 8
    G = NIMG // IPG
    TG = IPG * L
    TT = 2 * L
    NT = TG // TT
    ROWS = IPG * SIDE
    PH = PATCH * PATCH // 128
    ODD = 64
    PIX = PATCH * HW
    KC = C * PH
    PADL = L + 1
    INV = 1.0 / WSCALE
    PV, KEY, KV, G1, BH, WO = 0, 2, 4, 6, 10, 11
    NSLOT = 13

    with ExitStack() as ctx:
        def sb(name, shape, dt=F32):
            return ctx.enter_context(nc.sbuf_tensor(name, shape, dt))

        def sem(name):
            return ctx.enter_context(nc.semaphore(name))

        bank = [ctx.enter_context(nc.psum_tensor(f"pair{i}", [128, 2, 512], F32)) for i in range(4)]
        P01, P23, P45, P67 = bank

        arena = sb("arena", [128, 2 * C * PIX])
        x_raw = [arena[:, c * PIX:(c + 1) * PIX] for c in range(C)]
        x_pat = [arena[:, (C + c) * PIX:(C + c + 1) * PIX] for c in range(C)]
        n = DH * TG
        u_pc, u_ps, u_kc, u_ks, m_pc, m_ps, m_kc, m_ks = [arena[:, i * n:(i + 1) * n] for i in range(8)]
        ghl = arena[:, 8 * n:8 * n + FC * TG].bitcast(F16).rearrange("p (f s t) -> p f s t", f=FC, s=2)

        tokw_f = sb("tokw_f", [128, KC * D])
        gelu_ring = [tokw_f[:, i * TG:(i + 1) * TG] for i in range(3)]
        tokw_h = sb("tokw_h", [128, KC * D], F16)
        tokw_l = sb("tokw_l", [128, KC * D], F16)
        x_h = sb("x_h", [128, KC, TG], F16)
        x_l = sb("x_l", [128, KC, TG], F16)
        aw_f = sb("aw_f", [128, NSLOT * 256])
        out_ring = [aw_f[0:TT, i * NT * D:(i + 1) * NT * D] for i in range(2)]
        aw_h = sb("aw_h", [128, NSLOT * 256], F16)
        aw_l = sb("aw_l", [128, NSLOT * 256], F16)
        up_f = sb("up_f", [128, FC * D])
        dn_f = sb("dn_f", [128, DH * F])
        above = sb("above", [128, FC * D], F16)
        up_t = sb("up_t", [128, FC * D], F16)
        dn_t = sb("dn_t", [128, DH * F], F16)
        upT = sb("upT", [128, DH, F], F16)
        dnT = sb("dnT", [128, FC, D], F16)
        hF = [sb(f"hF{i}", [128, DH, TG]) for i in range(2)]
        ring_T = [sb(f"ring_T{i}", [TT, NT * D]) for i in range(2)]
        x1_h = [sb(f"x1_h{g}", [128, DH, IPG, PADL], F16) for g in range(G)]
        x1_l = [sb(f"x1_l{g}", [128, DH, IPG, PADL], F16) for g in range(G)]
        flat = lambda a: a[:, :, :, :].rearrange("p h i l -> p (h i l)")[:, 0:DH * TG].rearrange("p (h t) -> p h t", h=DH)
        x2_h = [flat(x1_h[g]) for g in range(G)]
        x2_l = [flat(x1_l[g]) for g in range(G)]
        res = [sb(f"res{g}", [TT, NT * D]) for g in range(G)]
        x_h32, x_l32 = (a[:, :, :].rearrange("p k t -> p (k t)").bitcast(F32) for a in (x_h, x_l))
        gh = x_h32[:, 0:DH * TG].rearrange("p (h t) -> p h t", h=DH)
        bh = x_h32[:, DH * TG:(DH + 1) * TG]
        th = x_l32[:, 0:DH * TG].rearrange("p (h t) -> p h t", h=DH)
        gate_e = x_l32[:, DH * TG:(DH + 1) * TG]
        th_abs = sb("th_abs", [128, DH, TG])
        key_c = [sb(f"key_c{i}", [128, DH, IPG, PADL]) for i in range(2)]
        key_s = [sb(f"key_s{i}", [128, DH, IPG, PADL]) for i in range(2)]
        gate = sb("gate", [128, TG])
        gate_sum = [sb(f"gate_sum{i}", [128, TG]) for i in range(2)]
        kvg = sb("kvg", [128, DH, TG])
        inside = sb("inside", [128, DH * TG])
        z_h = sb("z_h", [128, DH, TG], F16)
        z_l = sb("z_l", [128, DH, TG], F16)
        NV = 17
        vrows = sb("vrows", [NV, 128])
        vec = sb("vec", [128, NV])
        vec_s = sb("vec_s", [128, NV])
        srow = sb("srow", [1, 3])
        borow = sb("borow", [1, D])
        small = sb("small", [128, 4])
        wb2 = sb("wb2", [128, 2])
        wg2b = sb("wg2b", [128, DH, 128])
        lnbb = sb("lnbb", [128, DH, TT])
        ident = sb("ident", [128, 128])
        ident16 = sb("ident16", [128, 128], F16)
        ones = sb("ones", [128, 128])
        gmask = sb("gmask", [TT, 2, TT])
        half_pi = sb("half_pi", [128, 1])
        p_minus_half = sb("p_minus_half", [TT, NT])
        p_half = sb("p_half", [TT, 2 * NT])
        p_minus_one = sb("p_minus_one", [TT, NT])
        kvg_flat, abs_flat = (a[:, :, :].rearrange("p h t -> p (h t)") for a in (kvg, th_abs))
        ph, ph_k, ph_abs = [kvg_flat[0:L, i * D:(i + 1) * D] for i in range(3)]
        ph_cs = abs_flat[0:L, 0:2 * D].rearrange("p (a d) -> p a d", a=2)
        table = sb("table", [128, 2, DH, L])
        bias_T = sb("bias_T", [TT, D])
        abs_sum = sb("abs_sum", [128, 2])
        thr = sb("thr", [128, 4])
        st = sb("st", [TT, NT, 6])
        mv = sb("mv", [TT, NT, 2])
        ve = sb("ve", [TT, NT])
        rstd = sb("rstd", [TT, NT])
        nmr = sb("nmr", [TT, NT])
        zst = sb("zst", [TT, NT, 6])
        zmv = sb("zmv", [TT, NT, 2])
        zve = sb("zve", [TT, NT])
        zrs = sb("zrs", [TT, NT])
        znm = sb("znm", [TT, NT])
        hst = sb("hst", [TT, NT, 6])
        hmv = sb("hmv", [TT, NT, 2])
        hvv = sb("hvv", [TT, 2, NT])
        hsq = sb("hsq", [TT, 2, NT])
        hf = sb("hf", [TT, NT])
        hnm = sb("hnm", [TT, NT])
        zl = sb("zl", [TT, NT, 2])
        zmax = sb("zmax", [TT, NT, 1])
        ze = sb("ze", [TT, NT, 2])
        zsum = sb("zsum", [TT, NT])
        bw = [sb(f"bw{i}", [TT, 2, NT]) for i in range(2)]
        gc = sb("gc", [TT, NT])
        gcr = sb("gcr", [TT, NT])
        kvw = sb("kvw", [TT, NT])
        junk = sb("junk", [TT, 2 * TT])
        ss = sb("ss", [TT, NT])
        sr = sb("sr", [TT, NT])
        sf = sb("sf", [TT, NT])

        x_loaded = [sem(f"x_loaded{c}") for c in range(C)]
        x_sorted = sem("x_sorted")
        tokw_loaded = sem("tokw_loaded")
        tokwT_in_psum = sem("tokwT_in_psum")
        vec_loaded = sem("vec_loaded")
        aw_loaded = sem("aw_loaded")
        ph_loaded = sem("ph_loaded")
        up_loaded = sem("up_loaded")
        dn_loaded = sem("dn_loaded")
        out_stored = [sem(f"out_stored{i}") for i in range(2)]
        ident_done = sem("ident_done")
        consts_done = sem("consts_done")
        pool_step = sem("pool_step")
        dve_step = sem("dve_step")
        act_step = sem("act_step")
        vec_in_psum = sem("vec_in_psum")
        vec_done = sem("vec_done")
        tokw_head = sem("tokw_head")
        tokw_done = sem("tokw_done")
        ph_reduced = sem("ph_reduced")
        ph_cs_done = sem("ph_cs_done")
        abs_sum_done = sem("abs_sum_done")
        setup_in_psum = sem("setup_in_psum")
        setup_done = sem("setup_done")
        aw_done = sem("aw_done")
        tern_done = sem("tern_done")
        ternT_in_psum = sem("ternT_in_psum")
        ternT_done = sem("ternT_done")
        xT_in_psum = sem("xT_in_psum")
        x_head = sem("x_head")
        x_rest = sem("x_rest")
        tok_chunk = sem("tok_chunk")
        hF_done = sem("hF_done")
        hT_in_psum = sem("hT_in_psum")
        ve_done = sem("ve_done")
        rstd_done = sem("rstd_done")
        nmr_done = sem("nmr_done")
        x1T_done = sem("x1T_done")
        res_done = sem("res_done")
        res_biased = sem("res_biased")
        x1F_in_psum = sem("x1F_in_psum")
        x1_head = sem("x1_head")
        x1_rest = sem("x1_rest")
        g1_in_psum = sem("g1_in_psum")
        bh_in_psum = sem("bh_in_psum")
        key_in_psum = sem("key_in_psum")
        pv_in_psum = sem("pv_in_psum")
        gate_in_psum = sem("gate_in_psum")
        z_in_psum = sem("z_in_psum")
        kv_in_psum = sem("kv_in_psum")
        gh_done = sem("gh_done")
        bh_done = sem("bh_done")
        th_done = sem("th_done")
        th_abs_done = sem("th_abs_done")
        gate_e_done = sem("gate_e_done")
        zlog_done = sem("zlog_done")
        ze_done = sem("ze_done")
        key_cs_done = sem("key_cs_done")
        bw_done = sem("bw_done")
        u_pos_done = sem("u_pos_done")
        gate_done = sem("gate_done")
        gate_sum_done = sem("gate_sum_done")
        kvg_done = sem("kvg_done")
        u_kv_done = sem("u_kv_done")
        m_pos_done = sem("m_pos_done")
        m_kv_done = sem("m_kv_done")
        pos_ret_done = sem("pos_ret_done")
        kv_ret_done = sem("kv_ret_done")
        gc_in_psum = sem("gc_in_psum")
        gc_done = sem("gc_done")
        gcr_done = sem("gcr_done")
        posT_in_psum = sem("posT_in_psum")
        kvT_in_psum = sem("kvT_in_psum")
        pos_scaled = sem("pos_scaled")
        blend_done = sem("blend_done")
        zve_done = sem("zve_done")
        zrs_done = sem("zrs_done")
        znm_done = sem("znm_done")
        zT_done = sem("zT_done")
        zF_in_psum = sem("zF_in_psum")
        z_head = sem("z_head")
        z_rest = sem("z_rest")
        wo_in_psum = sem("wo_in_psum")
        h2_done = sem("h2_done")
        hvv_done = sem("hvv_done")
        hf_done = sem("hf_done")
        hnm_done = sem("hnm_done")
        x2T_done = sem("x2T_done")
        x2F_in_psum = sem("x2F_in_psum")
        x2_head = sem("x2_head")
        x2_rest = sem("x2_rest")
        up_in_psum = sem("up_in_psum")
        gelu_done = sem("gelu_done")
        g_head = sem("g_head")
        g_rest = sem("g_rest")
        gram_in_psum = sem("gram_in_psum")
        ss_done = sem("ss_done")
        sf_done = sem("sf_done")
        down_in_psum = sem("down_in_psum")
        out_done = sem("out_done")

        def last_group(g):
            return min(g, G - 1)

        def images(ap):
            return ap.rearrange("p (i l) -> p i l", i=IPG)

        def halves(ap):
            return ap.rearrange("p (h i l) -> p h i l", h=DH, i=IPG)

        def slot(w, s, k=0, width=256):
            return w[:, (s + k) * 256:(s + k) * 256 + width]

        def tiles(pair):
            return pair[0:TT, :, :].rearrange("p b (t d) -> p (b t) d", d=D)

        def flat_T(pair):
            return pair[0:TT, :, :].rearrange("p b n -> p (b n)")

        def tokw_bank(c):
            return P23[:, c, :] if c < 2 else P45[:, 0, :]

        block = ctx.enter_context(nc.Block())

        @block.sync
        def _(sp):
            def load_x(half):
                for c in range(C):
                    if half == 0:
                        sp.dma_start(x_raw[c][ROWS:ODD, :],
                                     x[0:ODD - ROWS, c, 0:PATCH, :].rearrange("n p w -> n (p w)")).then_inc(x_loaded[c], 16)
                    else:
                        sp.wait_ge(x_sorted, c + 1)
                    for b in range(2):
                        g = 2 * half + b
                        src = x[g * IPG:(g + 1) * IPG, c, :, :].rearrange("n (h p) w -> n h (p w)", p=PATCH)
                        sp.dma_start(x_raw[c][b * ODD:b * ODD + ROWS, :], src).then_inc(x_loaded[c], 16)

            for i, v in enumerate((tok_b, bpv, bk, bkv, bg1, None, ln_g, ln_b, None)):
                if v is not None:
                    r = (0, 2, 4, 6, 8, None, 11, 13)[i]
                    sp.dma_start(vrows[r:r + 2, :], v.rearrange("(m p) -> m p", p=128)).then_inc(vec_loaded, 16)
            sp.dma_start(vrows[10:11, :], bb1.rearrange("(m p) -> m p", p=128)).then_inc(vec_loaded, 16)
            sp.dma_start(vrows[15:17, :], Wg2.rearrange("(m p) o -> m (p o)", p=128)).then_inc(vec_loaded, 16)
            sp.dma_start(srow[:, 0:2], bb2.rearrange("(a n) -> a n", a=1)).then_inc(vec_loaded, 16)
            sp.dma_start(srow[:, 2:3], bg2.rearrange("(a n) -> a n", a=1)).then_inc(vec_loaded, 16)
            sp.dma_start(borow[:, :], bo.rearrange("(a n) -> a n", a=1)).then_inc(vec_loaded, 16)
            sp.dma_start(wb2[:, :], Wb2).then_inc(vec_loaded, 16)
            load_x(0)
            sp.dma_start(tokw_f[:, :].rearrange("p (m d) -> p m d", m=DH),
                         tok_W.rearrange("(m p) d -> p m d", p=128)).then_inc(tokw_loaded, 16)
            sp.dma_start(ph[:, :], phases[0:L, :]).then_inc(ph_loaded, 16)
            for w, s, k in ((Wpv, PV, 2), (Wk, KEY, 2), (Wkv, KV, 2), (Wg1, G1, 4), (Wo, WO, 2)):
                sp.dma_start(aw_f[:, s * 256:(s + k) * 256].rearrange("p (k m) -> p k m", k=k),
                             w.rearrange("(k p) m -> p k m", p=128)).then_inc(aw_loaded, 16)
            sp.dma_start(slot(aw_f, BH).rearrange("p (k m) -> p k m", k=2),
                         Wb1.rearrange("(k p) m -> p k m", p=128)).then_inc(aw_loaded, 16)
            sp.dma_start(up_f[:, :].rearrange("p (f d) -> p f d", f=FC),
                         w_up.rearrange("(f p) d -> p f d", p=128)).then_inc(up_loaded, 16)
            sp.dma_start(dn_f[:, :].rearrange("p (h f) -> p h f", h=DH),
                         w_down.rearrange("(h p) f -> p h f", p=128)).then_inc(dn_loaded, 16)
            load_x(1)
            out_v = out.rearrange("(g i) l d -> g (i l) d", g=G)
            for g in range(G):
                sp.wait_ge(out_done, g + 1)
                sp.dma_start(out_v[g].rearrange("(t p) d -> p t d", p=TT),
                             out_ring[g % 2].rearrange("p (t d) -> p t d", t=NT)).then_inc(out_stored[g % 2], 16)
            for i in range(2):
                sp.wait_ge(out_stored[i], 16 * G // 2)

        N_VEC = 13

        @block.gpsimd
        def _(pool):
            steps = [0]

            def chained(ins):
                steps[0] += 1
                ins.then_inc(pool_step, 1)
                pool.wait_ge(pool_step, steps[0])

            chained(nc.gpsimd.memset(ident[:, :], 0.0))
            chained(nc.gpsimd.affine_select(out=ident[:, :], in_=ident[:, :], compare_op=ALU.not_equal, fill=1.0,
                                            base=0, pattern=[[-1, 128]], channel_multiplier=1))
            nc.gpsimd.tensor_copy(ident16[:, :], ident[:, :]).then_inc(ident_done, 1)
            nc.gpsimd.tensor_copy(gmask[:, 0, :], ident[0:TT, 0:TT]).then_inc(consts_done, 1)
            nc.gpsimd.tensor_scalar(gmask[:, 1, :], ident[0:TT, 0:TT], 2.0, None, ALU.mult).then_inc(consts_done, 1)

            def split(a, b):
                w = aw_f[:, a * 256:b * 256]
                chained(nc.gpsimd.tensor_scalar(w, w, WSCALE, None, ALU.mult))
                chained(nc.gpsimd.tensor_copy(aw_h[:, a * 256:b * 256], w))
                nc.gpsimd.tensor_tensor(aw_l[:, a * 256:b * 256], w, aw_h[:, a * 256:b * 256],
                                        ALU.subtract).then_inc(aw_done, 1)

            pool.wait_ge(aw_loaded, 16 * 6)
            split(PV, WO)
            pool.wait_ge(setup_in_psum, 1)
            pool.wait_ge(vec_done, 1)
            for k in range(DH):
                chained(nc.gpsimd.tensor_scalar(slot(aw_f, WO, k), slot(aw_f, WO, k), vec[:, 11 + k:12 + k], None,
                                                ALU.mult))
            split(WO, NSLOT)

            def pow_rstd(g):
                pool.wait_ge(ve_done, g + 1)
                nc.gpsimd.tensor_tensor(rstd[:, :], ve[:, :], p_minus_half[:, :], ALU.pow).then_inc(rstd_done, 1)

            def bias_res(g):
                pool.wait_ge(res_done, g + 1)
                pool.wait_ge(setup_done, 1)
                r = res[g][:, :].rearrange("p (t d) -> p t d", t=NT)
                nc.gpsimd.tensor_tensor(r, r, bias_T[:, :].unsqueeze(1).broadcast_to([TT, NT, D]),
                                        ALU.add).then_inc(res_biased, 1)

            for g in range(G):
                pow_rstd(g)
            for g in range(G):
                bias_res(g)

            def shifted_key_terms(g):
                b = g % 2
                pool.wait_ge(kvg_done, g + 1)
                pool.wait_ge(key_cs_done, g + 1)
                pool.wait_ge(m_kv_done, 2 * g)
                for u, key in ((u_kc, key_c), (u_ks, key_s)):
                    nc.gpsimd.tensor_tensor(halves(u), kvg[:, :, :].rearrange("p h (i l) -> p h i l", i=IPG),
                                            key[b][:, :, :, 0:L], ALU.mult).then_inc(u_kv_done, 1)

            def pow_z(g):
                pool.wait_ge(zve_done, g + 1)
                nc.gpsimd.tensor_tensor(zrs[:, :], zve[:, :], p_minus_half[:, :], ALU.pow).then_inc(zrs_done, 1)

            def pos_ret(g):
                for i, m in enumerate((m_pc, m_ps)):
                    pool.wait_ge(m_pos_done, 2 * g + i + 1)
                    tab = table[:, i, :, :].unsqueeze(2).broadcast_to([128, DH, IPG, L])
                    chained(nc.gpsimd.tensor_tensor(halves(m), halves(m), tab, ALU.mult))
                nc.gpsimd.tensor_tensor(m_pc, m_pc, m_ps, ALU.add).then_inc(pos_ret_done, 1)

            def kv_ret(g):
                for i, (m, key) in enumerate(((m_kc, key_c), (m_ks, key_s))):
                    pool.wait_ge(m_kv_done, 2 * g + i + 1)
                    chained(nc.gpsimd.tensor_tensor(halves(m), halves(m), key[g % 2][:, :, :, 1:PADL], ALU.mult))
                nc.gpsimd.tensor_tensor(m_kc, m_kc, m_ks, ALU.add).then_inc(kv_ret_done, 1)

            def pow_gc(g):
                pool.wait_ge(gc_done, g + 1)
                nc.gpsimd.tensor_tensor(gcr[:, :], gc[:, :], p_minus_half[:, :], ALU.pow).then_inc(gcr_done, 1)

            def pow_h2(g):
                pool.wait_ge(hvv_done, g + 1)
                pool.wait_ge(hf_done, g)
                two = "p a t -> p (a t)"
                chained(nc.gpsimd.tensor_tensor(hsq[:, :, :].rearrange(two), hvv[:, :, :].rearrange(two), p_half[:, :],
                                                ALU.pow))
                chained(nc.gpsimd.tensor_scalar(hsq[:, 1, :], hsq[:, 1, :], RMS_EPS, None, ALU.mult))
                chained(nc.gpsimd.tensor_tensor(hsq[:, 0, :], hsq[:, 0, :], hsq[:, 1, :], ALU.add))
                nc.gpsimd.tensor_tensor(hf[:, :], hsq[:, 0, :], p_minus_one[:, :], ALU.pow).then_inc(hf_done, 1)

            def pow_ss(g):
                pool.wait_ge(ss_done, g + 1)
                pool.wait_ge(sf_done, g)
                chained(nc.gpsimd.tensor_scalar(sr[:, :], ss[:, :], 1.0 / F, None, ALU.mult))
                chained(nc.gpsimd.tensor_tensor(sr[:, :], sr[:, :], p_half[:, 0:NT], ALU.pow))
                chained(nc.gpsimd.tensor_scalar(sr[:, :], sr[:, :], RMS_EPS, None, ALU.add))
                nc.gpsimd.tensor_tensor(sf[:, :], sr[:, :], p_minus_one[:, :], ALU.pow).then_inc(sf_done, 1)

            for i in range(G + 2):
                a, t, f = i, i - 1, i - 2
                if a < G:
                    shifted_key_terms(a)
                if 0 <= t < G:
                    pow_z(t)
                if a < G:
                    pos_ret(a)
                if 0 <= f < G:
                    pow_ss(f)
                if 0 <= t < G:
                    pow_h2(t)
                if a < G:
                    kv_ret(a)
                    pow_gc(a)

        @block.scalar
        def _(act):
            for c in range(C):
                act.wait_ge(tokwT_in_psum, c + 1)
                s = slice(c * PH * D, (c + 1) * PH * D)
                nc.scalar.activation(tokw_h[:, s], tokw_bank(c), ACT.Copy, scale=WSCALE).then_inc(tokw_head, 1)

            def x_heads(g, j):
                n = g * KC + j
                act.wait_ge(xT_in_psum, n + 1)
                if n >= KC:
                    act.wait_ge(tok_chunk, n - KC + 1)
                nc.scalar.activation(x_h[:, j, :].rearrange("p (r w) -> p w r", w=SIDE),
                                     P01[:, j % 2, 0:TG].rearrange("p (w r) -> p w r", w=SIDE),
                                     ACT.Copy).then_inc(x_head, 1)

            def h_bias(g):
                act.wait_ge(tok_chunk, KC * (g + 1))
                act.wait_ge(vec_done, 1)
                if g >= 2:
                    act.wait_ge(hT_in_psum, g - 1)
                for m in range(DH):
                    ins = nc.scalar.activation(hF[g % 2][:, m, :], P23[:, m, 0:TG], ACT.Identity,
                                               bias=vec[:, m:m + 1], scale=INV)
                ins.then_inc(hF_done, 1)

            def normalise_h(g):
                act.wait_ge(nmr_done, g + 1)
                if g >= 2:
                    act.wait_ge(x1F_in_psum, g - 1)
                    act.wait_ge(res_done, g - 1)
                for t in range(NT):
                    ins = nc.scalar.activation(ring_T[g % 2][:, t * D:(t + 1) * D], tiles(P45)[:, t, :], ACT.Identity,
                                               bias=nmr[:, t:t + 1], scale=rstd[:, t:t + 1])
                ins.then_inc(x1T_done, 1)

            def x1_heads(g):
                act.wait_ge(x1F_in_psum, g + 1)
                nc.scalar.activation(x1_h[g][:, :, :, 1:PADL], P67[:, :, 0:TG].rearrange("p h (i l) -> p h i l", i=IPG),
                                     ACT.Copy).then_inc(x1_head, 1)

            def phase_tables():
                act.wait_ge(ph_reduced, 2)
                nc.scalar.activation(ph_cs[:, 1, :], ph[:, :], ACT.Sin)
                act.wait_ge(consts_done, 3)
                nc.scalar.activation(ph_cs[:, 0, :], ph_abs[:, :], ACT.Sin, bias=half_pi[0:L, :],
                                     scale=-1.0).then_inc(ph_cs_done, 1)

            def weight_sums():
                act.wait_ge(up_loaded, 16)
                nc.scalar.activation(up_t[:, :], up_f[:, :], ACT.Abs, accum_out=abs_sum[:, 0:1]).then_inc(abs_sum_done, 1)
                act.wait_ge(dn_loaded, 16)
                nc.scalar.activation(dn_t[:, :], dn_f[:, :], ACT.Abs, accum_out=abs_sum[:, 1:2]).then_inc(abs_sum_done, 1)

            for g in range(G + 1):
                for j in range(KC):
                    if g < G:
                        x_heads(g, j)
                    if g == 0 and j == KC - 1:
                        h_bias(0)
                        phase_tables()
                        weight_sums()
                    if j == 3 and g >= 1:
                        normalise_h(g - 1)
                if 1 <= g < G:
                    h_bias(g)
                if g >= 1:
                    x1_heads(g - 1)

            def hidden_gelus(g):
                for m in range(DH):
                    act.wait_ge(g1_in_psum, DH * g + m + 1)
                    if m == 0:
                        act.wait_ge(key_cs_done, g)
                        act.wait_ge(gate_in_psum, g)
                    ins = nc.scalar.activation(gh[:, m, :], P01[:, m, 0:TG], ACT.Gelu, bias=vec[:, 8 + m:9 + m],
                                               scale=INV)
                ins.then_inc(gh_done, 1)
                act.wait_ge(bh_in_psum, g + 1)
                act.wait_ge(z_in_psum, g)
                nc.scalar.activation(bh[:, :], P45[:, 0, 0:TG], ACT.Gelu, bias=vec[:, 10:11], scale=INV).then_inc(bh_done, 1)
                for m in range(DH):
                    act.wait_ge(key_in_psum, DH * g + m + 1)
                    ins = nc.scalar.activation(th[:, m, :], P23[:, m, 0:TG], ACT.Tanh, bias=vec[:, 4 + m:5 + m],
                                               scale=INV)
                ins.then_inc(th_done, 1)

            def exps(g):
                act.wait_ge(gate_in_psum, g + 1)
                act.wait_ge(gate_done, g)
                nc.scalar.activation(gate_e[:, :], P45[:, 1, 0:TG], ACT.Exp, bias=small[:, 3:4],
                                     scale=-1.0).then_inc(gate_e_done, 1)
                act.wait_ge(zlog_done, g + 1)
                act.wait_ge(bw_done, g)
                nc.scalar.activation(ze[:, :, :], zl[:, :, :], ACT.Exp).then_inc(ze_done, 1)

            def keys(g):
                b = g % 2
                if g >= 2:
                    act.wait_ge(kv_ret_done, g - 1)
                act.wait_ge(th_done, g + 1)
                nc.scalar.activation(th_abs[:, :, :], th[:, :, :], ACT.Abs).then_inc(th_abs_done, 1)
                nc.scalar.activation(key_s[b][:, :, :, 1:PADL], th[:, :, :].rearrange("p h (i l) -> p h i l", i=IPG),
                                     ACT.Sin, scale=PI_BELOW)
                act.wait_ge(th_abs_done, g + 1)
                nc.scalar.activation(key_c[b][:, :, :, 1:PADL], th_abs[:, :, :].rearrange("p h (i l) -> p h i l", i=IPG),
                                     ACT.Sin, bias=half_pi[:, :], scale=-PI).then_inc(key_cs_done, 1)

            def scale_pos(g):
                act.wait_ge(posT_in_psum, g + 1)
                act.wait_ge(bw_done, g + 1)
                if g >= 1:
                    act.wait_ge(zF_in_psum, g)
                else:
                    act.wait_ge(x1F_in_psum, G)
                    act.wait_ge(res_done, G)
                for t in range(NT):
                    ins = nc.scalar.activation(ring_T[0][:, t * D:(t + 1) * D], tiles(P23)[:, t, :], ACT.Copy,
                                               scale=bw[g % 2][:, 0, t:t + 1])
                ins.then_inc(pos_scaled, 1)

            def normalise_z(g):
                act.wait_ge(znm_done, g + 1)
                for t in range(NT):
                    r = ring_T[0][:, t * D:(t + 1) * D]
                    ins = nc.scalar.activation(r, r, ACT.Identity, bias=znm[:, t:t + 1], scale=zrs[:, t:t + 1])
                ins.then_inc(zT_done, 1)
                act.wait_ge(zF_in_psum, g + 1)
                act.wait_ge(wo_in_psum, g)
                nc.scalar.activation(z_h[:, :, :], P67[:, :, 0:TG], ACT.Copy).then_inc(z_head, 1)

            def normalise_h2(g):
                act.wait_ge(hnm_done, g + 1)
                act.wait_ge(x2F_in_psum, g)
                for t in range(NT):
                    ins = nc.scalar.activation(ring_T[1][:, t * D:(t + 1) * D], res[g][:, t * D:(t + 1) * D],
                                               ACT.Identity, bias=hnm[:, t:t + 1], scale=hf[:, t:t + 1])
                ins.then_inc(x2T_done, 1)
                act.wait_ge(x2F_in_psum, g + 1)
                nc.scalar.activation(x2_h[g], P67[:, :, 0:TG], ACT.Copy).then_inc(x2_head, 1)

            def ffn_gelus(g):
                for f in range(FC + 1):
                    n = FC * g + f
                    if f < FC:
                        act.wait_ge(up_in_psum, n + 1)
                        if n >= 3:
                            act.wait_ge(g_rest, n - 2)
                            act.wait_ge(g_head, n - 2)
                        nc.scalar.activation(gelu_ring[n % 3], P23[:, f % 2, 0:TG], ACT.Gelu).then_inc(gelu_done, 1)
                    if f >= 1:
                        act.wait_ge(gelu_done, n)
                        if f == 1:
                            act.wait_ge(down_in_psum, g)
                        nc.scalar.activation(ghl[:, f - 1, 0, :], gelu_ring[(n - 1) % 3], ACT.Copy).then_inc(g_head, 1)

            for i in range(G + 2):
                a, t, f = i, i - 1, i - 2
                if a < G:
                    hidden_gelus(a)
                    exps(a)
                    keys(a)
                if i == 1:
                    for n in range(4):
                        act.wait_ge(ternT_in_psum, n + 1)
                        dst = upT[:, n, :] if n < DH else \
                            dnT[:, (n - DH) * 4:(n - DH) * 4 + 4, :].rearrange("p f d -> p (f d)")
                        nc.scalar.activation(dst, P67[:, n % 2, :].bitcast(F16), ACT.Copy).then_inc(ternT_done, 1)
                if 0 <= t < G:
                    scale_pos(t)
                if 0 <= f < G:
                    ffn_gelus(f)
                if 0 <= t < G:
                    normalise_z(t)
                    normalise_h2(t)

        @block.vector
        def _(dve):
            steps = [0]

            def chained(ins):
                steps[0] += 1
                ins.then_inc(dve_step, 1)
                dve.wait_ge(dve_step, steps[0])

            nc.vector.memset(half_pi[:, :], PI / 2).then_inc(consts_done, 1)
            chained(nc.vector.memset(ones[:, :], 1.0))
            nc.vector.memset(p_minus_half[:, :], -0.5)
            nc.vector.memset(p_half[:, :], 0.5)
            nc.vector.memset(p_minus_one[:, :], -1.0)
            chained(nc.vector.memset(inside[:, :], 1.0))
            nc.vector.memset(inside[:, :].rearrange("p (n l) -> p n l", l=L)[:, :, 0:1], 0.0)
            for a in [*x1_h, *x1_l, *key_c, *key_s]:
                ins = nc.vector.memset(a[:, :, :, 0:1], 0.0)
            chained(ins)

            dve.wait_ge(vec_in_psum, 1)
            chained(nc.vector.tensor_copy(vec[:, :], P67[:, 1, 0:NV]))
            chained(nc.vector.tensor_copy(small[:, 0:3], P67[:, 1, 32:35]))
            nc.vector.tensor_scalar(small[:, 3:4], small[:, 2:3], -1.0, None, ALU.mult)
            nc.vector.tensor_scalar(vec_s[:, :], vec[:, :], WSCALE, None, ALU.mult)
            for k in range(DH):
                nc.vector.tensor_scalar(wg2b[:, k, :], ones[:, :], vec[:, 15 + k:16 + k], None, ALU.mult)
                ins = nc.vector.tensor_scalar(lnbb[:, k, :], ones[:, 0:TT], vec[:, 13 + k:14 + k], None, ALU.mult)
            ins.then_inc(vec_done, 1)

            def reduce_phases():
                dve.wait_ge(ph_loaded, 16)
                chained(nc.vector.tensor_scalar(ph_k[:, :], ph[:, :], 0.5 / PI, ROUND_MAGIC, ALU.mult, ALU.add))
                chained(nc.vector.tensor_scalar(ph_k[:, :], ph_k[:, :], ROUND_MAGIC, None, ALU.subtract))
                for part in TWO_PI_PARTS:
                    chained(nc.vector.scalar_tensor_tensor(out=ph[:, :], in0=ph_k[:, :], scalar=-part, in1=ph[:, :],
                                                           op0=ALU.mult, op1=ALU.add))
                nc.vector.tensor_scalar(ph[:, :], ph[:, :], PI_BELOW, -PI_BELOW, ALU.min, ALU.max).then_inc(ph_reduced, 1)
                dve.wait_ge(ph_reduced, 1)
                nc.vector.scalar_tensor_tensor(out=ph_abs, in0=ph, scalar=-1.0, in1=ph, op0=ALU.mult,
                                               op1=ALU.max).then_inc(ph_reduced, 1)

            def sort_pixels(half, c):
                dve.wait_ge(x_loaded[c], 48 + 32 * half)
                if half > 0:
                    dve.wait_ge(xT_in_psum, KC + (c + 1) * PH)
                n = ODD + ROWS
                nc.vector.tensor_copy(x_pat[c][0:n, :].rearrange("r (w p q) -> r p w q", w=SIDE, p=PATCH),
                                      x_raw[c][0:n, :].rearrange("r (p w q) -> r p w q", w=SIDE, p=PATCH)
                                      ).then_inc(x_sorted, 1)

            def x_rests(g, j):
                n = g * KC + j
                dve.wait_ge(x_head, n + 1)
                nc.vector.tensor_tensor(x_l[:, j, :].rearrange("p (r w) -> p w r", w=SIDE),
                                        P01[:, j % 2, 0:TG].rearrange("p (w r) -> p w r", w=SIDE),
                                        x_h[:, j, :].rearrange("p (r w) -> p w r", w=SIDE),
                                        ALU.subtract).then_inc(x_rest, 1)

            def stats(src, st_, mv_):
                for t in range(NT):
                    ins = nc.vector.bn_stats(st_[:, t, :], src(t))
                chained(ins)
                for t in range(NT):
                    ins = nc.vector.bn_aggr(mv_[:, t, :], st_[:, t, :])
                chained(ins)

            def stats_h(g):
                dve.wait_ge(hT_in_psum, g + 1)
                dve.wait_ge(nmr_done, g)
                stats(lambda t: tiles(P45)[:, t, :], st, mv)
                nc.vector.tensor_scalar(ve[:, :], mv[:, :, 1], LN_EPS, None, ALU.add).then_inc(ve_done, 1)
                dve.wait_ge(rstd_done, g + 1)
                dve.wait_ge(x1T_done, g)
                nc.vector.scalar_tensor_tensor(out=nmr[:, :], in0=mv[:, :, 0], scalar=-1.0, in1=rstd[:, :],
                                               op0=ALU.mult, op1=ALU.mult).then_inc(nmr_done, 1)

            def residual(g):
                dve.wait_ge(x1T_done, g + 1)
                nc.vector.tensor_tensor(res[g][:, :], flat_T(P45), ring_T[g % 2][:, :], ALU.add).then_inc(res_done, 1)

            def x1_rests(g):
                dve.wait_ge(x1_head, g + 1)
                nc.vector.tensor_tensor(x1_l[g][:, :, :, 1:PADL], P67[:, :, 0:TG].rearrange("p h (i l) -> p h i l", i=IPG),
                                        x1_h[g][:, :, :, 1:PADL], ALU.subtract).then_inc(x1_rest, 1)

            def setup_copies():
                dve.wait_ge(setup_in_psum, 1)
                nc.vector.tensor_copy(table[:, :, :, :].rearrange("p a h l -> p (a h l)"), P67[:, 0, 0:2 * DH * L])
                nc.vector.tensor_copy(bias_T[:, :], P67[0:TT, 1, 0:D])
                nc.vector.tensor_scalar(thr[:, 0:2], P67[:, 1, 256:258], 0.5 / (F * D), None, ALU.mult)
                nc.vector.tensor_scalar(thr[:, 2:4], P67[:, 1, 256:258], -0.5 / (F * D), None,
                                        ALU.mult).then_inc(setup_done, 1)

            def ternary(w, t, n):
                dve.wait_ge(setup_done, 1)
                dve.wait_ge(tern_done, n)
                chained(nc.vector.tensor_scalar(above[:, :], w[:, :], thr[:, 2 + n:3 + n], None, ALU.is_lt))
                nc.vector.scalar_tensor_tensor(out=t[:, :], in0=w[:, :], scalar=thr[:, n:n + 1], in1=above[:, :],
                                               op0=ALU.is_gt, op1=ALU.subtract).then_inc(tern_done, 1)

            sort_pixels(0, 0)
            for c in range(C):
                dve.wait_ge(tokw_head, c + 1)
                s = slice(c * PH * D, (c + 1) * PH * D)
                nc.vector.scalar_tensor_tensor(out=tokw_l[:, s], in0=tokw_bank(c), scalar=WSCALE, in1=tokw_h[:, s],
                                               op0=ALU.mult, op1=ALU.subtract).then_inc(tokw_done, 1)

            sort_pixels(0, 1)
            sort_pixels(0, 2)
            for g in range(G + 1):
                for j in range(KC):
                    if g < G:
                        x_rests(g, j)
                    if g == 1 and j % PH == PH - 1:
                        sort_pixels(1, j // PH)
                    if g == 0 and j == 1:
                        reduce_phases()
                    if g >= 1 and j == 2:
                        stats_h(g - 1)
                    if g >= 1 and j == 4:
                        residual(g - 1)
                if g == 0:
                    setup_copies()
                if g >= 1:
                    x1_rests(g - 1)

            def pos_terms(g):
                dve.wait_ge(pv_in_psum, g + 1)
                dve.wait_ge(m_pos_done, 2 * g)
                for i, u in enumerate((u_pc, u_ps)):
                    for m in range(DH):
                        ins = nc.vector.scalar_tensor_tensor(
                            out=images(u[:, m * TG:(m + 1) * TG]), in0=images(P67[:, m, 0:TG]),
                            scalar=vec_s[:, 2 + m:3 + m], in1=table[:, i, m, :].unsqueeze(1).broadcast_to([128, IPG, L]),
                            op0=ALU.add, op1=ALU.mult)
                ins.then_inc(u_pos_done, 1)

            def blend_logits(g):
                dve.wait_ge(z_in_psum, g + 1)
                dve.wait_ge(ze_done, g)
                chained(nc.vector.tensor_tensor(zl[:, :, :], P45[0:TT, 0, 0:2 * NT].rearrange("p (t c) -> p t c", c=2),
                                                small[0:TT, 0:2].unsqueeze(1).broadcast_to([TT, NT, 2]), ALU.add))
                chained(nc.vector.tensor_tensor(zmax[:, :, :], zl[:, :, 0:1], zl[:, :, 1:2], ALU.max))
                nc.vector.tensor_tensor(zl[:, :, :], zl[:, :, :], zmax[:, :, :].broadcast_to([TT, NT, 2]),
                                        ALU.subtract).then_inc(zlog_done, 1)

            def gates(g):
                dve.wait_ge(gate_e_done, g + 1)
                dve.wait_ge(gate_sum_done, g)
                chained(nc.vector.tensor_scalar(gate_e[:, :], gate_e[:, :], 1.0, None, ALU.add))
                nc.vector.reciprocal(gate[:, :], gate_e[:, :]).then_inc(gate_done, 1)
                dve.wait_ge(gate_done, g + 1)

            def gated_values(g):
                dve.wait_ge(kv_in_psum, g + 1)
                dve.wait_ge(u_kv_done, 2 * g)
                for m in range(DH):
                    ins = nc.vector.scalar_tensor_tensor(out=kvg[:, m, :], in0=P01[:, m, 0:TG],
                                                         scalar=vec_s[:, 6 + m:7 + m], in1=gate[:, :], op0=ALU.add,
                                                         op1=ALU.mult)
                ins.then_inc(kvg_done, 1)
                if g >= 2:
                    dve.wait_ge(gc_in_psum, g - 1)
                nc.vector.tensor_tensor_scan(gate_sum[g % 2][:, :], inside[:, 0:TG], gate[:, :], 0.0, ALU.mult,
                                             ALU.add).then_inc(gate_sum_done, 1)

            def blend_weights(g):
                b = bw[g % 2]
                dve.wait_ge(ze_done, g + 1)
                dve.wait_ge(bw_done, g)
                if g >= 2:
                    dve.wait_ge(pos_scaled, g - 1)
                chained(nc.vector.tensor_tensor(zsum[:, :], ze[:, :, 0], ze[:, :, 1], ALU.add))
                chained(nc.vector.reciprocal(zsum[:, :], zsum[:, :]))
                for c in range(2):
                    ins = nc.vector.scalar_tensor_tensor(out=b[:, c, :], in0=ze[:, :, c], scalar=INV / D ** 0.5,
                                                         in1=zsum[:, :], op0=ALU.mult, op1=ALU.mult)
                ins.then_inc(bw_done, 1)

            def scan(m, u, done):
                nc.vector.tensor_tensor_scan(m, inside[:, :], u, 0.0, ALU.mult, ALU.add).then_inc(done, 1)

            def scan_pos(g):
                dve.wait_ge(u_pos_done, g + 1)
                dve.wait_ge(posT_in_psum, g)
                scan(m_pc, u_pc, m_pos_done)
                scan(m_ps, u_ps, m_pos_done)

            def scan_kv(g):
                dve.wait_ge(u_kv_done, 2 * g + 1)
                dve.wait_ge(kvT_in_psum, g)
                scan(m_kc, u_kc, m_kv_done)
                dve.wait_ge(u_kv_done, 2 * g + 2)
                scan(m_ks, u_ks, m_kv_done)

            def gate_count(g):
                dve.wait_ge(gc_in_psum, g + 1)
                nc.vector.tensor_scalar(gc[:, :], P45[0:TT, 0, 0:NT], 1.0, None, ALU.max).then_inc(gc_done, 1)

            def blend(g):
                dve.wait_ge(gcr_done, g + 1)
                dve.wait_ge(bw_done, g + 1)
                dve.wait_ge(blend_done, g)
                dve.wait_ge(znm_done, g)
                chained(nc.vector.tensor_tensor(kvw[:, :], bw[g % 2][:, 1, :], gcr[:, :], ALU.mult))
                dve.wait_ge(kvT_in_psum, g + 1)
                dve.wait_ge(pos_scaled, g + 1)
                for t in range(NT):
                    r = ring_T[0][:, t * D:(t + 1) * D]
                    ins = nc.vector.scalar_tensor_tensor(out=r, in0=tiles(P45)[:, t, :], scalar=kvw[:, t:t + 1], in1=r,
                                                         op0=ALU.mult, op1=ALU.add)
                ins.then_inc(blend_done, 1)
                dve.wait_ge(blend_done, g + 1)
                stats(lambda t: ring_T[0][:, t * D:(t + 1) * D], zst, zmv)
                nc.vector.tensor_scalar(zve[:, :], zmv[:, :, 1], LN_EPS, None, ALU.add).then_inc(zve_done, 1)
                dve.wait_ge(zrs_done, g + 1)
                dve.wait_ge(zT_done, g)
                nc.vector.scalar_tensor_tensor(out=znm[:, :], in0=zmv[:, :, 0], scalar=-1.0, in1=zrs[:, :],
                                               op0=ALU.mult, op1=ALU.mult).then_inc(znm_done, 1)

            def z_rests(g):
                dve.wait_ge(z_head, g + 1)
                nc.vector.tensor_tensor(z_l[:, :, :], P67[:, :, 0:TG], z_h[:, :, :], ALU.subtract).then_inc(z_rest, 1)

            def second_residual(g):
                dve.wait_ge(wo_in_psum, g + 1)
                dve.wait_ge(res_biased, g + 1)
                dve.wait_ge(hnm_done, g)
                nc.vector.scalar_tensor_tensor(out=res[g][:, :], in0=flat_T(P01), scalar=INV, in1=res[g][:, :],
                                               op0=ALU.mult, op1=ALU.add).then_inc(h2_done, 1)
                dve.wait_ge(h2_done, g + 1)
                stats(lambda t: res[g][:, t * D:(t + 1) * D], hst, hmv)
                nc.vector.tensor_copy(hvv[:, 0, :], hmv[:, :, 1])
                nc.vector.tensor_scalar(hvv[:, 1, :], hmv[:, :, 1], LN_EPS, None, ALU.add).then_inc(hvv_done, 1)
                dve.wait_ge(hf_done, g + 1)
                dve.wait_ge(x2T_done, g)
                nc.vector.scalar_tensor_tensor(out=hnm[:, :], in0=hmv[:, :, 0], scalar=-1.0, in1=hf[:, :],
                                               op0=ALU.mult, op1=ALU.mult).then_inc(hnm_done, 1)

            def x2_rests(g):
                dve.wait_ge(x2_head, g + 1)
                nc.vector.tensor_tensor(x2_l[g], P67[:, :, 0:TG], x2_h[g], ALU.subtract).then_inc(x2_rest, 1)

            def hidden_rests(g):
                for f in range(FC):
                    dve.wait_ge(g_head, FC * g + f + 1)
                    nc.vector.tensor_tensor(ghl[:, f, 1, :], gelu_ring[(FC * g + f) % 3], ghl[:, f, 0, :],
                                            ALU.subtract).then_inc(g_rest, 1)

            def square_sums(g):
                dve.wait_ge(gram_in_psum, g + 1)
                dve.wait_ge(sf_done, g)
                dve.wait_ge(ss_done, g)
                dve.wait_ge(consts_done, 3)
                for t in range(NT):
                    ins = nc.vector.tensor_tensor_reduce(
                        out=junk[:, :], in0=P45[0:TT, t // 2, (t % 2) * 2 * TT:(t % 2 + 1) * 2 * TT],
                        in1=gmask[:, :, :].rearrange("p a t -> p (a t)"), scale=1.0, scalar=0.0, op0=ALU.mult,
                        op1=ALU.add, accum_out=ss[:, t:t + 1])
                    if t < NT - 1:
                        chained(ins)
                ins.then_inc(ss_done, 1)

            def outputs(g):
                dve.wait_ge(down_in_psum, g + 1)
                dve.wait_ge(sf_done, g + 1)
                if g >= 2:
                    dve.wait_ge(out_stored[g % 2], 16 * (g // 2))
                for t in range(NT):
                    ins = nc.vector.scalar_tensor_tensor(out=out_ring[g % 2][:, t * D:(t + 1) * D],
                                                         in0=tiles(P01)[:, t, :], scalar=sf[:, t:t + 1],
                                                         in1=res[g][:, t * D:(t + 1) * D], op0=ALU.mult, op1=ALU.add)
                ins.then_inc(out_done, 1)

            for i in range(G + 2):
                a, t, f = i, i - 1, i - 2
                if a < G:
                    pos_terms(a)
                    blend_logits(a)
                    gates(a)
                    gated_values(a)
                    blend_weights(a)
                if 0 <= t < G:
                    blend(t)
                if a < G:
                    scan_pos(a)
                if i == 0:
                    ternary(up_f, up_t, 0)
                    ternary(dn_f, dn_t, 1)
                if 0 <= f < G:
                    hidden_rests(f)
                if 0 <= t < G:
                    z_rests(t)
                if a < G:
                    scan_kv(a)
                if 0 <= f < G:
                    square_sums(f)
                if 0 <= t < G:
                    second_residual(t)
                if 0 <= f < G:
                    outputs(f)
                if 0 <= t < G:
                    x2_rests(t)
                if a < G:
                    gate_count(a)

        @block.tensor
        def _(pe):
            mm = nc.tensor.matmul

            pe.wait_ge(ident_done, 1)
            pe.wait_ge(dve_step, 1)
            pe.wait_ge(vec_loaded, 16 * N_VEC)
            nc.tensor.transpose(P67[:, 1, 0:NV], vrows[:, :], ident[0:NV, 0:NV])
            mm(P67[:, 1, 32:35], ones[0:1, :], srow[:, :], start=True, stop=True).then_inc(vec_in_psum, 1)

            pe.wait_ge(tokw_loaded, 16)
            w_in = tokw_f[:, :].rearrange("p (m h j c) -> p m c h j", m=DH, h=PH, c=C)
            for c in range(C):
                for h in range(PH):
                    for m in range(DH):
                        k = h * D + m * 128
                        ins = nc.tensor.transpose(tokw_bank(c)[:, k:k + 128], w_in[:, m, c, h, :], ident[:, :])
                ins.then_inc(tokwT_in_psum, 1)

            def x_transposes(g, j):
                n, c, h = g * KC + j, j // PH, j % PH
                if j % PH == 0:
                    pe.wait_ge(x_sorted, C * (g // 2) + c + 1)
                if n >= 2:
                    pe.wait_ge(x_rest, n - 1)
                lo = (g % 2) * ODD
                for w in range(SIDE):
                    ins = nc.tensor.transpose(P01[:, j % 2, w * ROWS:(w + 1) * ROWS],
                                              x_pat[c][lo:lo + ROWS, (w * PH + h) * 128:(w * PH + h + 1) * 128],
                                              ident[lo:lo + ROWS, lo:lo + ROWS])
                ins.then_inc(xT_in_psum, 1)

            def embed(g, j):
                n = g * KC + j
                pe.wait_ge(x_rest, n + 1)
                if g == 0:
                    pe.wait_ge(tokw_done, C)
                if j == 0:
                    pe.wait_ge(hF_done, g)
                for m in range(DH):
                    for i, (w, v) in enumerate(((tokw_h, x_h), (tokw_h, x_l), (tokw_l, x_h))):
                        ins = mm(P23[:, m, 0:TG], w[:, j * D + m * 128:j * D + (m + 1) * 128], v[:, j, :],
                                 start=(j == 0 and i == 0), stop=(j == KC - 1 and i == 2))
                ins.then_inc(tok_chunk, 1)

            def to_T(src, dst):
                for t in range(NT):
                    for m in range(DH):
                        ins = nc.tensor.transpose(tiles(dst)[:, t, m * 128:(m + 1) * 128], src(m, t), ident[:, :])
                return ins

            def to_F(src, dst):
                for m in range(DH):
                    for t in range(NT):
                        ins = nc.tensor.transpose(dst[:, m, t * TT:(t + 1) * TT],
                                                  src[:, t * D + m * 128:t * D + (m + 1) * 128], ident[0:TT, 0:TT])
                return ins

            def h_to_T(g):
                pe.wait_ge(hF_done, g + 1)
                pe.wait_ge(res_done, g)
                to_T(lambda m, t: hF[g % 2][:, m, t * TT:(t + 1) * TT], P45).then_inc(hT_in_psum, 1)

            def x1_to_F(g):
                pe.wait_ge(x1T_done, g + 1)
                pe.wait_ge(x1_rest, g)
                if g == 0:
                    pe.wait_ge(setup_done, 1)
                to_F(ring_T[g % 2], P67).then_inc(x1F_in_psum, 1)

            def setup():
                pe.wait_ge(ph_cs_done, 1)
                for a in range(2):
                    for m in range(DH):
                        k = (a * DH + m) * L
                        nc.tensor.transpose(P67[:, 0, k:k + L], ph_cs[:, a, m * 128:(m + 1) * 128], ident[0:L, 0:L])
                pe.wait_ge(vec_done, 1)
                pe.wait_ge(aw_loaded, 16 * 6)
                for k in range(DH):
                    mm(P67[0:TT, 1, 0:D], lnbb[:, k, :], slot(aw_f, WO, k), start=(k == 0), stop=False)
                mm(P67[0:TT, 1, 0:D], ones[0:1, 0:TT], borow[:, :], start=False, stop=True)
                pe.wait_ge(abs_sum_done, 2)
                mm(P67[:, 1, 256:258], ones[:, :], abs_sum[:, :], start=True, stop=True).then_inc(setup_in_psum, 1)

            for g in range(G):
                x_transposes(g, 0)
                for j in range(KC):
                    if j + 1 < KC:
                        x_transposes(g, j + 1)
                    embed(g, j)
                    if j == 1 and g >= 1:
                        h_to_T(g - 1)
                if g == 0:
                    setup()
                else:
                    x1_to_F(g - 1)
            h_to_T(G - 1)

            def parts(w, s, k, width, v_h, v_l):
                wh, wl = (a[:, s * 256 + k * width:s * 256 + (k + 1) * width] for a in (aw_h, aw_l))
                return ((wh, v_h), (wh, v_l), (wl, v_h))

            def project(pair, b, s, width, m, g, chunks):
                total = 3 * len(chunks)
                n = 0
                for k, (half, first) in enumerate(chunks):
                    v_h, v_l = (a[g][:, half, :, first:first + L] for a in (x1_h, x1_l))
                    for w, v in parts(None, s, k, width, v_h, v_l):
                        ins = mm(images(pair[:, b, 0:TG]), w[:, m * 128:(m + 1) * 128], v, start=(n == 0),
                                 stop=(n == total - 1))
                        n += 1
                return ins

            HERE = [(h, 1) for h in range(DH)]
            BEFORE = [(h, 0) for h in range(DH)]

            def gate_hidden(g):
                pe.wait_ge(x1_rest, g + 1)
                if g == 0:
                    pe.wait_ge(aw_done, 1)
                    pe.wait_ge(x_rest, KC * G)
                if g >= 2:
                    pe.wait_ge(h2_done, g - 1)
                if g >= 3:
                    pe.wait_ge(out_done, g - 2)
                for m in range(DH):
                    project(P01, m, G1, D, m, g, HERE + BEFORE).then_inc(g1_in_psum, 1)

            def projections(g):
                if g == 0:
                    pe.wait_ge(res_done, G)
                if g >= 1:
                    pe.wait_ge(gc_done, g)
                if g >= 2:
                    pe.wait_ge(blend_done, g - 1)
                if g >= 3:
                    pe.wait_ge(ss_done, g - 2)
                project(P45, 0, BH, 128, 0, g, HERE).then_inc(bh_in_psum, 1)
                if g == 0:
                    pe.wait_ge(hF_done, G)
                if g >= 2:
                    pe.wait_ge(pos_scaled, g - 1)
                if g >= 3:
                    pe.wait_ge(gelu_done, FC * (g - 2))
                for m in range(DH):
                    project(P23, m, KEY, D, m, g, HERE).then_inc(key_in_psum, 1)
                if g == 0:
                    pe.wait_ge(x1_rest, G)
                if g >= 2:
                    pe.wait_ge(x2_rest, g - 1)
                    pe.wait_ge(ternT_done, 4)
                for m in range(DH):
                    ins = project(P67, m, PV, D, m, g, HERE)
                ins.then_inc(pv_in_psum, 1)
                pe.wait_ge(gh_done, g + 1)
                for k in range(DH):
                    ins = mm(P45[:, 1, 0:TG], wg2b[:, k, :], gh[:, k, :], start=(k == 0), stop=(k == DH - 1))
                ins.then_inc(gate_in_psum, 1)
                pe.wait_ge(bh_done, g + 1)
                for t in range(NT):
                    ins = mm(P45[0:TT, 0, 2 * t:2 * t + 2], bh[:, t * TT:(t + 1) * TT], wb2[:, :], start=True, stop=True)
                ins.then_inc(z_in_psum, 1)
                for m in range(DH):
                    ins = project(P01, m, KV, D, m, g, HERE)
                ins.then_inc(kv_in_psum, 1)

            def ternary_to_F():
                pe.wait_ge(u_pos_done, 2)
                for n in range(4):
                    b = P67[:, n % 2, :].bitcast(F16)
                    pe.wait_ge(tern_done, n // 2 + 1)
                    if n >= 2:
                        pe.wait_ge(ternT_done, n - 1)
                    for q in range(8):
                        if n < DH:
                            src = up_t[:, q * D + n * 128:q * D + (n + 1) * 128]
                        else:
                            f, m = (n - DH) * 4 + q // 2, q % 2
                            src = dn_t[:, m * F + f * 128:m * F + (f + 1) * 128]
                        ins = nc.tensor.transpose(b[:, q * 128:(q + 1) * 128], src, ident16[:, :])
                    ins.then_inc(ternT_in_psum, 1)

            def gate_sums(g):
                pe.wait_ge(gate_sum_done, g + 1)
                pe.wait_ge(zlog_done, g + 1)
                pe.wait_ge(blend_done, g)
                if g >= 2:
                    pe.wait_ge(ss_done, g - 1)
                for t in range(NT):
                    ins = mm(P45[0:TT, 0, t:t + 1], gate_sum[g % 2][0:1, t * TT:(t + 1) * TT], ones[0:1, 0:1],
                             start=True, stop=True)
                ins.then_inc(gc_in_psum, 1)

            def returns_to_T(g):
                pe.wait_ge(pos_ret_done, g + 1)
                pe.wait_ge(th_done, last_group(g + 1) + 1)
                pe.wait_ge(pos_scaled, g)
                if g >= 2:
                    pe.wait_ge(gelu_done, FC * (g - 1))
                to_T(lambda m, t: m_pc[:, m * TG + t * TT:m * TG + (t + 1) * TT], P23).then_inc(posT_in_psum, 1)
                pe.wait_ge(kv_ret_done, g + 1)
                pe.wait_ge(gc_done, g + 1)
                pe.wait_ge(zlog_done, last_group(g + 1) + 1)
                pe.wait_ge(gate_e_done, last_group(g + 1) + 1)
                to_T(lambda m, t: m_kc[:, m * TG + t * TT:m * TG + (t + 1) * TT], P45).then_inc(kvT_in_psum, 1)

            def z_to_F(g):
                pe.wait_ge(zT_done, g + 1)
                pe.wait_ge(u_pos_done, last_group(g + 1) + 1)
                if g == 0:
                    pe.wait_ge(ternT_done, 4)
                to_F(ring_T[0], P67).then_inc(zF_in_psum, 1)

            def attention_out(g):
                pe.wait_ge(z_rest, g + 1)
                pe.wait_ge(aw_done, 2)
                pe.wait_ge(kvg_done, last_group(g + 1) + 1)
                if g >= 2:
                    pe.wait_ge(out_done, g - 1)
                for t in range(NT):
                    n = 0
                    for k in range(DH):
                        for v, w in ((z_h, aw_h), (z_l, aw_h), (z_h, aw_l)):
                            ins = mm(tiles(P01)[:, t, :], v[:, k, t * TT:(t + 1) * TT], slot(w, WO, k), start=(n == 0),
                                     stop=(n == 3 * DH - 1))
                            n += 1
                ins.then_inc(wo_in_psum, 1)

            def x2_to_F(g):
                pe.wait_ge(x2T_done, g + 1)
                pe.wait_ge(z_rest, g + 1)
                to_F(ring_T[1], P67).then_inc(x2F_in_psum, 1)

            def ffn_up(g):
                pe.wait_ge(x2_rest, g + 1)
                pe.wait_ge(ternT_done, 4)
                pe.wait_ge(pos_scaled, last_group(g + 1) + 1)
                for f in range(FC):
                    n = FC * g + f
                    if n >= 2:
                        pe.wait_ge(gelu_done, n - 1)
                    i = 0
                    for k in range(DH):
                        for v in (x2_h[g], x2_l[g]):
                            ins = mm(P23[:, f % 2, 0:TG], upT[:, k, f * 128:(f + 1) * 128], v[:, k, :], start=(i == 0),
                                     stop=(i == 2 * DH - 1))
                            i += 1
                    ins.then_inc(up_in_psum, 1)

            def gram(g):
                pe.wait_ge(g_rest, FC * (g + 1))
                pe.wait_ge(blend_done, last_group(g + 1) + 1)
                pe.wait_ge(ss_done, g)
                for t in range(NT):
                    o = P45[0:TT, t // 2, (t % 2) * 2 * TT:(t % 2 + 1) * 2 * TT].rearrange("p (a t) -> p a t", a=2)
                    for f in range(FC):
                        ins = mm(o, ghl[:, f, 0, t * TT:(t + 1) * TT], ghl[:, f, :, t * TT:(t + 1) * TT],
                                 start=(f == 0), stop=(f == FC - 1))
                ins.then_inc(gram_in_psum, 1)

            def ffn_down(g):
                pe.wait_ge(h2_done, last_group(g + 1) + 1)
                pe.wait_ge(out_done, g)
                for t in range(NT):
                    for f in range(FC):
                        for a in range(2):
                            ins = mm(tiles(P01)[:, t, :], ghl[:, f, a, t * TT:(t + 1) * TT], dnT[:, f, :],
                                     start=(f == 0 and a == 0), stop=(f == FC - 1 and a == 1))
                ins.then_inc(down_in_psum, 1)

            for i in range(G + 2):
                a, t, f = i, i - 1, i - 2
                if a < G:
                    gate_hidden(a)
                    if a == 0:
                        x1_to_F(G - 1)
                    projections(a)
                if i == 1:
                    ternary_to_F()
                if 0 <= t < G:
                    returns_to_T(t)
                if 0 <= f < G:
                    ffn_up(f)
                if 0 <= t < G:
                    z_to_F(t)
                if 0 <= f < G:
                    gram(f)
                if 0 <= t < G:
                    attention_out(t)
                if 0 <= f < G:
                    ffn_down(f)
                if 0 <= t < G:
                    x2_to_F(t)
                if a < G:
                    gate_sums(a)


_INS = ["x", "L0_tok_W", "L0_tok_b", "L0_attn_pos_phases", "L0_attn_Wpv", "L0_attn_bpv", "L0_attn_Wk", "L0_attn_bk",
        "L0_attn_Wkv", "L0_attn_bkv", "L0_attn_Wg1", "L0_attn_bg1", "L0_attn_Wg2", "L0_attn_bg2", "L0_attn_Wb1",
        "L0_attn_bb1", "L0_attn_Wb2", "L0_attn_bb2", "L0_attn_ln_g", "L0_attn_ln_b", "L0_attn_Wo", "L0_attn_bo",
        "L0_ffn_w_up", "L0_ffn_w_down"]
_OUTS = [((32, 49, 256), "float32")]


def kernel(**inputs):
    import numpy as _np
    import concourse.bacc as _bacc
    from concourse import mybir as _mybir
    from concourse.bass_utils import run_bass_kernel_spmd as _run

    nc = _bacc.Bacc("TRN2", target_bir_lowering=False, num_devices=1)
    arrays, args = {}, []
    for name in _INS:
        a = _np.ascontiguousarray(inputs[name])
        arrays[f"in_{name}_dram"] = a
        args.append(nc.dram_tensor(f"in_{name}_dram", a.shape, _mybir.dt.from_np(a.dtype), kind="ExternalInput").ap())
    for i, (shape, dtype) in enumerate(_OUTS):
        dt = _mybir.dt.from_np(_np.dtype(dtype))
        args.append(nc.dram_tensor(f"out_{i}_dram", shape, dt, kind="ExternalOutput").ap())
    vit_block_program(nc, *args)
    r = _run(nc, [arrays], core_ids=[0])
    return r.results[0]["out_0_dram"]
```

```python
from contextlib import ExitStack

import concourse.bass as bass
from concourse import mybir

ALU = mybir.AluOpType
ACT = mybir.ActivationFunctionType
F32 = mybir.dt.float32
F16 = mybir.dt.float16

PI = 3.14159265358979
WSCALE = 256.0
TWO_PI_PARTS = (6.28125, 0.0019350051879882812, 3.0199160514e-07)
ROUND_MAGIC = 12582912.0
PI_BELOW = 3.1415925
LN_EPS = 1e-5
RMS_EPS = 1e-8


def vit_block_program(nc, x, tok_W, tok_b, phases, Wpv, bpv, Wk, bk, Wkv, bkv, Wg1, bg1, Wg2, bg2,
                      Wb1, bb1, Wb2, bb2, ln_g, ln_b, Wo, bo, w_up, w_down, out):
    NIMG, C, HW, _ = x.shape
    PATCH = 16
    SIDE = HW // PATCH
    L = SIDE * SIDE
    D = tok_W.shape[0]
    DH = D // 128
    F = w_up.shape[0]
    FC = F // 128
    IPG = 8
    G = NIMG // IPG
    TG = IPG * L
    TT = 2 * L
    NT = TG // TT
    ROWS = IPG * SIDE
    PH = PATCH * PATCH // 128
    ODD = 64
    PIX = PATCH * HW
    KC = C * PH
    PADL = L + 1
    INV = 1.0 / WSCALE
    PV, KEY, KV, G1, BH, WO = 0, 2, 4, 6, 10, 11
    NSLOT = 13

    with ExitStack() as ctx:
        def sb(name, shape, dt=F32):
            return ctx.enter_context(nc.sbuf_tensor(name, shape, dt))

        def sem(name):
            return ctx.enter_context(nc.semaphore(name))

        bank = [ctx.enter_context(nc.psum_tensor(f"pair{i}", [128, 2, 512], F32)) for i in range(4)]
        P01, P23, P45, P67 = bank

        arena = sb("arena", [128, 2 * C * PIX])
        x_raw = [arena[:, c * PIX:(c + 1) * PIX] for c in range(C)]
        x_pat = [arena[:, (C + c) * PIX:(C + c + 1) * PIX] for c in range(C)]
        n = DH * TG
        u_pc, u_ps, u_kc, u_ks, m_pc, m_ps, m_kc, m_ks = [arena[:, i * n:(i + 1) * n] for i in range(8)]
        ghl = arena[:, 8 * n:8 * n + FC * TG].bitcast(F16).rearrange("p (f s t) -> p f s t", f=FC, s=2)

        tokw_f = sb("tokw_f", [128, KC * D])
        gelu_ring = [tokw_f[:, i * TG:(i + 1) * TG] for i in range(3)]
        tokw_h = sb("tokw_h", [128, KC * D], F16)
        tokw_l = sb("tokw_l", [128, KC * D], F16)
        x_h = sb("x_h", [128, KC, TG], F16)
        x_l = sb("x_l", [128, KC, TG], F16)
        aw_f = sb("aw_f", [128, NSLOT * 256])
        out_ring = [aw_f[0:TT, i * NT * D:(i + 1) * NT * D] for i in range(2)]
        aw_h = sb("aw_h", [128, NSLOT * 256], F16)
        aw_l = sb("aw_l", [128, NSLOT * 256], F16)
        up_f = sb("up_f", [128, FC * D])
        dn_f = sb("dn_f", [128, DH * F])
        above = sb("above", [128, FC * D], F16)
        up_t = sb("up_t", [128, FC * D], F16)
        dn_t = sb("dn_t", [128, DH * F], F16)
        upT = sb("upT", [128, DH, F], F16)
        dnT = sb("dnT", [128, FC, D], F16)
        hF = [sb(f"hF{i}", [128, DH, TG]) for i in range(2)]
        ring_T = [sb(f"ring_T{i}", [TT, NT * D]) for i in range(2)]
        x1_h = [sb(f"x1_h{g}", [128, DH, IPG, PADL], F16) for g in range(G)]
        x1_l = [sb(f"x1_l{g}", [128, DH, IPG, PADL], F16) for g in range(G)]
        flat = lambda a: a[:, :, :, :].rearrange("p h i l -> p (h i l)")[:, 0:DH * TG].rearrange("p (h t) -> p h t", h=DH)
        x2_h = [flat(x1_h[g]) for g in range(G)]
        x2_l = [flat(x1_l[g]) for g in range(G)]
        res = [sb(f"res{g}", [TT, NT * D]) for g in range(G)]
        x_h32, x_l32 = (a[:, :, :].rearrange("p k t -> p (k t)").bitcast(F32) for a in (x_h, x_l))
        gh = x_h32[:, 0:DH * TG].rearrange("p (h t) -> p h t", h=DH)
        bh = x_h32[:, DH * TG:(DH + 1) * TG]
        th = x_l32[:, 0:DH * TG].rearrange("p (h t) -> p h t", h=DH)
        gate = x_l32[:, DH * TG:(DH + 1) * TG]
        th_abs = sb("th_abs", [128, DH, TG])
        key_c = [sb(f"key_c{i}", [128, DH, IPG, PADL]) for i in range(2)]
        key_s = [sb(f"key_s{i}", [128, DH, IPG, PADL]) for i in range(2)]
        kvg = sb("kvg", [128, DH, TG])
        inside = sb("inside", [128, DH * TG])
        z_h = sb("z_h", [128, DH, TG], F16)
        z_l = sb("z_l", [128, DH, TG], F16)
        NV = 17
        vrows = sb("vrows", [NV, 128])
        vec = sb("vec", [128, NV])
        vec_s = sb("vec_s", [128, NV])
        srow = sb("srow", [1, 3])
        borow = sb("borow", [1, D])
        small = sb("small", [128, 4])
        wb2 = sb("wb2", [128, 2])
        gate_rows = sb("gate_rows", [TT, NT, 128])
        tri = sb("tri", [TT, TT])
        lnbb = sb("lnbb", [128, DH, TT])
        ident = sb("ident", [128, 128])
        ident16 = sb("ident16", [128, 128], F16)
        ones = sb("ones", [128, 128])
        gmask = sb("gmask", [TT, 2, TT])
        half_pi = sb("half_pi", [128, 1])
        p_minus_half = sb("p_minus_half", [TT, NT])
        p_half = sb("p_half", [TT, 2 * NT])
        kvg_flat, abs_flat = (a[:, :, :].rearrange("p h t -> p (h t)") for a in (kvg, th_abs))
        ph, ph_k, ph_abs = [kvg_flat[0:L, i * D:(i + 1) * D] for i in range(3)]
        ph_cs = abs_flat[0:L, 0:2 * D].rearrange("p (a d) -> p a d", a=2)
        table = sb("table", [128, 2, DH, L])
        bias_T = sb("bias_T", [TT, D])
        abs_sum = sb("abs_sum", [128, 2, 4])
        thr = sb("thr", [128, 4])
        thr_sum = sb("thr_sum", [128, 2])
        st = sb("st", [TT, NT, 6])
        mv = sb("mv", [TT, NT, 2])
        ve = sb("ve", [TT, NT])
        rstd = sb("rstd", [TT, NT])
        nmr = sb("nmr", [TT, NT])
        zst = sb("zst", [TT, NT, 6])
        zmv = sb("zmv", [TT, NT, 2])
        zve = sb("zve", [TT, NT])
        zrs = sb("zrs", [TT, NT])
        hst = sb("hst", [TT, NT, 6])
        hmv = sb("hmv", [TT, NT, 2])
        hvv = sb("hvv", [TT, 2, NT])
        hsq = sb("hsq", [TT, 2, NT])
        hf = sb("hf", [TT, NT])
        logit = sb("logit", [TT, NT, 3])
        logit_max = sb("logit_max", [TT, NT, 1])
        expo = sb("expo", [TT, NT, 3])
        denom = sb("denom", [TT, 2, NT])
        recip = sb("recip", [TT, 2, NT])
        bw = [sb(f"bw{i}", [TT, 2, NT]) for i in range(2)]
        gc = sb("gc", [TT, NT])
        gcr = [sb(f"gcr{i}", [TT, NT]) for i in range(2)]
        kvw = sb("kvw", [TT, NT])
        junk = sb("junk", [TT, 2 * TT])
        ss = sb("ss", [TT, NT])
        sr = sb("sr", [TT, NT])
        sf = sb("sf", [TT, NT])

        x_loaded = [sem(f"x_loaded{c}") for c in range(C)]
        x_sorted = sem("x_sorted")
        tokw_loaded = sem("tokw_loaded")
        tokwT_in_psum = sem("tokwT_in_psum")
        vec_loaded = sem("vec_loaded")
        aw_loaded = sem("aw_loaded")
        ph_loaded = sem("ph_loaded")
        up_loaded = sem("up_loaded")
        dn_loaded = sem("dn_loaded")
        out_stored = [sem(f"out_stored{i}") for i in range(2)]
        ident_done = sem("ident_done")
        consts_done = sem("consts_done")
        pool_step = sem("pool_step")
        dve_step = sem("dve_step")
        act_step = sem("act_step")
        vec_in_psum = sem("vec_in_psum")
        vec_done = sem("vec_done")
        tokw_head = sem("tokw_head")
        tokw_done = sem("tokw_done")
        ph_reduced = sem("ph_reduced")
        ph_cs_done = sem("ph_cs_done")
        abs_sum_done = sem("abs_sum_done")
        setup_in_psum = sem("setup_in_psum")
        setup_done = sem("setup_done")
        aw_head = sem("aw_head")
        aw_done = sem("aw_done")
        tern_done = sem("tern_done")
        ternT_in_psum = sem("ternT_in_psum")
        ternT_done = sem("ternT_done")
        xT_in_psum = sem("xT_in_psum")
        x_head = sem("x_head")
        x_rest = sem("x_rest")
        tok_chunk = sem("tok_chunk")
        hF_done = sem("hF_done")
        hT_in_psum = sem("hT_in_psum")
        ve_done = sem("ve_done")
        rstd_done = sem("rstd_done")
        nmr_done = sem("nmr_done")
        x1T_done = sem("x1T_done")
        res_done = sem("res_done")
        res_biased = sem("res_biased")
        x1F_in_psum = sem("x1F_in_psum")
        x1_head = sem("x1_head")
        x1_rest = sem("x1_rest")
        g1_in_psum = sem("g1_in_psum")
        bh_in_psum = sem("bh_in_psum")
        key_in_psum = sem("key_in_psum")
        pv_in_psum = sem("pv_in_psum")
        logits_in_psum = sem("logits_in_psum")
        gate_in_psum = sem("gate_in_psum")
        kv_in_psum = sem("kv_in_psum")
        gh_done = sem("gh_done")
        bh_done = sem("bh_done")
        th_done = sem("th_done")
        th_abs_done = sem("th_abs_done")
        logit_done = sem("logit_done")
        expo_done = sem("expo_done")
        key_cs_done = sem("key_cs_done")
        bw_done = sem("bw_done")
        gate_rows_done = sem("gate_rows_done")
        u_pos_done = sem("u_pos_done")
        gate_done = sem("gate_done")
        kvg_done = sem("kvg_done")
        u_kv_done = sem("u_kv_done")
        m_pos_done = sem("m_pos_done")
        m_kv_done = sem("m_kv_done")
        pos_ret_done = sem("pos_ret_done")
        kv_ret_done = sem("kv_ret_done")
        gc_done = sem("gc_done")
        gcr_done = sem("gcr_done")
        posT_in_psum = sem("posT_in_psum")
        kvT_in_psum = sem("kvT_in_psum")
        pos_scaled = sem("pos_scaled")
        blend_done = sem("blend_done")
        zve_done = sem("zve_done")
        zrs_done = sem("zrs_done")
        zT_done = sem("zT_done")
        zF_in_psum = sem("zF_in_psum")
        z_head = sem("z_head")
        z_rest = sem("z_rest")
        wo_in_psum = sem("wo_in_psum")
        h2_done = sem("h2_done")
        hvv_done = sem("hvv_done")
        hsq_done = sem("hsq_done")
        x2T_done = sem("x2T_done")
        x2F_in_psum = sem("x2F_in_psum")
        x2_head = sem("x2_head")
        x2_rest = sem("x2_rest")
        up_in_psum = sem("up_in_psum")
        gelu_done = sem("gelu_done")
        g_head = sem("g_head")
        g_rest = sem("g_rest")
        gram_in_psum = sem("gram_in_psum")
        ss_done = sem("ss_done")
        sr_done = sem("sr_done")
        down_in_psum = sem("down_in_psum")
        out_done = sem("out_done")

        BEFORE_Z = 6

        def last_group(g):
            return min(g, G - 1)

        def images(ap):
            return ap.rearrange("p (i l) -> p i l", i=IPG)

        def halves(ap):
            return ap.rearrange("p (h i l) -> p h i l", h=DH, i=IPG)

        def slot(w, s, k=0, width=256):
            return w[:, (s + k) * 256:(s + k) * 256 + width]

        def tiles(pair):
            return pair[0:TT, :, :].rearrange("p b (t d) -> p (b t) d", d=D)

        def flat_T(pair):
            return pair[0:TT, :, :].rearrange("p b n -> p (b n)")

        AW_ORDER = [G1, G1 + 1, G1 + 2, G1 + 3, KEY, KEY + 1, PV, PV + 1, KV, KV + 1, BH, WO, WO + 1]

        AHEAD = 3

        def x_bank(n):
            return (P01, P67)[n % 4 // 2][:, n % 2, :]

        def tokw_bank(c):
            return P23[:, c, :] if c < 2 else P45[:, 0, :]

        def gates_in(g):
            return P67 if g == 0 else P45

        block = ctx.enter_context(nc.Block())

        @block.sync
        def _(sp):
            def load_x(half, c):
                if half == 0:
                    sp.dma_start(x_raw[c][ROWS:ODD, :],
                                 x[0:ODD - ROWS, c, 0:PATCH, :].rearrange("n p w -> n (p w)")).then_inc(x_loaded[c], 16)
                else:
                    sp.wait_ge(x_sorted, c + 1)
                for b in range(2):
                    g = 2 * half + b
                    src = x[g * IPG:(g + 1) * IPG, c, :, :].rearrange("n (h p) w -> n h (p w)", p=PATCH)
                    sp.dma_start(x_raw[c][b * ODD:b * ODD + ROWS, :], src).then_inc(x_loaded[c], 16)

            sp.dma_start(tokw_f[:, :].rearrange("p (m d) -> p m d", m=DH),
                         tok_W.rearrange("(m p) d -> p m d", p=128)).then_inc(tokw_loaded, 16)
            for c in range(C):
                load_x(0, c)
            for v, row in ((tok_b, 0), (bpv, 2), (bk, 4), (bkv, 6), (bg1, 8), (bb1, 10), (ln_g, 11), (ln_b, 13)):
                n = v.shape[0] // 128
                sp.dma_start(vrows[row:row + n, :], v.rearrange("(m p) -> m p", p=128)).then_inc(vec_loaded, 16)
            sp.dma_start(vrows[15:17, :], Wg2.rearrange("(m p) o -> m (p o)", p=128)).then_inc(vec_loaded, 16)
            sp.dma_start(srow[:, 0:2], bb2.rearrange("(a n) -> a n", a=1)).then_inc(vec_loaded, 16)
            sp.dma_start(srow[:, 2:3], bg2.rearrange("(a n) -> a n", a=1)).then_inc(vec_loaded, 16)
            sp.dma_start(borow[:, :], bo.rearrange("(a n) -> a n", a=1)).then_inc(vec_loaded, 16)
            sp.dma_start(wb2[:, :], Wb2).then_inc(vec_loaded, 16)
            sp.dma_start(ph[:, :], phases[0:L, :]).then_inc(ph_loaded, 16)
            load_x(1, 0)
            for w, s, k in ((Wg1, G1, 4), (Wk, KEY, 2), (Wpv, PV, 2), (Wkv, KV, 2), (Wo, WO, 2)):
                sp.dma_start(aw_f[:, s * 256:(s + k) * 256].rearrange("p (k m) -> p k m", k=k),
                             w.rearrange("(k p) m -> p k m", p=128)).then_inc(aw_loaded, 16)
            sp.dma_start(slot(aw_f, BH).rearrange("p (k m) -> p k m", k=2),
                         Wb1.rearrange("(k p) m -> p k m", p=128)).then_inc(aw_loaded, 16)
            load_x(1, 1)
            load_x(1, 2)
            sp.dma_start(up_f[:, :].rearrange("p (f d) -> p f d", f=FC),
                         w_up.rearrange("(f p) d -> p f d", p=128)).then_inc(up_loaded, 16)
            sp.dma_start(dn_f[:, :].rearrange("p (h f) -> p h f", h=DH),
                         w_down.rearrange("(h p) f -> p h f", p=128)).then_inc(dn_loaded, 16)
            out_v = out.rearrange("(g i) l d -> g (i l) d", g=G)
            for g in range(G):
                for k in range(2):
                    sp.wait_ge(out_done, 2 * g + k + 1)
                    sp.dma_start(out_v[g][2 * k * TT:2 * (k + 1) * TT, :].rearrange("(t p) d -> p t d", p=TT),
                                 out_ring[g % 2][:, 2 * k * D:2 * (k + 1) * D].rearrange("p (t d) -> p t d", t=2)
                                 ).then_inc(out_stored[g % 2], 16)
            for i in range(2):
                sp.wait_ge(out_stored[i], 32 * G // 2)

        N_VEC = 13
        N_AW = 6

        @block.gpsimd
        def _(pool):
            steps = [0]

            def chained(ins):
                steps[0] += 1
                ins.then_inc(pool_step, 1)
                pool.wait_ge(pool_step, steps[0])

            chained(nc.gpsimd.memset(ident[:, :], 0.0))
            nc.gpsimd.affine_select(out=ident[:, :], in_=ident[:, :], compare_op=ALU.not_equal, fill=1.0,
                                    base=0, pattern=[[-1, 128]], channel_multiplier=1).then_inc(ident_done, 1)
            pool.wait_ge(ident_done, 1)
            nc.gpsimd.tensor_copy(ident16[:, :], ident[:, :]).then_inc(consts_done, 1)
            nc.gpsimd.tensor_copy(gmask[:, 0, :], ident[0:TT, 0:TT]).then_inc(consts_done, 1)
            nc.gpsimd.tensor_scalar(gmask[:, 1, :], ident[0:TT, 0:TT], 2.0, None, ALU.mult).then_inc(consts_done, 1)
            chained(nc.gpsimd.memset(tri[:, :], 1.0))
            chained(nc.gpsimd.affine_select(out=tri[:, :], in_=tri[:, :], compare_op=ALU.is_ge, fill=0.0, base=0,
                                            pattern=[[1, TT]], channel_multiplier=-1))
            nc.gpsimd.affine_select(out=tri[:, L:TT], in_=tri[:, L:TT], compare_op=ALU.is_ge, fill=0.0, base=-L,
                                    pattern=[[0, L]], channel_multiplier=1).then_inc(consts_done, 1)

            def weight_rests(order):
                for s in order:
                    pool.wait_ge(aw_head, AW_ORDER.index(s) + 1)
                    nc.gpsimd.tensor_tensor(slot(aw_l, s), slot(aw_f, s), slot(aw_h, s), ALU.subtract).then_inc(aw_done, 1)

            def pow_rstd(g):
                pool.wait_ge(ve_done, g + 1)
                nc.gpsimd.tensor_tensor(rstd[:, :], ve[:, :], p_minus_half[:, :], ALU.pow).then_inc(rstd_done, 1)

            def bias_res(g):
                pool.wait_ge(res_done, g + 1)
                pool.wait_ge(setup_done, 1)
                r = res[g][:, :].rearrange("p (t d) -> p t d", t=NT)
                nc.gpsimd.tensor_tensor(r, r, bias_T[:, :].unsqueeze(1).broadcast_to([TT, NT, D]),
                                        ALU.add).then_inc(res_biased, 1)

            pow_rstd(0)
            weight_rests(AW_ORDER[0:4])
            pow_rstd(1)
            weight_rests(AW_ORDER[4:8])
            pow_rstd(2)
            weight_rests(AW_ORDER[8:11])
            pow_rstd(3)

            def shifted_key_terms(g):
                b = g % 2
                pool.wait_ge(kvg_done, g + 1)
                pool.wait_ge(key_cs_done, g + 1)
                pool.wait_ge(m_kv_done, 2 * g)
                for u, key in ((u_kc, key_c), (u_ks, key_s)):
                    nc.gpsimd.tensor_tensor(halves(u), kvg[:, :, :].rearrange("p h (i l) -> p h i l", i=IPG),
                                            key[b][:, :, :, 0:L], ALU.mult).then_inc(u_kv_done, 1)

            def pow_z(g):
                pool.wait_ge(zve_done, g + 1)
                nc.gpsimd.tensor_tensor(zrs[:, :], zve[:, :], p_minus_half[:, :], ALU.pow).then_inc(zrs_done, 1)

            def pos_ret(g):
                for i, m in enumerate((m_pc, m_ps)):
                    pool.wait_ge(m_pos_done, 2 * g + i + 1)
                    tab = table[:, i, :, :].unsqueeze(2).broadcast_to([128, DH, IPG, L])
                    chained(nc.gpsimd.tensor_tensor(halves(m), halves(m), tab, ALU.mult))
                nc.gpsimd.tensor_tensor(m_pc, m_pc, m_ps, ALU.add).then_inc(pos_ret_done, 1)

            def kv_ret(g):
                for i, (m, key) in enumerate(((m_kc, key_c), (m_ks, key_s))):
                    pool.wait_ge(m_kv_done, 2 * g + i + 1)
                    chained(nc.gpsimd.tensor_tensor(halves(m), halves(m), key[g % 2][:, :, :, 1:PADL], ALU.mult))
                nc.gpsimd.tensor_tensor(m_kc, m_kc, m_ks, ALU.add).then_inc(kv_ret_done, 1)

            def pow_gc(g):
                pool.wait_ge(gc_done, g + 1)
                nc.gpsimd.tensor_tensor(gcr[g % 2][:, :], gc[:, :], p_minus_half[:, :], ALU.pow).then_inc(gcr_done, 1)

            def pow_h2(g):
                pool.wait_ge(hvv_done, g + 1)
                two = "p a t -> p (a t)"
                nc.gpsimd.tensor_tensor(hsq[:, :, :].rearrange(two), hvv[:, :, :].rearrange(two), p_half[:, :],
                                        ALU.pow).then_inc(hsq_done, 1)

            def pow_ss(g):
                pool.wait_ge(ss_done, g + 1)
                nc.gpsimd.tensor_tensor(sr[:, :], ss[:, :], p_half[:, 0:NT], ALU.pow).then_inc(sr_done, 1)

            for i in range(G + 2):
                a, t, f = i, i - 1, i - 2
                if a < G:
                    if a == 0:
                        pos_ret(0)
                    pow_gc(a)
                if 0 <= t < G:
                    pow_z(t)
                if a < G:
                    if a > 0:
                        pos_ret(a)
                    shifted_key_terms(a)
                if 0 <= t < G:
                    pow_h2(t)
                if 0 <= f < G:
                    pow_ss(f)
                if a < G:
                    kv_ret(a)
                    if a == 0:
                        weight_rests(AW_ORDER[11:])
                    bias_res(a)

        @block.scalar
        def _(act):
            for c in range(C):
                act.wait_ge(tokwT_in_psum, c + 1)
                s = slice(c * PH * D, (c + 1) * PH * D)
                nc.scalar.activation(tokw_h[:, s], tokw_bank(c), ACT.Copy, scale=WSCALE).then_inc(tokw_head, 1)

            def x_heads(g, j):
                n = g * KC + j
                act.wait_ge(xT_in_psum, n + 1)
                if n >= KC:
                    act.wait_ge(tok_chunk, n - KC + 1)
                nc.scalar.activation(x_h[:, j, :].rearrange("p (r w) -> p w r", w=SIDE),
                                     x_bank(n)[:, 0:TG].rearrange("p (w r) -> p w r", w=SIDE),
                                     ACT.Copy).then_inc(x_head, 1)

            def h_bias(g):
                act.wait_ge(tok_chunk, KC * (g + 1))
                act.wait_ge(vec_done, 1)
                if g >= 2:
                    act.wait_ge(hT_in_psum, g - 1)
                for m in range(DH):
                    ins = nc.scalar.activation(hF[g % 2][:, m, :], P23[:, m, 0:TG], ACT.Identity,
                                               bias=vec[:, m:m + 1], scale=INV)
                ins.then_inc(hF_done, 1)

            def normalise_h(g):
                act.wait_ge(nmr_done, g + 1)
                if g >= 2:
                    act.wait_ge(x1F_in_psum, g - 1)
                    act.wait_ge(res_done, g - 1)
                for t in range(NT):
                    ins = nc.scalar.activation(ring_T[g % 2][:, t * D:(t + 1) * D], tiles(P45)[:, t, :], ACT.Identity,
                                               bias=nmr[:, t:t + 1], scale=rstd[:, t:t + 1])
                ins.then_inc(x1T_done, 1)

            def x1_heads(g):
                act.wait_ge(x1F_in_psum, g + 1)
                nc.scalar.activation(x1_h[g][:, :, :, 1:PADL], P45[:, :, 0:TG].rearrange("p h (i l) -> p h i l", i=IPG),
                                     ACT.Copy).then_inc(x1_head, 1)

            def phase_tables():
                act.wait_ge(ph_reduced, 2)
                nc.scalar.activation(ph_cs[:, 1, :], ph[:, :], ACT.Sin)
                act.wait_ge(consts_done, 5)
                nc.scalar.activation(ph_cs[:, 0, :], ph_abs[:, :], ACT.Sin, bias=half_pi[0:L, :],
                                     scale=-1.0).then_inc(ph_cs_done, 1)

            def weight_sums(n, quarters):
                w, junk_w = ((up_f, up_t), (dn_f, dn_t))[n]
                act.wait_ge((up_loaded, dn_loaded)[n], 16)
                q = FC * D // 4
                for k in quarters:
                    nc.scalar.activation(junk_w[:, k * q:(k + 1) * q], w[:, k * q:(k + 1) * q], ACT.Abs,
                                         accum_out=abs_sum[:, n, k:k + 1]).then_inc(abs_sum_done, 1)

            def weight_heads(order):
                act.wait_ge(aw_loaded, 16 * N_AW)
                for s in order:
                    if s < WO:
                        nc.scalar.activation(slot(aw_f, s), slot(aw_f, s), ACT.Copy, scale=WSCALE).then_inc(act_step, 1)
                    else:
                        act.wait_ge(setup_in_psum, 1)
                        nc.scalar.activation(slot(aw_f, s), slot(aw_f, s), ACT.Copy,
                                             scale=vec_s[:, 11 + s - WO:12 + s - WO]).then_inc(act_step, 1)
                for s in order:
                    act.wait_ge(act_step, AW_ORDER.index(s) + 1)
                    nc.scalar.activation(slot(aw_h, s), slot(aw_f, s), ACT.Copy).then_inc(aw_head, 1)

            weights_at = {(1, 3): (0, 1), (1, 5): (1, 2), (2, 0): (2, 3), (2, 1): (3, 4), (2, 3): (4, 5), (2, 4): (5, 6),
                          (2, 5): (6, 7), (3, 0): (7, 8), (3, 1): (8, 10), (3, 4): (10, 11)}
            sums_at = {(3, 3): (0, range(0, 1)), (3, 4): (0, range(1, 2)), (3, 5): (0, range(2, 4)),
                       (4, 0): (1, range(0, 2)), (4, 1): (1, range(2, 4))}
            for g in range(G + 1):
                for j in range(KC):
                    if g < G:
                        x_heads(g, j)
                    if j == 0 and g >= 3:
                        x1_heads(g - 3)
                    if j == 2 and g >= 1:
                        h_bias(g - 1)
                    if j == 3 and g >= 2:
                        normalise_h(g - 2)
                    if g == 1 and j == 4:
                        phase_tables()
                    if (g, j) in weights_at:
                        first, end = weights_at[(g, j)]
                        weight_heads(AW_ORDER[first:end])
                    if (g, j) in sums_at:
                        weight_sums(*sums_at[(g, j)])

            def gelu_g1(g):
                for m in range(DH):
                    act.wait_ge(g1_in_psum, DH * g + m + 1)
                    if m == 0:
                        act.wait_ge(logits_in_psum, g)
                    ins = nc.scalar.activation(gh[:, m, :], P01[:, m, 0:TG], ACT.Gelu, bias=vec[:, 8 + m:9 + m],
                                               scale=INV)
                ins.then_inc(gh_done, 1)

            def gelu_bh(g):
                act.wait_ge(bh_in_psum, g + 1)
                act.wait_ge(logits_in_psum, g)
                nc.scalar.activation(bh[:, :], gates_in(g)[:, 0, 0:TG], ACT.Gelu, bias=vec[:, 10:11], scale=INV).then_inc(bh_done, 1)

            def tanh_key(g):
                for m in range(DH):
                    act.wait_ge(key_in_psum, DH * g + m + 1)
                    if m == 0:
                        act.wait_ge(key_cs_done, g)
                    ins = nc.scalar.activation(th[:, m, :], P23[:, m, 0:TG], ACT.Tanh, bias=vec[:, 4 + m:5 + m],
                                               scale=INV)
                ins.then_inc(th_done, 1)

            def exps(g):
                act.wait_ge(logit_done, g + 1)
                act.wait_ge(gate_rows_done, g)
                nc.scalar.activation(expo[:, :, :], logit[:, :, :], ACT.Exp).then_inc(expo_done, 1)

            def copy_gate(g):
                act.wait_ge(gate_in_psum, g + 1)
                act.wait_ge(kvg_done, g)
                nc.scalar.activation(gate, gates_in(g)[:, 1, 0:TG], ACT.Copy).then_inc(gate_done, 1)

            def keys(g):
                b = g % 2
                if g >= 2:
                    act.wait_ge(kv_ret_done, g - 1)
                act.wait_ge(th_done, g + 1)
                nc.scalar.activation(th_abs[:, :, :], th[:, :, :], ACT.Abs).then_inc(th_abs_done, 1)
                nc.scalar.activation(key_s[b][:, :, :, 1:PADL], th[:, :, :].rearrange("p h (i l) -> p h i l", i=IPG),
                                     ACT.Sin, scale=PI_BELOW)
                act.wait_ge(th_abs_done, g + 1)
                nc.scalar.activation(key_c[b][:, :, :, 1:PADL], th_abs[:, :, :].rearrange("p h (i l) -> p h i l", i=IPG),
                                     ACT.Sin, bias=half_pi[:, :], scale=-PI).then_inc(key_cs_done, 1)

            def scale_pos(g):
                act.wait_ge(posT_in_psum, g + 1)
                act.wait_ge(bw_done, g + 1)
                if g >= 1:
                    act.wait_ge(zF_in_psum, g)
                else:
                    act.wait_ge(x1F_in_psum, G)
                    act.wait_ge(res_done, G)
                for t in range(NT):
                    ins = nc.scalar.activation(ring_T[0][:, t * D:(t + 1) * D], tiles(P23)[:, t, :], ACT.Copy,
                                               scale=bw[g % 2][:, 0, t:t + 1])
                ins.then_inc(pos_scaled, 1)

            def z_heads(g):
                act.wait_ge(zF_in_psum, g + 1)
                act.wait_ge(wo_in_psum, g)
                nc.scalar.activation(z_h[:, :, :], P67[:, :, 0:TG], ACT.Copy).then_inc(z_head, 1)

            def x2_heads(g):
                act.wait_ge(x2F_in_psum, g + 1)
                nc.scalar.activation(x2_h[g], P67[:, :, 0:TG], ACT.Copy).then_inc(x2_head, 1)

            def ffn_gelus(g, chunks):
                for f in chunks:
                    n = FC * g + f
                    act.wait_ge(up_in_psum, n + 1)
                    if n >= 3:
                        act.wait_ge(g_rest, n - 2)
                    nc.scalar.activation(gelu_ring[n % 3], P23[:, f % 2, 0:TG], ACT.Gelu).then_inc(gelu_done, 1)
                    if f % 2 == 0:
                        act.wait_ge(gelu_done, n + 1)
                        if f == 0:
                            act.wait_ge(down_in_psum, 2 * g)
                        nc.scalar.activation(ghl[:, f, 0, :], gelu_ring[n % 3], ACT.Copy).then_inc(g_head, 1)

            def ternary_copies():
                for n in range(4):
                    act.wait_ge(ternT_in_psum, n + 1)
                    dst = upT[:, n, :] if n < DH else \
                        dnT[:, (n - DH) * 4:(n - DH) * 4 + 4, :].rearrange("p f d -> p (f d)")
                    nc.scalar.activation(dst, P67[:, n % 2, :].bitcast(F16), ACT.Copy).then_inc(ternT_done, 1)

            for i in range(G + 2):
                a, t, f = i, i - 1, i - 2
                if 0 <= f < G:
                    x2_heads(f)
                if a == 0:
                    gelu_g1(0)
                    x1_heads(G - 2)
                    tanh_key(0)
                    gelu_bh(0)
                    normalise_h(G - 1)
                    exps(0)
                    keys(0)
                    x1_heads(G - 1)
                    copy_gate(0)
                    weight_heads(AW_ORDER[11:])
                elif a < G:
                    gelu_bh(a)
                    gelu_g1(a)
                    exps(a)
                    if a == 1:
                        ternary_copies()
                    copy_gate(a)
                if 0 <= t < G:
                    scale_pos(t)
                if 0 < a < G:
                    tanh_key(a)
                if 0 <= f < G:
                    ffn_gelus(f, range(0, BEFORE_Z))
                if 0 <= t < G:
                    z_heads(t)
                if 0 <= f < G:
                    ffn_gelus(f, range(BEFORE_Z, FC))
                if 0 < a < G:
                    keys(a)

        @block.vector
        def _(dve):
            steps = [0]

            def chained(ins):
                steps[0] += 1
                ins.then_inc(dve_step, 1)
                dve.wait_ge(dve_step, steps[0])

            nc.vector.memset(half_pi[:, :], PI / 2).then_inc(consts_done, 1)
            chained(nc.vector.memset(ones[:, :], 1.0))
            nc.vector.memset(p_minus_half[:, :], -0.5)
            nc.vector.memset(p_half[:, :], 0.5)
            chained(nc.vector.memset(inside[:, :], 1.0))
            nc.vector.memset(inside[:, :].rearrange("p (n l) -> p n l", l=L)[:, :, 0:1], 0.0)
            for a in [*x1_h, *x1_l, *key_c, *key_s]:
                ins = nc.vector.memset(a[:, :, :, 0:1], 0.0)
            chained(ins)

            def vectors():
                dve.wait_ge(vec_in_psum, 1)
                chained(nc.vector.tensor_copy(vec[:, :], P45[:, 1, 0:NV]))
                nc.vector.tensor_copy(small[:, 0:3], P45[:, 1, 32:35])
                nc.vector.tensor_scalar(vec_s[:, :], vec[:, :], WSCALE, None, ALU.mult)
                for k in range(DH):
                    ins = nc.vector.tensor_scalar(lnbb[:, k, :], ones[:, 0:TT], vec[:, 13 + k:14 + k], None, ALU.mult)
                ins.then_inc(vec_done, 1)

            def reduce_phases():
                dve.wait_ge(ph_loaded, 16)
                chained(nc.vector.tensor_scalar(ph_k[:, :], ph[:, :], 0.5 / PI, ROUND_MAGIC, ALU.mult, ALU.add))
                chained(nc.vector.tensor_scalar(ph_k[:, :], ph_k[:, :], ROUND_MAGIC, None, ALU.subtract))
                for part in TWO_PI_PARTS:
                    chained(nc.vector.scalar_tensor_tensor(out=ph[:, :], in0=ph_k[:, :], scalar=-part, in1=ph[:, :],
                                                           op0=ALU.mult, op1=ALU.add))
                nc.vector.tensor_scalar(ph[:, :], ph[:, :], PI_BELOW, -PI_BELOW, ALU.min, ALU.max).then_inc(ph_reduced, 1)
                dve.wait_ge(ph_reduced, 1)
                nc.vector.scalar_tensor_tensor(out=ph_abs, in0=ph, scalar=-1.0, in1=ph, op0=ALU.mult,
                                               op1=ALU.max).then_inc(ph_reduced, 1)

            def sort_pixels(half, c):
                dve.wait_ge(x_loaded[c], 48 + 32 * half)
                if half > 0:
                    dve.wait_ge(xT_in_psum, KC + (c + 1) * PH)
                n = ODD + ROWS
                nc.vector.tensor_copy(x_pat[c][0:n, :].rearrange("r (w p q) -> r p w q", w=SIDE, p=PATCH),
                                      x_raw[c][0:n, :].rearrange("r (p w q) -> r p w q", w=SIDE, p=PATCH)
                                      ).then_inc(x_sorted, 1)

            def x_rests(g, j):
                n = g * KC + j
                dve.wait_ge(x_head, n + 1)
                nc.vector.tensor_tensor(x_l[:, j, :].rearrange("p (r w) -> p w r", w=SIDE),
                                        x_bank(n)[:, 0:TG].rearrange("p (w r) -> p w r", w=SIDE),
                                        x_h[:, j, :].rearrange("p (r w) -> p w r", w=SIDE),
                                        ALU.subtract).then_inc(x_rest, 1)

            def stats(src, st_, mv_):
                for t in range(NT):
                    ins = nc.vector.bn_stats(st_[:, t, :], src(t))
                chained(ins)
                for t in range(NT):
                    ins = nc.vector.bn_aggr(mv_[:, t, :], st_[:, t, :])
                chained(ins)

            def stats_h(g):
                dve.wait_ge(hT_in_psum, g + 1)
                dve.wait_ge(nmr_done, g)
                stats(lambda t: tiles(P45)[:, t, :], st, mv)
                nc.vector.tensor_scalar(ve[:, :], mv[:, :, 1], LN_EPS, None, ALU.add).then_inc(ve_done, 1)

            def mean_h(g):
                dve.wait_ge(rstd_done, g + 1)
                dve.wait_ge(x1T_done, g)
                nc.vector.scalar_tensor_tensor(out=nmr[:, :], in0=mv[:, :, 0], scalar=-1.0, in1=rstd[:, :],
                                               op0=ALU.mult, op1=ALU.mult).then_inc(nmr_done, 1)

            def residual(g):
                dve.wait_ge(x1T_done, g + 1)
                nc.vector.tensor_tensor(res[g][:, :], flat_T(P45), ring_T[g % 2][:, :], ALU.add).then_inc(res_done, 1)

            def x1_rests(g):
                dve.wait_ge(x1_head, g + 1)
                nc.vector.tensor_tensor(x1_l[g][:, :, :, 1:PADL], P45[:, :, 0:TG].rearrange("p h (i l) -> p h i l", i=IPG),
                                        x1_h[g][:, :, :, 1:PADL], ALU.subtract).then_inc(x1_rest, 1)

            def setup_copies():
                dve.wait_ge(setup_in_psum, 1)
                nc.vector.tensor_copy(table[:, :, :, :].rearrange("p a h l -> p (a h l)"), P67[:, 0, 0:2 * DH * L])
                nc.vector.tensor_copy(bias_T[:, :], P67[0:TT, 1, 0:D])
                chained(nc.vector.tensor_reduce(thr_sum[:, :], P67[:, 1, 256:264].rearrange("p (n k) -> p n k", k=4),
                                                mybir.AxisListType.X, ALU.add))
                nc.vector.tensor_scalar(thr[:, 0:2], thr_sum[:, :], 0.5 / (F * D), None, ALU.mult)
                nc.vector.tensor_scalar(thr[:, 2:4], thr_sum[:, :], -0.5 / (F * D), None, ALU.mult).then_inc(setup_done, 1)

            def ternary(w, t, n):
                dve.wait_ge(setup_done, 1)
                dve.wait_ge(tern_done, n)
                chained(nc.vector.tensor_scalar(above[:, :], w[:, :], thr[:, 2 + n:3 + n], None, ALU.is_lt))
                nc.vector.scalar_tensor_tensor(out=t[:, :], in0=w[:, :], scalar=thr[:, n:n + 1], in1=above[:, :],
                                               op0=ALU.is_gt, op1=ALU.subtract).then_inc(tern_done, 1)

            sort_pixels(0, 0)
            for c in range(C):
                dve.wait_ge(tokw_head, c + 1)
                s = slice(c * PH * D, (c + 1) * PH * D)
                nc.vector.scalar_tensor_tensor(out=tokw_l[:, s], in0=tokw_bank(c), scalar=WSCALE, in1=tokw_h[:, s],
                                               op0=ALU.mult, op1=ALU.subtract).then_inc(tokw_done, 1)
            for g in range(G + 1):
                for j in range(KC):
                    if g < G:
                        x_rests(g, j)
                    if g == 0 and j < C - 1:
                        sort_pixels(0, j + 1)
                    if g == 1 and j == 0:
                        vectors()
                    if g == 1 and j == 1:
                        reduce_phases()
                    if g == 1 and j % PH == PH - 1:
                        sort_pixels(1, j // PH)
                    if g >= 3 and j == 0:
                        x1_rests(g - 3)
                    if g >= 2 and j == 1:
                        stats_h(g - 2)
                    if g >= 2 and j == 3:
                        mean_h(g - 2)
                    if g >= 2 and j == 4:
                        residual(g - 2)
            setup_copies()
            x1_rests(G - 2)

            def pos_terms(g, i):
                u = (u_pc, u_ps)[i]
                if i == 0:
                    dve.wait_ge(pv_in_psum, g + 1)
                    dve.wait_ge(m_pos_done, 2 * g)
                for m in range(DH):
                    ins = nc.vector.scalar_tensor_tensor(
                        out=images(u[:, m * TG:(m + 1) * TG]), in0=images(P67[:, m, 0:TG]),
                        scalar=vec_s[:, 2 + m:3 + m], in1=table[:, i, m, :].unsqueeze(1).broadcast_to([128, IPG, L]),
                        op0=ALU.add, op1=ALU.mult)
                ins.then_inc(u_pos_done, 1)

            def logits(g):
                dve.wait_ge(logits_in_psum, g + 1)
                dve.wait_ge(expo_done, g)
                chained(nc.vector.tensor_tensor(logit[:, :, :],
                                                gates_in(g)[0:TT, 1, 0:3 * NT].rearrange("p (t c) -> p t c", c=3),
                                                small[0:TT, 0:3].unsqueeze(1).broadcast_to([TT, NT, 3]), ALU.add))
                nc.vector.tensor_scalar(logit[:, :, 2:3], logit[:, :, 2:3], -1.0, None, ALU.mult)
                chained(nc.vector.tensor_tensor(logit_max[:, :, :], logit[:, :, 0:1], logit[:, :, 1:2], ALU.max))
                nc.vector.tensor_tensor(logit[:, :, 0:2], logit[:, :, 0:2], logit_max[:, :, :].broadcast_to([TT, NT, 2]),
                                        ALU.subtract).then_inc(logit_done, 1)

            def weights(g):
                b = bw[g % 2]
                dve.wait_ge(expo_done, g + 1)
                dve.wait_ge(gate_rows_done, g)
                if g >= 1:
                    dve.wait_ge(gate_in_psum, g)
                if g >= 2:
                    dve.wait_ge(pos_scaled, g - 1)
                nc.vector.tensor_tensor(denom[:, 0, :], expo[:, :, 0], expo[:, :, 1], ALU.add)
                chained(nc.vector.tensor_scalar(denom[:, 1, :], expo[:, :, 2], 1.0, None, ALU.add))
                chained(nc.vector.reciprocal(recip[:, :, :], denom[:, :, :]))
                for t in range(NT):
                    nc.vector.tensor_scalar(gate_rows[:, t, :], ones[0:TT, :], recip[:, 1, t:t + 1], None, ALU.mult)
                for c in range(2):
                    ins = nc.vector.scalar_tensor_tensor(out=b[:, c, :], in0=expo[:, :, c], scalar=INV / D ** 0.5,
                                                         in1=recip[:, 0, :], op0=ALU.mult, op1=ALU.mult)
                    ins.then_inc((bw_done, gate_rows_done)[c], 1)

            def gated_values(g):
                dve.wait_ge(kv_in_psum, g + 1)
                dve.wait_ge(gate_done, g + 1)
                dve.wait_ge(u_kv_done, 2 * g)
                for m in range(DH):
                    ins = nc.vector.scalar_tensor_tensor(out=kvg[:, m, :], in0=P01[:, m, 0:TG],
                                                         scalar=vec_s[:, 6 + m:7 + m], in1=gate, op0=ALU.add,
                                                         op1=ALU.mult)
                ins.then_inc(kvg_done, 1)

            def gate_count(g):
                dve.wait_ge(gate_in_psum, g + 1)
                dve.wait_ge(gcr_done, g)
                nc.vector.tensor_scalar(gc[:, :], gates_in(g)[0:TT, 0, 0:NT], 1.0, None, ALU.max).then_inc(gc_done, 1)

            def scan(m, u, done):
                nc.vector.tensor_tensor_scan(m, inside[:, :], u, 0.0, ALU.mult, ALU.add).then_inc(done, 1)

            def scan_pos(g):
                dve.wait_ge(u_pos_done, 2 * g + 2)
                dve.wait_ge(posT_in_psum, g)
                scan(m_pc, u_pc, m_pos_done)
                scan(m_ps, u_ps, m_pos_done)

            def scan_kv(g):
                dve.wait_ge(u_kv_done, 2 * g + 1)
                dve.wait_ge(kvT_in_psum, g)
                scan(m_kc, u_kc, m_kv_done)
                dve.wait_ge(u_kv_done, 2 * g + 2)
                scan(m_ks, u_ks, m_kv_done)

            def kv_weight(g):
                dve.wait_ge(gcr_done, g + 1)
                dve.wait_ge(gate_rows_done, g + 1)
                dve.wait_ge(blend_done, g)
                chained(nc.vector.tensor_tensor(kvw[:, :], bw[g % 2][:, 1, :], gcr[g % 2][:, :], ALU.mult))

            def blend(g):
                kv_weight(g)
                dve.wait_ge(kvT_in_psum, g + 1)
                dve.wait_ge(pos_scaled, g + 1)
                for t in range(NT):
                    r = ring_T[0][:, t * D:(t + 1) * D]
                    ins = nc.vector.scalar_tensor_tensor(out=r, in0=tiles(P45)[:, t, :], scalar=kvw[:, t:t + 1], in1=r,
                                                         op0=ALU.mult, op1=ALU.add)
                ins.then_inc(blend_done, 1)
                dve.wait_ge(blend_done, g + 1)
                dve.wait_ge(zT_done, g)
                stats(lambda t: ring_T[0][:, t * D:(t + 1) * D], zst, zmv)
                nc.vector.tensor_scalar(zve[:, :], zmv[:, :, 1], LN_EPS, None, ALU.add).then_inc(zve_done, 1)

            def normalise(dst, src, mean, scale):
                for t in range(NT):
                    s = slice(t * D, (t + 1) * D)
                    ins = nc.vector.tensor_scalar(dst[:, s], src[:, s], mean[:, t, 0:1], scale[:, t:t + 1],
                                                  ALU.subtract, ALU.mult)
                return ins

            def normalise_z(g):
                dve.wait_ge(zrs_done, g + 1)
                normalise(ring_T[0], ring_T[0], zmv, zrs).then_inc(zT_done, 1)

            def z_rests(g):
                dve.wait_ge(z_head, g + 1)
                nc.vector.tensor_tensor(z_l[:, :, :], P67[:, :, 0:TG], z_h[:, :, :], ALU.subtract).then_inc(z_rest, 1)

            def second_residual(g):
                dve.wait_ge(wo_in_psum, g + 1)
                dve.wait_ge(res_biased, g + 1)
                dve.wait_ge(x2T_done, g)
                nc.vector.scalar_tensor_tensor(out=res[g][:, :], in0=flat_T(P01), scalar=INV, in1=res[g][:, :],
                                               op0=ALU.mult, op1=ALU.add).then_inc(h2_done, 1)
                dve.wait_ge(h2_done, g + 1)
                stats(lambda t: res[g][:, t * D:(t + 1) * D], hst, hmv)
                nc.vector.tensor_copy(hvv[:, 0, :], hmv[:, :, 1])
                nc.vector.tensor_scalar(hvv[:, 1, :], hmv[:, :, 1], LN_EPS, None, ALU.add).then_inc(hvv_done, 1)

            def normalise_h2(g):
                dve.wait_ge(hsq_done, g + 1)
                dve.wait_ge(x2F_in_psum, g)
                chained(nc.vector.scalar_tensor_tensor(out=hf[:, :], in0=hsq[:, 1, :], scalar=RMS_EPS, in1=hsq[:, 0, :],
                                                       op0=ALU.mult, op1=ALU.add))
                chained(nc.vector.reciprocal(hf[:, :], hf[:, :]))
                normalise(ring_T[1], res[g], hmv, hf).then_inc(x2T_done, 1)

            def x2_rests(g):
                dve.wait_ge(x2_head, g + 1)
                nc.vector.tensor_tensor(x2_l[g], P67[:, :, 0:TG], x2_h[g], ALU.subtract).then_inc(x2_rest, 1)

            def hidden_rests(g, chunks):
                for f in chunks:
                    n = FC * g + f
                    if f % 2 == 0:
                        dve.wait_ge(g_head, n // 2 + 1)
                    else:
                        dve.wait_ge(gelu_done, n + 1)
                        chained(nc.vector.tensor_copy(ghl[:, f, 0, :], gelu_ring[n % 3]))
                    nc.vector.tensor_tensor(ghl[:, f, 1, :], gelu_ring[(FC * g + f) % 3], ghl[:, f, 0, :],
                                            ALU.subtract).then_inc(g_rest, 1)

            def square_sums(g):
                dve.wait_ge(gram_in_psum, g + 1)
                dve.wait_ge(sr_done, g)
                dve.wait_ge(ss_done, g)
                dve.wait_ge(consts_done, 5)
                for t in range(NT):
                    ins = nc.vector.tensor_tensor_reduce(
                        out=junk[:, :], in0=P45[0:TT, t // 2, (t % 2) * 2 * TT:(t % 2 + 1) * 2 * TT],
                        in1=gmask[:, :, :].rearrange("p a t -> p (a t)"), scale=1.0, scalar=0.0, op0=ALU.mult,
                        op1=ALU.add, accum_out=ss[:, t:t + 1])
                    if t < NT - 1:
                        chained(ins)
                ins.then_inc(ss_done, 1)

            def outputs(g):
                dve.wait_ge(sr_done, g + 1)
                dve.wait_ge(out_done, 2 * g)
                chained(nc.vector.tensor_scalar(sf[:, :], sr[:, :], F ** -0.5, RMS_EPS, ALU.mult, ALU.add))
                chained(nc.vector.reciprocal(sf[:, :], sf[:, :]))
                if g >= 2:
                    dve.wait_ge(out_stored[g % 2], 32 * (g // 2))
                for t in range(NT):
                    if t % 2 == 0:
                        dve.wait_ge(down_in_psum, 2 * g + t // 2 + 1)
                    ins = nc.vector.scalar_tensor_tensor(out=out_ring[g % 2][:, t * D:(t + 1) * D],
                                                         in0=tiles(P23)[:, t, :], scalar=sf[:, t:t + 1],
                                                         in1=res[g][:, t * D:(t + 1) * D], op0=ALU.mult, op1=ALU.add)
                    if t % 2 == 1:
                        ins.then_inc(out_done, 1)

            for i in range(G + 3):
                a, t, f, o = i, i - 1, i - 2, i - 3
                if 0 <= o < G:
                    outputs(o)
                if a == 0:
                    pos_terms(0, 0)
                    pos_terms(0, 1)
                    stats_h(G - 1)
                    mean_h(G - 1)
                    scan_pos(0)
                if 0 <= f < G:
                    x2_rests(f)
                if a < G:
                    logits(a)
                    if a == 0:
                        residual(G - 1)
                    weights(a)
                    if a == 0:
                        x1_rests(G - 1)
                    else:
                        pos_terms(a, 0)
                        pos_terms(a, 1)
                    gate_count(a)
                    gated_values(a)
                if 0 <= t < G:
                    blend(t)
                if 0 < a < G:
                    scan_pos(a)
                if a == 0:
                    ternary(up_f, up_t, 0)
                    ternary(dn_f, dn_t, 1)
                if 0 <= f < G:
                    hidden_rests(f, range(0, 2))
                if 0 <= t < G:
                    normalise_z(t)
                if 0 <= f < G:
                    hidden_rests(f, range(2, BEFORE_Z))
                if 0 <= t < G:
                    z_rests(t)
                if 0 <= f < G:
                    hidden_rests(f, range(BEFORE_Z, FC))
                if 0 <= t < G:
                    second_residual(t)
                if a < G:
                    scan_kv(a)
                if 0 <= t < G:
                    normalise_h2(t)
                if 0 <= f < G:
                    square_sums(f)

        @block.tensor
        def _(pe):
            mm = nc.tensor.matmul

            pe.wait_ge(ident_done, 1)
            pe.wait_ge(tokw_loaded, 16)
            w_in = tokw_f[:, :].rearrange("p (m h j c) -> p m c h j", m=DH, h=PH, c=C)
            for c in range(C):
                for h in range(PH):
                    for m in range(DH):
                        k = h * D + m * 128
                        ins = nc.tensor.transpose(tokw_bank(c)[:, k:k + 128], w_in[:, m, c, h, :], ident[:, :])
                ins.then_inc(tokwT_in_psum, 1)

            def vector_columns():
                pe.wait_ge(dve_step, 1)
                pe.wait_ge(vec_loaded, 16 * N_VEC)
                nc.tensor.transpose(P45[:, 1, 0:NV], vrows[:, :], ident[0:NV, 0:NV])
                mm(P45[:, 1, 32:35], ones[0:1, :], srow[:, :], start=True, stop=True).then_inc(vec_in_psum, 1)

            def x_transposes(g, j):
                n, c, h = g * KC + j, j // PH, j % PH
                if j % PH == 0:
                    pe.wait_ge(x_sorted, C * (g // 2) + c + 1)
                if n >= 4:
                    pe.wait_ge(x_rest, n - 3)
                lo = (g % 2) * ODD
                for w in range(SIDE):
                    ins = nc.tensor.transpose(x_bank(n)[:, w * ROWS:(w + 1) * ROWS],
                                              x_pat[c][lo:lo + ROWS, (w * PH + h) * 128:(w * PH + h + 1) * 128],
                                              ident[lo:lo + ROWS, lo:lo + ROWS])
                ins.then_inc(xT_in_psum, 1)

            def embed(g, j):
                n = g * KC + j
                pe.wait_ge(x_rest, n + 1)
                if g == 0:
                    pe.wait_ge(tokw_done, C)
                if j == 0 and g >= 1:
                    pe.wait_ge(hF_done, g)
                for m in range(DH):
                    for i, (w, v) in enumerate(((tokw_h, x_h), (tokw_h, x_l), (tokw_l, x_h))):
                        ins = mm(P23[:, m, 0:TG], w[:, j * D + m * 128:j * D + (m + 1) * 128], v[:, j, :],
                                 start=(j == 0 and i == 0), stop=(j == KC - 1 and i == 2))
                ins.then_inc(tok_chunk, 1)

            def to_T(src, dst):
                for t in range(NT):
                    for m in range(DH):
                        ins = nc.tensor.transpose(tiles(dst)[:, t, m * 128:(m + 1) * 128], src(m, t), ident[:, :])
                return ins

            def to_F(src, dst):
                for m in range(DH):
                    for t in range(NT):
                        ins = nc.tensor.transpose(dst[:, m, t * TT:(t + 1) * TT],
                                                  src[:, t * D + m * 128:t * D + (m + 1) * 128], ident[0:TT, 0:TT])
                return ins

            def h_to_T(g):
                pe.wait_ge(hF_done, g + 1)
                pe.wait_ge(x1_rest, g)
                if g == 0:
                    pe.wait_ge(tokw_done, C)
                    pe.wait_ge(vec_done, 1)
                to_T(lambda m, t: hF[g % 2][:, m, t * TT:(t + 1) * TT], P45).then_inc(hT_in_psum, 1)

            def x1_to_F(g):
                pe.wait_ge(x1T_done, g + 1)
                pe.wait_ge(res_done, g + 1)
                to_F(ring_T[g % 2], P45).then_inc(x1F_in_psum, 1)

            def setup():
                pe.wait_ge(x_rest, KC * G)
                pe.wait_ge(ph_cs_done, 1)
                for a in range(2):
                    for m in range(DH):
                        k = (a * DH + m) * L
                        nc.tensor.transpose(P67[:, 0, k:k + L], ph_cs[:, a, m * 128:(m + 1) * 128], ident[0:L, 0:L])
                pe.wait_ge(vec_done, 1)
                pe.wait_ge(aw_loaded, 16 * N_AW)
                for k in range(DH):
                    mm(P67[0:TT, 1, 0:D], lnbb[:, k, :], slot(aw_f, WO, k), start=(k == 0), stop=False)
                mm(P67[0:TT, 1, 0:D], ones[0:1, 0:TT], borow[:, :], start=False, stop=True)
                pe.wait_ge(abs_sum_done, 8)
                mm(P67[:, 1, 256:264], ones[:, :], abs_sum[:, :, :].rearrange("p n k -> p (n k)"), start=True,
                   stop=True).then_inc(setup_in_psum, 1)

            def project(pair, b, s, width, m, g, chunks):
                total = 3 * len(chunks)
                n = 0
                for k, (half, first) in enumerate(chunks):
                    v_h, v_l = (a[g][:, half, :, first:first + L] for a in (x1_h, x1_l))
                    at = s * 256 + k * width + m * 128
                    for w, v in ((aw_h, v_h), (aw_h, v_l), (aw_l, v_h)):
                        ins = mm(images(pair[:, b, 0:TG]), w[:, at:at + 128], v, start=(n == 0), stop=(n == total - 1))
                        n += 1
                return ins

            HERE = [(h, 1) for h in range(DH)]
            BEFORE = [(h, 0) for h in range(DH)]

            def gate_hidden(g):
                pe.wait_ge(x1_rest, g + 1)
                if g == 0:
                    pe.wait_ge(aw_done, 4)
                    pe.wait_ge(x_rest, KC * G)
                if g == 1:
                    pe.wait_ge(kvg_done, 1)
                if g >= 2:
                    pe.wait_ge(h2_done, g - 1)
                for m in range(DH):
                    project(P01, m, G1, D, m, g, HERE + BEFORE).then_inc(g1_in_psum, 1)

            def blend_hidden(g):
                if g == 0:
                    pe.wait_ge(u_pos_done, 2)
                    pe.wait_ge(aw_done, 11)
                if g == 1:
                    pe.wait_ge(x1_rest, G)
                if g >= 2:
                    pe.wait_ge(blend_done, g - 1)
                if g >= 3:
                    pe.wait_ge(ss_done, g - 2)
                project(gates_in(g), 0, BH, 128, 0, g, HERE).then_inc(bh_in_psum, 1)

            def key_phases(g):
                if g == 0:
                    pe.wait_ge(hF_done, G)
                    pe.wait_ge(aw_done, 10)
                else:
                    pe.wait_ge(pos_scaled, g)
                for m in range(DH):
                    project(P23, m, KEY, D, m, g, HERE).then_inc(key_in_psum, 1)

            def pos_values(g):
                if g == 0:
                    pe.wait_ge(setup_done, 1)
                if g == 1:
                    pe.wait_ge(ternT_done, 4)
                if g >= 1:
                    pe.wait_ge(u_pos_done, 2 * g)
                if g >= 2:
                    pe.wait_ge(x2_rest, g - 1)
                for m in range(DH):
                    ins = project(P67, m, PV, D, m, g, HERE)
                ins.then_inc(pv_in_psum, 1)

            def kv_values(g):
                pe.wait_ge(gh_done, g + 1)
                for m in range(DH):
                    ins = project(P01, m, KV, D, m, g, HERE)
                ins.then_inc(kv_in_psum, 1)

            def token_logits(g):
                pe.wait_ge(gh_done, g + 1)
                pe.wait_ge(bh_done, g + 1)
                for t in range(NT):
                    s = slice(t * TT, (t + 1) * TT)
                    mm(gates_in(g)[0:TT, 1, 3 * t:3 * t + 2], bh[:, s], wb2[:, :], start=True, stop=True)
                    for k in range(DH):
                        ins = mm(gates_in(g)[0:TT, 1, 3 * t + 2:3 * t + 3], gh[:, k, s], vec[:, 15 + k:16 + k],
                                 start=(k == 0), stop=(k == DH - 1))
                ins.then_inc(logits_in_psum, 1)

            def spread_gates(g):
                pe.wait_ge(gate_rows_done, g + 1)
                pe.wait_ge(logit_done, g + 1)
                pe.wait_ge(consts_done, 5)
                mm(gates_in(g)[0:TT, 0, 0:NT], tri[:, :], recip[:, 1, :], start=True, stop=True)
                for t in range(NT):
                    ins = mm(gates_in(g)[:, 1, t * TT:(t + 1) * TT], gate_rows[:, t, :], ident[0:TT, 0:TT], start=True,
                             stop=True)
                ins.then_inc(gate_in_psum, 1)

            def ternary_to_F():
                pe.wait_ge(gate_done, 1)
                pe.wait_ge(gc_done, 1)
                pe.wait_ge(consts_done, 5)
                for n in range(4):
                    b = P67[:, n % 2, :].bitcast(F16)
                    pe.wait_ge(tern_done, n // 2 + 1)
                    if n >= 2:
                        pe.wait_ge(ternT_done, n - 1)
                    for q in range(8):
                        if n < DH:
                            src = up_t[:, q * D + n * 128:q * D + (n + 1) * 128]
                        else:
                            f, m = (n - DH) * 4 + q // 2, q % 2
                            src = dn_t[:, m * F + f * 128:m * F + (f + 1) * 128]
                        ins = nc.tensor.transpose(b[:, q * 128:(q + 1) * 128], src, ident16[:, :])
                    ins.then_inc(ternT_in_psum, 1)

            def returns_to_T(g):
                after = last_group(g + 1) + 1
                pe.wait_ge(pos_ret_done, g + 1)
                pe.wait_ge(th_done, g + 1)
                if g >= 2:
                    pe.wait_ge(out_done, 2 * (g - 1))
                to_T(lambda m, t: m_pc[:, m * TG + t * TT:m * TG + (t + 1) * TT], P23).then_inc(posT_in_psum, 1)
                pe.wait_ge(kv_ret_done, g + 1)
                pe.wait_ge(gc_done, after)
                pe.wait_ge(gate_done, after)
                if g >= 2:
                    pe.wait_ge(ss_done, g - 1)
                to_T(lambda m, t: m_kc[:, m * TG + t * TT:m * TG + (t + 1) * TT], P45).then_inc(kvT_in_psum, 1)

            def z_to_F(g):
                pe.wait_ge(zT_done, g + 1)
                pe.wait_ge(u_pos_done, 2 * (last_group(g + 1) + 1))
                if g >= 1:
                    pe.wait_ge(x2_rest, g)
                to_F(ring_T[0], P67).then_inc(zF_in_psum, 1)

            def attention_out(g):
                pe.wait_ge(z_rest, g + 1)
                pe.wait_ge(aw_done, NSLOT)
                pe.wait_ge(kvg_done, last_group(g + 1) + 1)
                for t in range(NT):
                    n = 0
                    for k in range(DH):
                        for v, w in ((z_h, aw_h), (z_l, aw_h), (z_h, aw_l)):
                            ins = mm(tiles(P01)[:, t, :], v[:, k, t * TT:(t + 1) * TT], slot(w, WO, k), start=(n == 0),
                                     stop=(n == 3 * DH - 1))
                            n += 1
                ins.then_inc(wo_in_psum, 1)

            def x2_to_F(g):
                pe.wait_ge(x2T_done, g + 1)
                pe.wait_ge(z_rest, g + 1)
                to_F(ring_T[1], P67).then_inc(x2F_in_psum, 1)

            def ffn_up(g, chunks):
                pe.wait_ge(x2_rest, g + 1)
                pe.wait_ge(ternT_done, 4)
                pe.wait_ge(th_done, last_group(g + 2) + 1)
                pe.wait_ge(pos_scaled, last_group(g + 1) + 1)
                if g >= 1:
                    pe.wait_ge(out_done, 2 * g)
                for f in chunks:
                    n = FC * g + f
                    if f >= 2:
                        pe.wait_ge(gelu_done, n - 1)
                    i = 0
                    for k in range(DH):
                        for v in (x2_h[g], x2_l[g]):
                            ins = mm(P23[:, f % 2, 0:TG], upT[:, k, f * 128:(f + 1) * 128], v[:, k, :], start=(i == 0),
                                     stop=(i == 2 * DH - 1))
                            i += 1
                    ins.then_inc(up_in_psum, 1)

            def gram(g):
                pe.wait_ge(g_rest, FC * (g + 1))
                pe.wait_ge(blend_done, last_group(g + 1) + 1)
                pe.wait_ge(ss_done, g)
                for t in range(NT):
                    o = P45[0:TT, t // 2, (t % 2) * 2 * TT:(t % 2 + 1) * 2 * TT].rearrange("p (a t) -> p a t", a=2)
                    for f in range(FC):
                        ins = mm(o, ghl[:, f, 0, t * TT:(t + 1) * TT], ghl[:, f, :, t * TT:(t + 1) * TT],
                                 start=(f == 0), stop=(f == FC - 1))
                ins.then_inc(gram_in_psum, 1)

            def ffn_down(g):
                pe.wait_ge(gelu_done, FC * (g + 1))
                for t in range(NT):
                    for f in range(FC):
                        for a in range(2):
                            ins = mm(tiles(P23)[:, t, :], ghl[:, f, a, t * TT:(t + 1) * TT], dnT[:, f, :],
                                     start=(f == 0 and a == 0), stop=(f == FC - 1 and a == 1))
                    if t % 2 == 1:
                        ins.then_inc(down_in_psum, 1)

            ahead = {0: (), 1: (2,), 2: (3, 4), 3: (5, 6)}
            x_transposes(0, 0)
            x_transposes(0, 1)
            for g in range(G):
                for j in range(KC):
                    n = g * KC + j
                    for k in ahead.get(n, (n + AHEAD,)):
                        if k < KC * G:
                            x_transposes(k // KC, k % KC)
                    embed(g, j)
                    if g == 0 and j == 3:
                        vector_columns()
                    if j == 2 and g >= 2:
                        x1_to_F(g - 2)
                    if j == 4 and g >= 1:
                        h_to_T(g - 1)

            for i in range(G + 2):
                a, t, f = i, i - 1, i - 2
                if a == 0:
                    gate_hidden(0)
                    setup()
                    x1_to_F(G - 2)
                    pos_values(0)
                    h_to_T(G - 1)
                    key_phases(0)
                    kv_values(0)
                    blend_hidden(0)
                    token_logits(0)
                    x1_to_F(G - 1)
                    spread_gates(0)
                    continue
                if 0 <= f < G:
                    x2_to_F(f)
                if a < G:
                    blend_hidden(a)
                    gate_hidden(a)
                    token_logits(a)
                    if a == 1:
                        ternary_to_F()
                    pos_values(a)
                    kv_values(a)
                    spread_gates(a)
                if 0 <= t < G:
                    returns_to_T(t)
                if a < G:
                    key_phases(a)
                if 0 <= f < G:
                    ffn_up(f, range(0, BEFORE_Z))
                if 0 <= t < G:
                    z_to_F(t)
                if 0 <= f < G:
                    ffn_up(f, range(BEFORE_Z, FC))
                if 0 <= t < G:
                    attention_out(t)
                if 0 <= f < G:
                    gram(f)
                    ffn_down(f)


_INS = ["x", "L0_tok_W", "L0_tok_b", "L0_attn_pos_phases", "L0_attn_Wpv", "L0_attn_bpv", "L0_attn_Wk", "L0_attn_bk",
        "L0_attn_Wkv", "L0_attn_bkv", "L0_attn_Wg1", "L0_attn_bg1", "L0_attn_Wg2", "L0_attn_bg2", "L0_attn_Wb1",
        "L0_attn_bb1", "L0_attn_Wb2", "L0_attn_bb2", "L0_attn_ln_g", "L0_attn_ln_b", "L0_attn_Wo", "L0_attn_bo",
        "L0_ffn_w_up", "L0_ffn_w_down"]
_OUTS = [((32, 49, 256), "float32")]


def kernel(**inputs):
    import numpy as _np
    import concourse.bacc as _bacc
    from concourse import mybir as _mybir
    from concourse.bass_utils import run_bass_kernel_spmd as _run

    nc = _bacc.Bacc("TRN2", target_bir_lowering=False, num_devices=1)
    arrays, args = {}, []
    for name in _INS:
        a = _np.ascontiguousarray(inputs[name])
        arrays[f"in_{name}_dram"] = a
        args.append(nc.dram_tensor(f"in_{name}_dram", a.shape, _mybir.dt.from_np(a.dtype), kind="ExternalInput").ap())
    for i, (shape, dtype) in enumerate(_OUTS):
        dt = _mybir.dt.from_np(_np.dtype(dtype))
        args.append(nc.dram_tensor(f"out_{i}_dram", shape, dt, kind="ExternalOutput").ap())
    vit_block_program(nc, *args)
    r = _run(nc, [arrays], core_ids=[0])
    return r.results[0]["out_0_dram"]
```

```python
from contextlib import ExitStack

import concourse.bass as bass
from concourse import mybir

ALU = mybir.AluOpType
ACT = mybir.ActivationFunctionType
F32 = mybir.dt.float32
F16 = mybir.dt.float16

PI = 3.14159265358979
WSCALE = 256.0
TWO_PI_PARTS = (6.28125, 0.0019350051879882812, 3.0199160514e-07)
ROUND_MAGIC = 12582912.0
PI_BELOW = 3.1415925
LN_EPS = 1e-5
RMS_EPS = 1e-8


def vit_block_program(nc, x, tok_W, tok_b, phases, Wpv, bpv, Wk, bk, Wkv, bkv, Wg1, bg1, Wg2, bg2,
                      Wb1, bb1, Wb2, bb2, ln_g, ln_b, Wo, bo, w_up, w_down, out):
    NIMG, C, HW, _ = x.shape
    PATCH = 16
    SIDE = HW // PATCH
    L = SIDE * SIDE
    D = tok_W.shape[0]
    DH = D // 128
    F = w_up.shape[0]
    FC = F // 128
    IPG = 8
    G = NIMG // IPG
    TG = IPG * L
    TT = 2 * L
    NT = TG // TT
    ROWS = IPG * SIDE
    PH = PATCH * PATCH // 128
    ODD = 64
    PIX = PATCH * HW
    KC = C * PH
    PADL = L + 1
    INV = 1.0 / WSCALE
    PV, KEY, KV, G1, BH, WO = 0, 2, 4, 6, 10, 11
    NSLOT = 13

    with ExitStack() as ctx:
        def sb(name, shape, dt=F32):
            return ctx.enter_context(nc.sbuf_tensor(name, shape, dt))

        def sem(name):
            return ctx.enter_context(nc.semaphore(name))

        bank = [ctx.enter_context(nc.psum_tensor(f"pair{i}", [128, 2, 512], F32)) for i in range(4)]
        P01, P23, P45, P67 = bank

        arena = sb("arena", [128, 2 * C * PIX])
        x_raw = [arena[:, c * PIX:(c + 1) * PIX] for c in range(C)]
        x_pat = [arena[:, (C + c) * PIX:(C + c + 1) * PIX] for c in range(C)]
        n = DH * TG
        u_pc, u_ps, u_kc, u_ks, m_pc, m_ps, m_kc, m_ks = [arena[:, i * n:(i + 1) * n] for i in range(8)]
        ghl = arena[:, 8 * n:8 * n + FC * TG].bitcast(F16).rearrange("p (f s t) -> p f s t", f=FC, s=2)

        tokw_f = sb("tokw_f", [128, KC * D])
        tokw_h = sb("tokw_h", [128, KC * D], F16)
        tokw_l = sb("tokw_l", [128, KC * D], F16)
        x_h = sb("x_h", [128, KC, TG], F16)
        x_l = sb("x_l", [128, KC, TG], F16)
        aw_f = sb("aw_f", [128, NSLOT * 256])
        out_ring = [aw_f[0:TT, i * NT * D:(i + 1) * NT * D] for i in range(2)]
        aw_h = sb("aw_h", [128, NSLOT * 256], F16)
        aw_l = sb("aw_l", [128, NSLOT * 256], F16)
        up_f = sb("up_f", [128, FC * D])
        dn_f = sb("dn_f", [128, DH * F])
        per = FC * D // TG
        hidden = [(up_f, dn_f)[f // per][:, f % per * TG:(f % per + 1) * TG] for f in range(FC)]
        below = sb("below", [128, FC * D], F16)
        up_t = sb("up_t", [128, FC * D], F16)
        dn_t = sb("dn_t", [128, DH * F], F16)
        upT = sb("upT", [128, DH, F], F16)
        dnT = sb("dnT", [128, FC, D], F16)
        hF = [sb(f"hF{i}", [128, DH, TG]) for i in range(2)]
        ring_T = [sb(f"ring_T{i}", [TT, NT * D]) for i in range(2)]
        x1_h = [sb(f"x1_h{g}", [128, DH, IPG, PADL], F16) for g in range(G)]
        x1_l = [sb(f"x1_l{g}", [128, DH, IPG, PADL], F16) for g in range(G)]
        flat = lambda a: a[:, :, :, :].rearrange("p h i l -> p (h i l)")[:, 0:DH * TG].rearrange("p (h t) -> p h t", h=DH)
        x2_h = [flat(x1_h[g]) for g in range(G)]
        x2_l = [flat(x1_l[g]) for g in range(G)]
        res = [sb(f"res{g}", [TT, NT * D]) for g in range(G)]
        x_h32, x_l32 = (a[:, :, :].rearrange("p k t -> p (k t)").bitcast(F32) for a in (x_h, x_l))
        gh = x_h32[:, 0:DH * TG].rearrange("p (h t) -> p h t", h=DH)
        bh = x_h32[:, DH * TG:(DH + 1) * TG]
        th = x_l32[:, 0:DH * TG].rearrange("p (h t) -> p h t", h=DH)
        gate = x_l32[:, DH * TG:(DH + 1) * TG]
        th_abs = sb("th_abs", [128, DH, TG])
        key_c = [sb(f"key_c{i}", [128, DH, IPG, PADL]) for i in range(2)]
        key_s = [sb(f"key_s{i}", [128, DH, IPG, PADL]) for i in range(2)]
        kvg = sb("kvg", [128, DH, TG])
        inside = sb("inside", [128, DH * TG])
        z_h = sb("z_h", [128, DH, TG], F16)
        z_l = sb("z_l", [128, DH, TG], F16)
        NV = 17
        vrows = sb("vrows", [NV, 128])
        vec = sb("vec", [128, NV])
        vec_s = sb("vec_s", [128, NV])
        srow = sb("srow", [1, 3])
        borow = sb("borow", [1, D])
        small = sb("small", [128, 4])
        wb2 = sb("wb2", [128, 2])
        gate_rows = sb("gate_rows", [TT, NT, 128])
        tri = sb("tri", [TT, TT])
        lnbb = sb("lnbb", [128, DH, TT])
        ident = sb("ident", [128, 128])
        ident16 = sb("ident16", [128, 128], F16)
        ones = sb("ones", [128, 128])
        gmask = sb("gmask", [TT, 2, TT])
        half_pi = sb("half_pi", [128, 1])
        p_minus_half = sb("p_minus_half", [TT, NT])
        p_half = sb("p_half", [TT, 2 * NT])
        kvg_flat, abs_flat = (a[:, :, :].rearrange("p h t -> p (h t)") for a in (kvg, th_abs))
        ph, ph_k, ph_abs = [kvg_flat[0:L, i * D:(i + 1) * D] for i in range(3)]
        ph_cs = abs_flat[0:L, 0:2 * D].rearrange("p (a d) -> p a d", a=2)
        table = sb("table", [128, 2, DH, L])
        bias_T = sb("bias_T", [TT, D])
        abs_sum = sb("abs_sum", [128, 2, 4])
        thr = sb("thr", [128, 4])
        thr_sum = sb("thr_sum", [128, 2])
        st = sb("st", [TT, NT, 6])
        mv = sb("mv", [TT, NT, 2])
        ve = sb("ve", [TT, NT])
        rstd = sb("rstd", [TT, NT])
        nmr = sb("nmr", [TT, NT])
        zst = sb("zst", [TT, NT, 6])
        zmv = sb("zmv", [TT, NT, 2])
        zve = sb("zve", [TT, NT])
        zrs = sb("zrs", [TT, NT])
        hst = sb("hst", [TT, NT, 6])
        hmv = sb("hmv", [TT, NT, 2])
        hvv = sb("hvv", [TT, 2, NT])
        hsq = sb("hsq", [TT, 2, NT])
        hf = sb("hf", [TT, NT])
        logit = sb("logit", [TT, NT, 3])
        logit_max = sb("logit_max", [TT, NT, 1])
        expo = sb("expo", [TT, NT, 3])
        denom = sb("denom", [TT, 2, NT])
        recip = sb("recip", [TT, 2, NT])
        bw = [sb(f"bw{i}", [TT, 2, NT]) for i in range(2)]
        gc = sb("gc", [TT, NT])
        gcr = [sb(f"gcr{i}", [TT, NT]) for i in range(2)]
        kvw = sb("kvw", [TT, NT])
        junk = sb("junk", [TT, 2 * TT])
        ss = sb("ss", [TT, NT])
        sr = sb("sr", [TT, NT])
        sf = sb("sf", [TT, NT])

        x_loaded = [sem(f"x_loaded{c}") for c in range(C)]
        x_sorted = sem("x_sorted")
        tokw_loaded = sem("tokw_loaded")
        tokwT_in_psum = sem("tokwT_in_psum")
        vec_loaded = sem("vec_loaded")
        aw_loaded = sem("aw_loaded")
        ph_loaded = sem("ph_loaded")
        up_loaded = sem("up_loaded")
        dn_loaded = sem("dn_loaded")
        out_stored = [sem(f"out_stored{i}") for i in range(2)]
        ident_done = sem("ident_done")
        consts_done = sem("consts_done")
        pool_step = sem("pool_step")
        dve_step = sem("dve_step")
        act_step = sem("act_step")
        vec_in_psum = sem("vec_in_psum")
        vec_done = sem("vec_done")
        tokw_head = sem("tokw_head")
        tokw_done = sem("tokw_done")
        ph_reduced = sem("ph_reduced")
        ph_cs_done = sem("ph_cs_done")
        abs_sum_done = sem("abs_sum_done")
        setup_in_psum = sem("setup_in_psum")
        setup_done = sem("setup_done")
        aw_head = sem("aw_head")
        aw_done = sem("aw_done")
        below_done = sem("below_done")
        tern_done = sem("tern_done")
        ternT_in_psum = sem("ternT_in_psum")
        ternT_done = sem("ternT_done")
        xT_in_psum = sem("xT_in_psum")
        x_head = sem("x_head")
        x_rest = sem("x_rest")
        tok_chunk = sem("tok_chunk")
        hF_done = sem("hF_done")
        hT_in_psum = sem("hT_in_psum")
        ve_done = sem("ve_done")
        rstd_done = sem("rstd_done")
        nmr_done = sem("nmr_done")
        x1T_done = sem("x1T_done")
        res_done = sem("res_done")
        res_biased = sem("res_biased")
        x1F_in_psum = sem("x1F_in_psum")
        x1_head = sem("x1_head")
        x1_rest = sem("x1_rest")
        g1_in_psum = sem("g1_in_psum")
        bh_in_psum = sem("bh_in_psum")
        key_in_psum = sem("key_in_psum")
        pv_in_psum = sem("pv_in_psum")
        logits_in_psum = sem("logits_in_psum")
        gate_in_psum = sem("gate_in_psum")
        kv_in_psum = sem("kv_in_psum")
        gh_done = sem("gh_done")
        bh_done = sem("bh_done")
        th_done = sem("th_done")
        th_abs_done = sem("th_abs_done")
        logit_done = sem("logit_done")
        expo_done = sem("expo_done")
        key_cs_done = sem("key_cs_done")
        bw_done = sem("bw_done")
        gate_rows_done = sem("gate_rows_done")
        u_pos_done = sem("u_pos_done")
        gate_done = sem("gate_done")
        kvg_done = sem("kvg_done")
        u_kv_done = sem("u_kv_done")
        m_pos_done = sem("m_pos_done")
        m_kv_done = sem("m_kv_done")
        pos_ret_done = sem("pos_ret_done")
        kv_multiplied = sem("kv_multiplied")
        kv_ret_done = sem("kv_ret_done")
        gc_done = sem("gc_done")
        gcr_done = sem("gcr_done")
        posT_in_psum = sem("posT_in_psum")
        kvT_in_psum = sem("kvT_in_psum")
        pos_scaled = sem("pos_scaled")
        blend_done = sem("blend_done")
        zve_done = sem("zve_done")
        zrs_done = sem("zrs_done")
        zT_done = sem("zT_done")
        zF_in_psum = sem("zF_in_psum")
        z_head = sem("z_head")
        z_rest = sem("z_rest")
        wo_in_psum = sem("wo_in_psum")
        h2_done = sem("h2_done")
        hvv_done = sem("hvv_done")
        hsq_done = sem("hsq_done")
        x2T_done = sem("x2T_done")
        x2F_in_psum = sem("x2F_in_psum")
        x2_head = sem("x2_head")
        x2_rest = sem("x2_rest")
        up_in_psum = sem("up_in_psum")
        gelu_done = sem("gelu_done")
        g_head = sem("g_head")
        g_rest = sem("g_rest")
        gram_in_psum = sem("gram_in_psum")
        ss_done = sem("ss_done")
        sr_done = sem("sr_done")
        down_in_psum = sem("down_in_psum")
        out_done = sem("out_done")


        def last_group(g):
            return min(g, G - 1)

        def images(ap):
            return ap.rearrange("p (i l) -> p i l", i=IPG)

        def halves(ap):
            return ap.rearrange("p (h i l) -> p h i l", h=DH, i=IPG)

        def slot(w, s, k=0, width=256):
            return w[:, (s + k) * 256:(s + k) * 256 + width]

        def tiles(pair):
            return pair[0:TT, :, :].rearrange("p b (t d) -> p (b t) d", d=D)

        def flat_T(pair):
            return pair[0:TT, :, :].rearrange("p b n -> p (b n)")

        AW_ORDER = [G1, G1 + 1, G1 + 2, G1 + 3, KEY, KEY + 1, PV, PV + 1, KV, KV + 1, BH, WO, WO + 1]

        AHEAD = 3

        def x_bank(n):
            return (P01, P67)[n % 4 // 2][:, n % 2, :]

        def tokw_bank(c):
            return P23[:, c, :] if c < 2 else P45[:, 0, :]

        def pos_in(g):
            return P23 if g < G - 1 else P01

        def up_banks(g):
            return (P23,) if g < G - 1 else (P01, P67)

        def up_bank(g, f):
            pairs = up_banks(g)
            return pairs[f // 2 % len(pairs)][:, f % 2, 0:TG]

        def split(i):
            return 4 if i + 1 < G else 5 if i < G else 2

        def g1_in(g):
            return P23 if g == 1 else P01

        def gates_in(g):
            return P67 if g == 0 else P45

        block = ctx.enter_context(nc.Block())

        @block.sync
        def _(sp):
            def load_x(half, c):
                if half == 0:
                    sp.dma_start(x_raw[c][ROWS:ODD, :],
                                 x[0:ODD - ROWS, c, 0:PATCH, :].rearrange("n p w -> n (p w)")).then_inc(x_loaded[c], 16)
                else:
                    sp.wait_ge(x_sorted, c + 1)
                for b in range(2):
                    g = 2 * half + b
                    src = x[g * IPG:(g + 1) * IPG, c, :, :].rearrange("n (h p) w -> n h (p w)", p=PATCH)
                    sp.dma_start(x_raw[c][b * ODD:b * ODD + ROWS, :], src).then_inc(x_loaded[c], 16)

            sp.dma_start(tokw_f[:, :].rearrange("p (m d) -> p m d", m=DH),
                         tok_W.rearrange("(m p) d -> p m d", p=128)).then_inc(tokw_loaded, 16)
            for c in range(C):
                load_x(0, c)
            for v, row in ((tok_b, 0), (bpv, 2), (bk, 4), (bkv, 6), (bg1, 8), (bb1, 10), (ln_g, 11), (ln_b, 13)):
                n = v.shape[0] // 128
                sp.dma_start(vrows[row:row + n, :], v.rearrange("(m p) -> m p", p=128)).then_inc(vec_loaded, 16)
            sp.dma_start(vrows[15:17, :], Wg2.rearrange("(m p) o -> m (p o)", p=128)).then_inc(vec_loaded, 16)
            sp.dma_start(srow[:, 0:2], bb2.rearrange("(a n) -> a n", a=1)).then_inc(vec_loaded, 16)
            sp.dma_start(srow[:, 2:3], bg2.rearrange("(a n) -> a n", a=1)).then_inc(vec_loaded, 16)
            sp.dma_start(borow[:, :], bo.rearrange("(a n) -> a n", a=1)).then_inc(vec_loaded, 16)
            sp.dma_start(wb2[:, :], Wb2).then_inc(vec_loaded, 16)
            sp.dma_start(ph[:, :], phases[0:L, :]).then_inc(ph_loaded, 16)
            load_x(1, 0)
            for w, s, k in ((Wg1, G1, 4), (Wk, KEY, 2), (Wpv, PV, 2), (Wkv, KV, 2), (Wo, WO, 2)):
                sp.dma_start(aw_f[:, s * 256:(s + k) * 256].rearrange("p (k m) -> p k m", k=k),
                             w.rearrange("(k p) m -> p k m", p=128)).then_inc(aw_loaded, 16)
            sp.dma_start(slot(aw_f, BH).rearrange("p (k m) -> p k m", k=2),
                         Wb1.rearrange("(k p) m -> p k m", p=128)).then_inc(aw_loaded, 16)
            load_x(1, 1)
            load_x(1, 2)
            sp.dma_start(up_f[:, :].rearrange("p (f d) -> p f d", f=FC),
                         w_up.rearrange("(f p) d -> p f d", p=128)).then_inc(up_loaded, 16)
            sp.dma_start(dn_f[:, :].rearrange("p (h f) -> p h f", h=DH),
                         w_down.rearrange("(h p) f -> p h f", p=128)).then_inc(dn_loaded, 16)
            out_v = out.rearrange("(g i) l d -> g (i l) d", g=G)
            for g in range(G):
                for k in range(2):
                    sp.wait_ge(out_done, 2 * g + k + 1)
                    sp.dma_start(out_v[g][2 * k * TT:2 * (k + 1) * TT, :].rearrange("(t p) d -> p t d", p=TT),
                                 out_ring[g % 2][:, 2 * k * D:2 * (k + 1) * D].rearrange("p (t d) -> p t d", t=2)
                                 ).then_inc(out_stored[g % 2], 16)
            for i in range(2):
                sp.wait_ge(out_stored[i], 32 * G // 2)

        N_VEC = 13
        N_AW = 6

        @block.gpsimd
        def _(pool):
            steps = [0]

            def chained(ins):
                steps[0] += 1
                ins.then_inc(pool_step, 1)
                pool.wait_ge(pool_step, steps[0])

            chained(nc.gpsimd.memset(ident[:, :], 0.0))
            nc.gpsimd.affine_select(out=ident[:, :], in_=ident[:, :], compare_op=ALU.not_equal, fill=1.0,
                                    base=0, pattern=[[-1, 128]], channel_multiplier=1).then_inc(ident_done, 1)
            pool.wait_ge(ident_done, 1)
            nc.gpsimd.tensor_copy(ident16[:, :], ident[:, :]).then_inc(consts_done, 1)
            nc.gpsimd.tensor_copy(gmask[:, 0, :], ident[0:TT, 0:TT]).then_inc(consts_done, 1)
            nc.gpsimd.tensor_scalar(gmask[:, 1, :], ident[0:TT, 0:TT], 2.0, None, ALU.mult).then_inc(consts_done, 1)
            chained(nc.gpsimd.memset(tri[:, :], 1.0))
            chained(nc.gpsimd.affine_select(out=tri[:, :], in_=tri[:, :], compare_op=ALU.is_ge, fill=0.0, base=0,
                                            pattern=[[1, TT]], channel_multiplier=-1))
            nc.gpsimd.affine_select(out=tri[:, L:TT], in_=tri[:, L:TT], compare_op=ALU.is_ge, fill=0.0, base=-L,
                                    pattern=[[0, L]], channel_multiplier=1).then_inc(consts_done, 1)

            def weight_rests(order):
                for s in order:
                    pool.wait_ge(aw_head, AW_ORDER.index(s) + 1)
                    nc.gpsimd.tensor_tensor(slot(aw_l, s), slot(aw_f, s), slot(aw_h, s), ALU.subtract).then_inc(aw_done, 1)

            def pow_rstd(g):
                pool.wait_ge(ve_done, g + 1)
                nc.gpsimd.tensor_tensor(rstd[:, :], ve[:, :], p_minus_half[:, :], ALU.pow).then_inc(rstd_done, 1)

            def bias_res(g):
                pool.wait_ge(res_done, g + 1)
                pool.wait_ge(setup_done, 1)
                r = res[g][:, :].rearrange("p (t d) -> p t d", t=NT)
                nc.gpsimd.tensor_tensor(r, r, bias_T[:, :].unsqueeze(1).broadcast_to([TT, NT, D]),
                                        ALU.add).then_inc(res_biased, 1)

            pow_rstd(0)
            weight_rests(AW_ORDER[0:4])
            pow_rstd(1)
            weight_rests(AW_ORDER[4:8])
            pow_rstd(2)
            weight_rests(AW_ORDER[8:11])
            pow_rstd(3)

            def shifted_key_terms(g):
                b = g % 2
                pool.wait_ge(kvg_done, g + 1)
                pool.wait_ge(key_cs_done, g + 1)
                pool.wait_ge(m_kv_done, 2 * g)
                for u, key in ((u_kc, key_c), (u_ks, key_s)):
                    nc.gpsimd.tensor_tensor(halves(u), kvg[:, :, :].rearrange("p h (i l) -> p h i l", i=IPG),
                                            key[b][:, :, :, 0:L], ALU.mult).then_inc(u_kv_done, 1)

            def pow_z(g):
                pool.wait_ge(zve_done, g + 1)
                nc.gpsimd.tensor_tensor(zrs[:, :], zve[:, :], p_minus_half[:, :], ALU.pow).then_inc(zrs_done, 1)

            def pos_ret(g):
                for i, m in enumerate((m_pc, m_ps)):
                    pool.wait_ge(m_pos_done, 2 * g + i + 1)
                    tab = table[:, i, :, :].unsqueeze(2).broadcast_to([128, DH, IPG, L])
                    chained(nc.gpsimd.tensor_tensor(halves(m), halves(m), tab, ALU.mult))
                nc.gpsimd.tensor_tensor(m_pc, m_pc, m_ps, ALU.add).then_inc(pos_ret_done, 1)

            def kv_products(g):
                for i, (m, key) in enumerate(((m_kc, key_c), (m_ks, key_s))):
                    pool.wait_ge(m_kv_done, 2 * g + i + 1)
                    nc.gpsimd.tensor_tensor(halves(m), halves(m), key[g % 2][:, :, :, 1:PADL], ALU.mult
                                            ).then_inc(kv_multiplied, 1)

            def kv_ret(g):
                pool.wait_ge(kv_multiplied, 2 * g + 2)
                nc.gpsimd.tensor_tensor(m_kc, m_kc, m_ks, ALU.add).then_inc(kv_ret_done, 1)

            def pow_gc(g):
                pool.wait_ge(gc_done, g + 1)
                nc.gpsimd.tensor_tensor(gcr[g % 2][:, :], gc[:, :], p_minus_half[:, :], ALU.pow).then_inc(gcr_done, 1)

            def pow_h2(g):
                pool.wait_ge(hvv_done, g + 1)
                two = "p a t -> p (a t)"
                nc.gpsimd.tensor_tensor(hsq[:, :, :].rearrange(two), hvv[:, :, :].rearrange(two), p_half[:, :],
                                        ALU.pow).then_inc(hsq_done, 1)

            def pow_ss(g):
                pool.wait_ge(ss_done, g + 1)
                nc.gpsimd.tensor_tensor(sr[:, :], ss[:, :], p_half[:, 0:NT], ALU.pow).then_inc(sr_done, 1)

            for i in range(G + 2):
                a, t, f = i, i - 1, i - 2
                if a < G:
                    if a == 0:
                        pos_ret(0)
                    pow_gc(a)
                if 0 <= t < G:
                    pow_z(t)
                if 0 < a < G - 1:
                    pos_ret(a)
                if a < G:
                    shifted_key_terms(a)
                if a == G - 1:
                    pos_ret(a)
                if a == G - 1:
                    kv_products(a)
                if 0 <= t < G:
                    pow_h2(t)
                if a == G - 1:
                    kv_ret(a)
                if 0 <= f < G:
                    pow_ss(f)
                if a < G - 1:
                    kv_products(a)
                    kv_ret(a)
                if a < G:
                    if a == 0:
                        weight_rests(AW_ORDER[11:])
                    bias_res(a)

        @block.scalar
        def _(act):
            for c in range(C):
                act.wait_ge(tokwT_in_psum, c + 1)
                s = slice(c * PH * D, (c + 1) * PH * D)
                nc.scalar.activation(tokw_h[:, s], tokw_bank(c), ACT.Copy, scale=WSCALE).then_inc(tokw_head, 1)

            def x_heads(g, j):
                n = g * KC + j
                act.wait_ge(xT_in_psum, n + 1)
                if n >= KC:
                    act.wait_ge(tok_chunk, n - KC + 1)
                nc.scalar.activation(x_h[:, j, :].rearrange("p (r w) -> p w r", w=SIDE),
                                     x_bank(n)[:, 0:TG].rearrange("p (w r) -> p w r", w=SIDE),
                                     ACT.Copy).then_inc(x_head, 1)

            def h_bias(g):
                act.wait_ge(tok_chunk, KC * (g + 1))
                act.wait_ge(vec_done, 1)
                if g >= 2:
                    act.wait_ge(hT_in_psum, g - 1)
                for m in range(DH):
                    ins = nc.scalar.activation(hF[g % 2][:, m, :], P23[:, m, 0:TG], ACT.Identity,
                                               bias=vec[:, m:m + 1], scale=INV)
                ins.then_inc(hF_done, 1)

            def normalise_h(g):
                act.wait_ge(nmr_done, g + 1)
                if g >= 2:
                    act.wait_ge(x1F_in_psum, g - 1)
                    act.wait_ge(res_done, g - 1)
                for t in range(NT):
                    ins = nc.scalar.activation(ring_T[g % 2][:, t * D:(t + 1) * D], tiles(P45)[:, t, :], ACT.Identity,
                                               bias=nmr[:, t:t + 1], scale=rstd[:, t:t + 1])
                ins.then_inc(x1T_done, 1)

            def x1_heads(g):
                act.wait_ge(x1F_in_psum, g + 1)
                nc.scalar.activation(x1_h[g][:, :, :, 1:PADL], P45[:, :, 0:TG].rearrange("p h (i l) -> p h i l", i=IPG),
                                     ACT.Copy).then_inc(x1_head, 1)

            def phase_tables():
                act.wait_ge(ph_reduced, 2)
                nc.scalar.activation(ph_cs[:, 1, :], ph[:, :], ACT.Sin)
                act.wait_ge(consts_done, 5)
                nc.scalar.activation(ph_cs[:, 0, :], ph_abs[:, :], ACT.Sin, bias=half_pi[0:L, :],
                                     scale=-1.0).then_inc(ph_cs_done, 1)

            def weight_sums(n, quarters):
                w, junk_w = ((up_f, up_t), (dn_f, dn_t))[n]
                act.wait_ge((up_loaded, dn_loaded)[n], 16)
                q = FC * D // 4
                for k in quarters:
                    nc.scalar.activation(junk_w[:, k * q:(k + 1) * q], w[:, k * q:(k + 1) * q], ACT.Abs,
                                         accum_out=abs_sum[:, n, k:k + 1]).then_inc(abs_sum_done, 1)

            def weight_heads(order):
                act.wait_ge(aw_loaded, 16 * N_AW)
                for s in order:
                    if s < WO:
                        nc.scalar.activation(slot(aw_f, s), slot(aw_f, s), ACT.Copy, scale=WSCALE).then_inc(act_step, 1)
                    else:
                        act.wait_ge(setup_in_psum, 1)
                        nc.scalar.activation(slot(aw_f, s), slot(aw_f, s), ACT.Copy,
                                             scale=vec_s[:, 11 + s - WO:12 + s - WO]).then_inc(act_step, 1)
                for s in order:
                    act.wait_ge(act_step, AW_ORDER.index(s) + 1)
                    nc.scalar.activation(slot(aw_h, s), slot(aw_f, s), ACT.Copy).then_inc(aw_head, 1)

            weights_at = {(1, 3): (0, 1), (1, 5): (1, 2), (2, 0): (2, 3), (2, 1): (3, 4), (2, 3): (4, 5), (2, 4): (5, 6),
                          (2, 5): (6, 7), (3, 0): (7, 8), (3, 1): (8, 10), (3, 4): (10, 11)}
            sums_at = {(3, 3): (0, range(0, 1)), (3, 4): (0, range(1, 2)), (4, 0): (0, range(2, 4)),
                       (4, 1): (1, range(0, 4))}
            for g in range(G + 1):
                for j in range(KC):
                    if g < G:
                        x_heads(g, j)
                    if j == 0 and g >= 3:
                        x1_heads(g - 3)
                    if j == 2 and g >= 1:
                        h_bias(g - 1)
                    if j == 3 and g >= 2:
                        normalise_h(g - 2)
                    if g == 1 and j == 4:
                        phase_tables()
                    if (g, j) in weights_at:
                        first, end = weights_at[(g, j)]
                        weight_heads(AW_ORDER[first:end])
                    if (g, j) in sums_at:
                        weight_sums(*sums_at[(g, j)])

            def gelu_g1(g):
                for m in range(DH):
                    act.wait_ge(g1_in_psum, DH * g + m + 1)
                    if m == 0:
                        act.wait_ge(logits_in_psum, g)
                    ins = nc.scalar.activation(gh[:, m, :], g1_in(g)[:, m, 0:TG], ACT.Gelu, bias=vec[:, 8 + m:9 + m],
                                               scale=INV)
                ins.then_inc(gh_done, 1)

            def gelu_bh(g):
                act.wait_ge(bh_in_psum, g + 1)
                act.wait_ge(logits_in_psum, g)
                nc.scalar.activation(bh[:, :], gates_in(g)[:, 0, 0:TG], ACT.Gelu, bias=vec[:, 10:11], scale=INV).then_inc(bh_done, 1)

            def tanh_key(g):
                for m in range(DH):
                    act.wait_ge(key_in_psum, DH * g + m + 1)
                    if m == 0:
                        act.wait_ge(key_cs_done, g)
                    ins = nc.scalar.activation(th[:, m, :], P23[:, m, 0:TG], ACT.Tanh, bias=vec[:, 4 + m:5 + m],
                                               scale=INV)
                ins.then_inc(th_done, 1)

            def exps(g):
                act.wait_ge(logit_done, g + 1)
                act.wait_ge(gate_rows_done, g)
                nc.scalar.activation(expo[:, :, :], logit[:, :, :], ACT.Exp).then_inc(expo_done, 1)

            def copy_gate(g):
                act.wait_ge(gate_in_psum, g + 1)
                act.wait_ge(kvg_done, g)
                nc.scalar.activation(gate, gates_in(g)[:, 1, 0:TG], ACT.Copy).then_inc(gate_done, 1)

            def keys(g):
                b = g % 2
                if g >= 2:
                    act.wait_ge(kv_ret_done, g - 1)
                act.wait_ge(th_done, g + 1)
                nc.scalar.activation(th_abs[:, :, :], th[:, :, :], ACT.Abs).then_inc(th_abs_done, 1)
                nc.scalar.activation(key_s[b][:, :, :, 1:PADL], th[:, :, :].rearrange("p h (i l) -> p h i l", i=IPG),
                                     ACT.Sin, scale=PI_BELOW)
                act.wait_ge(th_abs_done, g + 1)
                nc.scalar.activation(key_c[b][:, :, :, 1:PADL], th_abs[:, :, :].rearrange("p h (i l) -> p h i l", i=IPG),
                                     ACT.Sin, bias=half_pi[:, :], scale=-PI).then_inc(key_cs_done, 1)

            def scale_pos(g):
                act.wait_ge(posT_in_psum, g + 1)
                act.wait_ge(bw_done, g + 1)
                if g >= 1:
                    act.wait_ge(zF_in_psum, g)
                else:
                    act.wait_ge(x1F_in_psum, G)
                    act.wait_ge(res_done, G)
                for t in range(NT):
                    ins = nc.scalar.activation(ring_T[0][:, t * D:(t + 1) * D], tiles(pos_in(g))[:, t, :], ACT.Copy,
                                               scale=bw[g % 2][:, 0, t:t + 1])
                ins.then_inc(pos_scaled, 1)

            def z_heads(g):
                act.wait_ge(zF_in_psum, g + 1)
                act.wait_ge(wo_in_psum, g)
                nc.scalar.activation(z_h[:, :, :], P67[:, :, 0:TG], ACT.Copy).then_inc(z_head, 1)

            def x2_heads(g):
                act.wait_ge(x2F_in_psum, g + 1)
                nc.scalar.activation(x2_h[g], P67[:, :, 0:TG], ACT.Copy).then_inc(x2_head, 1)

            def ffn_gelus(g, chunks):
                for f in chunks:
                    n = FC * g + f
                    act.wait_ge(up_in_psum, n + 1)
                    if g >= 1:
                        act.wait_ge(g_rest, n - FC + 1)
                    elif f == 0:
                        act.wait_ge(tern_done, 2)
                    nc.scalar.activation(hidden[f], up_bank(g, f), ACT.Gelu).then_inc(gelu_done, 1)
                    if f % 2 == 0:
                        act.wait_ge(gelu_done, n + 1)
                        if f == 0:
                            act.wait_ge(down_in_psum, 2 * g)
                        nc.scalar.activation(ghl[:, f, 0, :], hidden[f], ACT.Copy).then_inc(g_head, 1)

            def ternary_copies(parts):
                for n in parts:
                    act.wait_ge(ternT_in_psum, n + 1)
                    dst = upT[:, n, :] if n < DH else \
                        dnT[:, (n - DH) * 4:(n - DH) * 4 + 4, :].rearrange("p f d -> p (f d)")
                    nc.scalar.activation(dst, P67[:, n % 2, :].bitcast(F16), ACT.Copy).then_inc(ternT_done, 1)

            for i in range(G + 2):
                a, t, f = i, i - 1, i - 2
                if a == 0:
                    gelu_g1(0)
                    x1_heads(G - 2)
                    tanh_key(0)
                    gelu_bh(0)
                    normalise_h(G - 1)
                    exps(0)
                    keys(0)
                    x1_heads(G - 1)
                    copy_gate(0)
                    gelu_g1(1)
                    gelu_bh(1)
                    exps(1)
                    weight_heads(AW_ORDER[11:])
                if i == 2:
                    copy_gate(2)
                    scale_pos(1)
                    tanh_key(2)
                    x2_heads(0)
                else:
                    if i == 3:
                        copy_gate(3)
                    if 0 <= f < G:
                        x2_heads(f)
                    if 0 <= t < G - 1:
                        scale_pos(t)
                    if i == 1:
                        copy_gate(1)
                    if 0 < a < G:
                        tanh_key(a)
                if i == 1:
                    ternary_copies(range(0, 2))
                if 0 < i < 3:
                    gelu_g1(a + 1)
                if a == G - 1:
                    keys(a)
                if 0 <= f < G:
                    ffn_gelus(f, range(0, min(4, split(i))))
                if 0 <= f < G:
                    ffn_gelus(f, range(min(4, split(i)), split(i)))
                if 0 <= t < G:
                    z_heads(t)
                if 0 < i < 3:
                    gelu_bh(a + 1)
                if 0 <= f < G:
                    ffn_gelus(f, range(split(i), FC))
                if 0 < i < 3:
                    keys(a)
                    exps(a + 1)
                if i == 1:
                    ternary_copies(range(2, 4))
                if a == G - 1:
                    scale_pos(a)

        @block.vector
        def _(dve):
            steps = [0]

            def chained(ins):
                steps[0] += 1
                ins.then_inc(dve_step, 1)
                dve.wait_ge(dve_step, steps[0])

            nc.vector.memset(half_pi[:, :], PI / 2).then_inc(consts_done, 1)
            chained(nc.vector.memset(ones[:, :], 1.0))
            nc.vector.memset(p_minus_half[:, :], -0.5)
            nc.vector.memset(p_half[:, :], 0.5)
            chained(nc.vector.memset(inside[:, :], 1.0))
            nc.vector.memset(inside[:, :].rearrange("p (n l) -> p n l", l=L)[:, :, 0:1], 0.0)
            for a in [*x1_h, *x1_l, *key_c, *key_s]:
                ins = nc.vector.memset(a[:, :, :, 0:1], 0.0)
            chained(ins)

            def vectors():
                dve.wait_ge(vec_in_psum, 1)
                chained(nc.vector.tensor_copy(vec[:, :], P45[:, 1, 0:NV]))
                nc.vector.tensor_copy(small[:, 0:3], P45[:, 1, 32:35])
                nc.vector.tensor_scalar(vec_s[:, :], vec[:, :], WSCALE, None, ALU.mult)
                for k in range(DH):
                    ins = nc.vector.tensor_scalar(lnbb[:, k, :], ones[:, 0:TT], vec[:, 13 + k:14 + k], None, ALU.mult)
                ins.then_inc(vec_done, 1)

            def reduce_phases():
                dve.wait_ge(ph_loaded, 16)
                chained(nc.vector.tensor_scalar(ph_k[:, :], ph[:, :], 0.5 / PI, ROUND_MAGIC, ALU.mult, ALU.add))
                chained(nc.vector.tensor_scalar(ph_k[:, :], ph_k[:, :], ROUND_MAGIC, None, ALU.subtract))
                for part in TWO_PI_PARTS:
                    chained(nc.vector.scalar_tensor_tensor(out=ph[:, :], in0=ph_k[:, :], scalar=-part, in1=ph[:, :],
                                                           op0=ALU.mult, op1=ALU.add))
                nc.vector.tensor_scalar(ph[:, :], ph[:, :], PI_BELOW, -PI_BELOW, ALU.min, ALU.max).then_inc(ph_reduced, 1)
                dve.wait_ge(ph_reduced, 1)
                nc.vector.scalar_tensor_tensor(out=ph_abs, in0=ph, scalar=-1.0, in1=ph, op0=ALU.mult,
                                               op1=ALU.max).then_inc(ph_reduced, 1)

            def sort_pixels(half, c):
                dve.wait_ge(x_loaded[c], 48 + 32 * half)
                if half > 0:
                    dve.wait_ge(xT_in_psum, KC + (c + 1) * PH)
                n = ODD + ROWS
                nc.vector.tensor_copy(x_pat[c][0:n, :].rearrange("r (w p q) -> r p w q", w=SIDE, p=PATCH),
                                      x_raw[c][0:n, :].rearrange("r (p w q) -> r p w q", w=SIDE, p=PATCH)
                                      ).then_inc(x_sorted, 1)

            def x_rests(g, j):
                n = g * KC + j
                dve.wait_ge(x_head, n + 1)
                nc.vector.tensor_tensor(x_l[:, j, :].rearrange("p (r w) -> p w r", w=SIDE),
                                        x_bank(n)[:, 0:TG].rearrange("p (w r) -> p w r", w=SIDE),
                                        x_h[:, j, :].rearrange("p (r w) -> p w r", w=SIDE),
                                        ALU.subtract).then_inc(x_rest, 1)

            def stats(src, st_, mv_):
                for t in range(NT):
                    ins = nc.vector.bn_stats(st_[:, t, :], src(t))
                chained(ins)
                for t in range(NT):
                    ins = nc.vector.bn_aggr(mv_[:, t, :], st_[:, t, :])
                chained(ins)

            def stats_h(g):
                dve.wait_ge(hT_in_psum, g + 1)
                dve.wait_ge(nmr_done, g)
                stats(lambda t: tiles(P45)[:, t, :], st, mv)
                nc.vector.tensor_scalar(ve[:, :], mv[:, :, 1], LN_EPS, None, ALU.add).then_inc(ve_done, 1)

            def mean_h(g):
                dve.wait_ge(rstd_done, g + 1)
                dve.wait_ge(x1T_done, g)
                nc.vector.scalar_tensor_tensor(out=nmr[:, :], in0=mv[:, :, 0], scalar=-1.0, in1=rstd[:, :],
                                               op0=ALU.mult, op1=ALU.mult).then_inc(nmr_done, 1)

            def residual(g):
                dve.wait_ge(x1T_done, g + 1)
                nc.vector.tensor_tensor(res[g][:, :], flat_T(P45), ring_T[g % 2][:, :], ALU.add).then_inc(res_done, 1)

            def x1_rests(g):
                dve.wait_ge(x1_head, g + 1)
                nc.vector.tensor_tensor(x1_l[g][:, :, :, 1:PADL], P45[:, :, 0:TG].rearrange("p h (i l) -> p h i l", i=IPG),
                                        x1_h[g][:, :, :, 1:PADL], ALU.subtract).then_inc(x1_rest, 1)

            def setup_copies():
                dve.wait_ge(setup_in_psum, 1)
                nc.vector.tensor_copy(table[:, :, :, :].rearrange("p a h l -> p (a h l)"), P67[:, 0, 0:2 * DH * L])
                nc.vector.tensor_copy(bias_T[:, :], P67[0:TT, 1, 0:D])
                chained(nc.vector.tensor_reduce(thr_sum[:, :], P67[:, 1, 256:264].rearrange("p (n k) -> p n k", k=4),
                                                mybir.AxisListType.X, ALU.add))
                nc.vector.tensor_scalar(thr[:, 0:2], thr_sum[:, :], 0.5 / (F * D), None, ALU.mult)
                nc.vector.tensor_scalar(thr[:, 2:4], thr_sum[:, :], -0.5 / (F * D), None, ALU.mult).then_inc(setup_done, 1)

            def ternary_below(w, n):
                dve.wait_ge(setup_done, 1)
                dve.wait_ge(tern_done, n)
                nc.vector.tensor_scalar(below[:, :], w[:, :], thr[:, 2 + n:3 + n], None, ALU.is_lt).then_inc(below_done, 1)

            def ternary(w, t, n):
                dve.wait_ge(below_done, n + 1)
                nc.vector.scalar_tensor_tensor(out=t[:, :], in0=w[:, :], scalar=thr[:, n:n + 1], in1=below[:, :],
                                               op0=ALU.is_gt, op1=ALU.subtract).then_inc(tern_done, 1)

            sort_pixels(0, 0)
            for c in range(C):
                dve.wait_ge(tokw_head, c + 1)
                s = slice(c * PH * D, (c + 1) * PH * D)
                nc.vector.scalar_tensor_tensor(out=tokw_l[:, s], in0=tokw_bank(c), scalar=WSCALE, in1=tokw_h[:, s],
                                               op0=ALU.mult, op1=ALU.subtract).then_inc(tokw_done, 1)
            for g in range(G + 1):
                for j in range(KC):
                    if g < G:
                        x_rests(g, j)
                    if g == 0 and j < C - 1:
                        sort_pixels(0, j + 1)
                    if g == 1 and j == 0:
                        vectors()
                    if g == 1 and j == 1:
                        reduce_phases()
                    if g == 1 and j % PH == PH - 1:
                        sort_pixels(1, j // PH)
                    if g >= 3 and j == 0:
                        x1_rests(g - 3)
                    if g >= 2 and j == 1:
                        stats_h(g - 2)
                    if g >= 2 and j == 2:
                        mean_h(g - 2)
                    if g >= 2 and j == 3:
                        residual(g - 2)
            setup_copies()
            x1_rests(G - 2)

            def pos_terms(g, i):
                u = (u_pc, u_ps)[i]
                if i == 0:
                    dve.wait_ge(pv_in_psum, g + 1)
                    dve.wait_ge(m_pos_done, 2 * g)
                for m in range(DH):
                    ins = nc.vector.scalar_tensor_tensor(
                        out=images(u[:, m * TG:(m + 1) * TG]), in0=images(P67[:, m, 0:TG]),
                        scalar=vec_s[:, 2 + m:3 + m], in1=table[:, i, m, :].unsqueeze(1).broadcast_to([128, IPG, L]),
                        op0=ALU.add, op1=ALU.mult)
                ins.then_inc(u_pos_done, 1)

            def logits(g):
                dve.wait_ge(logits_in_psum, g + 1)
                dve.wait_ge(expo_done, g)
                chained(nc.vector.tensor_tensor(logit[:, :, :],
                                                gates_in(g)[0:TT, 1, 0:3 * NT].rearrange("p (t c) -> p t c", c=3),
                                                small[0:TT, 0:3].unsqueeze(1).broadcast_to([TT, NT, 3]), ALU.add))
                nc.vector.tensor_scalar(logit[:, :, 2:3], logit[:, :, 2:3], -1.0, None, ALU.mult)
                chained(nc.vector.tensor_tensor(logit_max[:, :, :], logit[:, :, 0:1], logit[:, :, 1:2], ALU.max))
                nc.vector.tensor_tensor(logit[:, :, 0:2], logit[:, :, 0:2], logit_max[:, :, :].broadcast_to([TT, NT, 2]),
                                        ALU.subtract).then_inc(logit_done, 1)

            def weights(g):
                b = bw[g % 2]
                dve.wait_ge(expo_done, g + 1)
                dve.wait_ge(gate_rows_done, g)
                if g >= 1:
                    dve.wait_ge(gate_in_psum, g)
                if g >= 2:
                    dve.wait_ge(pos_scaled, g - 1)
                nc.vector.tensor_tensor(denom[:, 0, :], expo[:, :, 0], expo[:, :, 1], ALU.add)
                chained(nc.vector.tensor_scalar(denom[:, 1, :], expo[:, :, 2], 1.0, None, ALU.add))
                chained(nc.vector.reciprocal(recip[:, :, :], denom[:, :, :]))
                for t in range(NT):
                    nc.vector.tensor_scalar(gate_rows[:, t, :], ones[0:TT, :], recip[:, 1, t:t + 1], None, ALU.mult)
                for c in range(2):
                    ins = nc.vector.scalar_tensor_tensor(out=b[:, c, :], in0=expo[:, :, c], scalar=INV / D ** 0.5,
                                                         in1=recip[:, 0, :], op0=ALU.mult, op1=ALU.mult)
                    ins.then_inc((bw_done, gate_rows_done)[c], 1)

            def gated_values(g):
                dve.wait_ge(kv_in_psum, g + 1)
                dve.wait_ge(gate_done, g + 1)
                dve.wait_ge(u_kv_done, 2 * g)
                for m in range(DH):
                    ins = nc.vector.scalar_tensor_tensor(out=kvg[:, m, :], in0=P01[:, m, 0:TG],
                                                         scalar=vec_s[:, 6 + m:7 + m], in1=gate, op0=ALU.add,
                                                         op1=ALU.mult)
                ins.then_inc(kvg_done, 1)

            def gate_count(g):
                dve.wait_ge(gate_in_psum, g + 1)
                dve.wait_ge(gcr_done, g)
                nc.vector.tensor_scalar(gc[:, :], gates_in(g)[0:TT, 0, 0:NT], 1.0, None, ALU.max).then_inc(gc_done, 1)

            def scan(m, u, done):
                nc.vector.tensor_tensor_scan(m, inside[:, :], u, 0.0, ALU.mult, ALU.add).then_inc(done, 1)

            def scan_pos(g):
                dve.wait_ge(u_pos_done, 2 * g + 2)
                dve.wait_ge(posT_in_psum, g)
                scan(m_pc, u_pc, m_pos_done)
                scan(m_ps, u_ps, m_pos_done)

            def scan_kv(g):
                dve.wait_ge(u_kv_done, 2 * g + 1)
                dve.wait_ge(kvT_in_psum, g)
                scan(m_kc, u_kc, m_kv_done)
                dve.wait_ge(u_kv_done, 2 * g + 2)
                scan(m_ks, u_ks, m_kv_done)

            def kv_weight(g):
                dve.wait_ge(gcr_done, g + 1)
                dve.wait_ge(gate_rows_done, g + 1)
                dve.wait_ge(blend_done, g)
                chained(nc.vector.tensor_tensor(kvw[:, :], bw[g % 2][:, 1, :], gcr[g % 2][:, :], ALU.mult))

            def blend(g):
                kv_weight(g)
                dve.wait_ge(kvT_in_psum, g + 1)
                dve.wait_ge(pos_scaled, g + 1)
                for t in range(NT):
                    r = ring_T[0][:, t * D:(t + 1) * D]
                    ins = nc.vector.scalar_tensor_tensor(out=r, in0=tiles(P45)[:, t, :], scalar=kvw[:, t:t + 1], in1=r,
                                                         op0=ALU.mult, op1=ALU.add)
                ins.then_inc(blend_done, 1)
                dve.wait_ge(blend_done, g + 1)
                dve.wait_ge(zT_done, g)
                stats(lambda t: ring_T[0][:, t * D:(t + 1) * D], zst, zmv)
                nc.vector.tensor_scalar(zve[:, :], zmv[:, :, 1], LN_EPS, None, ALU.add).then_inc(zve_done, 1)

            def normalise(dst, src, mean, scale):
                for t in range(NT):
                    s = slice(t * D, (t + 1) * D)
                    ins = nc.vector.tensor_scalar(dst[:, s], src[:, s], mean[:, t, 0:1], scale[:, t:t + 1],
                                                  ALU.subtract, ALU.mult)
                return ins

            def normalise_z(g):
                dve.wait_ge(zrs_done, g + 1)
                normalise(ring_T[0], ring_T[0], zmv, zrs).then_inc(zT_done, 1)

            def z_rests(g):
                dve.wait_ge(z_head, g + 1)
                nc.vector.tensor_tensor(z_l[:, :, :], P67[:, :, 0:TG], z_h[:, :, :], ALU.subtract).then_inc(z_rest, 1)

            def second_residual(g):
                dve.wait_ge(wo_in_psum, g + 1)
                dve.wait_ge(res_biased, g + 1)
                dve.wait_ge(x2T_done, g)
                nc.vector.scalar_tensor_tensor(out=res[g][:, :], in0=flat_T(P01), scalar=INV, in1=res[g][:, :],
                                               op0=ALU.mult, op1=ALU.add).then_inc(h2_done, 1)
                dve.wait_ge(h2_done, g + 1)
                stats(lambda t: res[g][:, t * D:(t + 1) * D], hst, hmv)
                nc.vector.tensor_copy(hvv[:, 0, :], hmv[:, :, 1])
                nc.vector.tensor_scalar(hvv[:, 1, :], hmv[:, :, 1], LN_EPS, None, ALU.add).then_inc(hvv_done, 1)

            def normalise_h2(g):
                dve.wait_ge(hsq_done, g + 1)
                dve.wait_ge(x2F_in_psum, g)
                chained(nc.vector.scalar_tensor_tensor(out=hf[:, :], in0=hsq[:, 1, :], scalar=RMS_EPS, in1=hsq[:, 0, :],
                                                       op0=ALU.mult, op1=ALU.add))
                chained(nc.vector.reciprocal(hf[:, :], hf[:, :]))
                normalise(ring_T[1], res[g], hmv, hf).then_inc(x2T_done, 1)

            def x2_rests(g):
                dve.wait_ge(x2_head, g + 1)
                nc.vector.tensor_tensor(x2_l[g], P67[:, :, 0:TG], x2_h[g], ALU.subtract).then_inc(x2_rest, 1)

            def hidden_rests(g, chunks):
                for f in chunks:
                    n = FC * g + f
                    if f % 2 == 0:
                        dve.wait_ge(g_head, n // 2 + 1)
                    else:
                        dve.wait_ge(gelu_done, n + 1)
                        chained(nc.vector.tensor_copy(ghl[:, f, 0, :], hidden[f]))
                    nc.vector.tensor_tensor(ghl[:, f, 1, :], hidden[f], ghl[:, f, 0, :],
                                            ALU.subtract).then_inc(g_rest, 1)

            def square_sums(g):
                dve.wait_ge(gram_in_psum, g + 1)
                dve.wait_ge(sr_done, g)
                dve.wait_ge(ss_done, g)
                dve.wait_ge(consts_done, 5)
                for t in range(NT):
                    ins = nc.vector.tensor_tensor_reduce(
                        out=junk[:, :], in0=P45[0:TT, t // 2, (t % 2) * 2 * TT:(t % 2 + 1) * 2 * TT],
                        in1=gmask[:, :, :].rearrange("p a t -> p (a t)"), scale=1.0, scalar=0.0, op0=ALU.mult,
                        op1=ALU.add, accum_out=ss[:, t:t + 1])
                    if t < NT - 1:
                        chained(ins)
                ins.then_inc(ss_done, 1)

            def outputs(g):
                dve.wait_ge(sr_done, g + 1)
                dve.wait_ge(out_done, 2 * g)
                chained(nc.vector.tensor_scalar(sf[:, :], sr[:, :], F ** -0.5, RMS_EPS, ALU.mult, ALU.add))
                chained(nc.vector.reciprocal(sf[:, :], sf[:, :]))
                if g >= 2:
                    dve.wait_ge(out_stored[g % 2], 32 * (g // 2))
                for t in range(NT):
                    if t % 2 == 0:
                        dve.wait_ge(down_in_psum, 2 * g + t // 2 + 1)
                    ins = nc.vector.scalar_tensor_tensor(out=out_ring[g % 2][:, t * D:(t + 1) * D],
                                                         in0=tiles(P23)[:, t, :], scalar=sf[:, t:t + 1],
                                                         in1=res[g][:, t * D:(t + 1) * D], op0=ALU.mult, op1=ALU.add)
                    if t % 2 == 1:
                        ins.then_inc(out_done, 1)

            for i in range(G + 3):
                a, t, f, o = i, i - 1, i - 2, i - 3
                if 0 <= o < G and i <= G:
                    outputs(o)
                if a == 0:
                    pos_terms(0, 0)
                    pos_terms(0, 1)
                    stats_h(G - 1)
                    mean_h(G - 1)
                    scan_pos(0)
                if a == 0:
                    logits(0)
                    residual(G - 1)
                    weights(0)
                    x1_rests(G - 1)
                if 0 <= f < G and i != 2:
                    x2_rests(f)
                if i > G:
                    outputs(o)
                if a < G:
                    if a >= 2:
                        pos_terms(a, 0)
                        pos_terms(a, 1)
                    gate_count(a)
                    gated_values(a)
                if 0 <= t < G - 1:
                    blend(t)
                if i == 2:
                    x2_rests(0)
                if a == 0:
                    ternary_below(up_f, 0)
                    ternary(up_f, up_t, 0)
                    scan_kv(0)
                    logits(1)
                    pos_terms(1, 0)
                    weights(1)
                    pos_terms(1, 1)
                if i == G:
                    normalise_z(t)
                if i == 1:
                    ternary_below(dn_f, 1)
                if 0 <= t < G - 1:
                    normalise_z(t)
                if 0 <= f < G:
                    hidden_rests(f, range(0, 2))
                if 0 < a < G:
                    scan_pos(a)
                if 0 <= f < G:
                    hidden_rests(f, range(2, min(4, split(i))))
                if 0 <= t < G:
                    z_rests(t)
                if i == 1:
                    ternary(dn_f, dn_t, 1)
                if 0 <= f < G:
                    hidden_rests(f, range(min(4, split(i)), 6))
                if 0 < i < 3:
                    logits(a + 1)
                if 0 <= f < G:
                    hidden_rests(f, range(6, FC))
                if a == G - 1:
                    scan_kv(a)
                if i == 1:
                    weights(2)
                if 0 <= t < G:
                    second_residual(t)
                if 0 <= f < G:
                    square_sums(f)
                if i == 2:
                    weights(3)
                if 0 < i < 3:
                    scan_kv(a)
                if 0 <= t < G:
                    normalise_h2(t)
                if i == G - 1:
                    blend(i)

        @block.tensor
        def _(pe):
            mm = nc.tensor.matmul

            pe.wait_ge(ident_done, 1)
            pe.wait_ge(tokw_loaded, 16)
            w_in = tokw_f[:, :].rearrange("p (m h j c) -> p m c h j", m=DH, h=PH, c=C)
            for c in range(C):
                for h in range(PH):
                    for m in range(DH):
                        k = h * D + m * 128
                        ins = nc.tensor.transpose(tokw_bank(c)[:, k:k + 128], w_in[:, m, c, h, :], ident[:, :])
                ins.then_inc(tokwT_in_psum, 1)

            def vector_columns():
                pe.wait_ge(dve_step, 1)
                pe.wait_ge(vec_loaded, 16 * N_VEC)
                nc.tensor.transpose(P45[:, 1, 0:NV], vrows[:, :], ident[0:NV, 0:NV])
                mm(P45[:, 1, 32:35], ones[0:1, :], srow[:, :], start=True, stop=True).then_inc(vec_in_psum, 1)

            def x_transposes(g, j):
                n, c, h = g * KC + j, j // PH, j % PH
                if j % PH == 0:
                    pe.wait_ge(x_sorted, C * (g // 2) + c + 1)
                if n >= 4:
                    pe.wait_ge(x_rest, n - 3)
                lo = (g % 2) * ODD
                for w in range(SIDE):
                    ins = nc.tensor.transpose(x_bank(n)[:, w * ROWS:(w + 1) * ROWS],
                                              x_pat[c][lo:lo + ROWS, (w * PH + h) * 128:(w * PH + h + 1) * 128],
                                              ident[lo:lo + ROWS, lo:lo + ROWS])
                ins.then_inc(xT_in_psum, 1)

            def embed(g, j):
                n = g * KC + j
                pe.wait_ge(x_rest, n + 1)
                if g == 0:
                    pe.wait_ge(tokw_done, C)
                if j == 0 and g >= 1:
                    pe.wait_ge(hF_done, g)
                for m in range(DH):
                    for i, (w, v) in enumerate(((tokw_h, x_h), (tokw_h, x_l), (tokw_l, x_h))):
                        ins = mm(P23[:, m, 0:TG], w[:, j * D + m * 128:j * D + (m + 1) * 128], v[:, j, :],
                                 start=(j == 0 and i == 0), stop=(j == KC - 1 and i == 2))
                ins.then_inc(tok_chunk, 1)

            def to_T(src, dst):
                for t in range(NT):
                    for m in range(DH):
                        ins = nc.tensor.transpose(tiles(dst)[:, t, m * 128:(m + 1) * 128], src(m, t), ident[:, :])
                return ins

            def to_F(src, dst):
                for m in range(DH):
                    for t in range(NT):
                        ins = nc.tensor.transpose(dst[:, m, t * TT:(t + 1) * TT],
                                                  src[:, t * D + m * 128:t * D + (m + 1) * 128], ident[0:TT, 0:TT])
                return ins

            def h_to_T(g):
                pe.wait_ge(hF_done, g + 1)
                pe.wait_ge(x1_rest, g)
                if g == 0:
                    pe.wait_ge(tokw_done, C)
                    pe.wait_ge(vec_done, 1)
                to_T(lambda m, t: hF[g % 2][:, m, t * TT:(t + 1) * TT], P45).then_inc(hT_in_psum, 1)

            def x1_to_F(g):
                pe.wait_ge(x1T_done, g + 1)
                pe.wait_ge(res_done, g + 1)
                to_F(ring_T[g % 2], P45).then_inc(x1F_in_psum, 1)

            def setup():
                pe.wait_ge(x_rest, KC * G)
                pe.wait_ge(ph_cs_done, 1)
                for a in range(2):
                    for m in range(DH):
                        k = (a * DH + m) * L
                        nc.tensor.transpose(P67[:, 0, k:k + L], ph_cs[:, a, m * 128:(m + 1) * 128], ident[0:L, 0:L])
                pe.wait_ge(vec_done, 1)
                pe.wait_ge(aw_loaded, 16 * N_AW)
                for k in range(DH):
                    mm(P67[0:TT, 1, 0:D], lnbb[:, k, :], slot(aw_f, WO, k), start=(k == 0), stop=False)
                mm(P67[0:TT, 1, 0:D], ones[0:1, 0:TT], borow[:, :], start=False, stop=True)
                pe.wait_ge(abs_sum_done, 8)
                mm(P67[:, 1, 256:264], ones[:, :], abs_sum[:, :, :].rearrange("p n k -> p (n k)"), start=True,
                   stop=True).then_inc(setup_in_psum, 1)

            def project(pair, b, s, width, m, g, chunks):
                total = 3 * len(chunks)
                n = 0
                for k, (half, first) in enumerate(chunks):
                    v_h, v_l = (a[g][:, half, :, first:first + L] for a in (x1_h, x1_l))
                    at = s * 256 + k * width + m * 128
                    for w, v in ((aw_h, v_h), (aw_h, v_l), (aw_l, v_h)):
                        ins = mm(images(pair[:, b, 0:TG]), w[:, at:at + 128], v, start=(n == 0), stop=(n == total - 1))
                        n += 1
                return ins

            HERE = [(h, 1) for h in range(DH)]
            BEFORE = [(h, 0) for h in range(DH)]

            def gate_hidden(g):
                pe.wait_ge(x1_rest, g + 1)
                if g == 0:
                    pe.wait_ge(aw_done, 4)
                    pe.wait_ge(x_rest, KC * G)
                if g == 1:
                    pe.wait_ge(th_done, 1)
                if g >= 2:
                    pe.wait_ge(kvg_done, g)
                for m in range(DH):
                    project(g1_in(g), m, G1, D, m, g, HERE + BEFORE).then_inc(g1_in_psum, 1)

            def blend_hidden(g):
                if g == 0:
                    pe.wait_ge(u_pos_done, 2)
                    pe.wait_ge(aw_done, 11)
                if g == 1:
                    pe.wait_ge(x1_rest, G)
                if g >= 2:
                    pe.wait_ge(blend_done, g - 1)
                project(gates_in(g), 0, BH, 128, 0, g, HERE).then_inc(bh_in_psum, 1)

            def key_phases(g):
                if g == 0:
                    pe.wait_ge(hF_done, G)
                    pe.wait_ge(aw_done, 10)
                else:
                    pe.wait_ge(pos_scaled, g)
                for m in range(DH):
                    project(P23, m, KEY, D, m, g, HERE).then_inc(key_in_psum, 1)

            def pos_values(g):
                if g == 0:
                    pe.wait_ge(setup_done, 1)
                if g == 1:
                    pe.wait_ge(gate_done, 1)
                    pe.wait_ge(gc_done, 1)
                if g >= 1:
                    pe.wait_ge(u_pos_done, 2 * g)
                if g == 2:
                    pe.wait_ge(ternT_done, 4)
                if g >= 3:
                    pe.wait_ge(x2_rest, g - 1)
                for m in range(DH):
                    ins = project(P67, m, PV, D, m, g, HERE)
                ins.then_inc(pv_in_psum, 1)

            def kv_values(g):
                if g != 1:
                    pe.wait_ge(gh_done, g + 1)
                if g >= 1:
                    pe.wait_ge(kvg_done, g)
                if g >= 2:
                    pe.wait_ge(h2_done, g - 1)
                for m in range(DH):
                    ins = project(P01, m, KV, D, m, g, HERE)
                ins.then_inc(kv_in_psum, 1)

            def token_logits(g, its_tiles):
                pe.wait_ge(gh_done, g + 1)
                pe.wait_ge(bh_done, g + 1)
                for t in its_tiles:
                    s = slice(t * TT, (t + 1) * TT)
                    mm(gates_in(g)[0:TT, 1, 3 * t:3 * t + 2], bh[:, s], wb2[:, :], start=True, stop=True)
                    for k in range(DH):
                        ins = mm(gates_in(g)[0:TT, 1, 3 * t + 2:3 * t + 3], gh[:, k, s], vec[:, 15 + k:16 + k],
                                 start=(k == 0), stop=(k == DH - 1))
                    if t == NT - 1:
                        ins.then_inc(logits_in_psum, 1)

            def spread_gates(g):
                pe.wait_ge(gate_rows_done, g + 1)
                pe.wait_ge(logit_done, g + 1)
                pe.wait_ge(consts_done, 5)
                if g >= 3:
                    pe.wait_ge(ss_done, g - 2)
                mm(gates_in(g)[0:TT, 0, 0:NT], tri[:, :], recip[:, 1, :], start=True, stop=True)
                for t in range(NT):
                    ins = mm(gates_in(g)[:, 1, t * TT:(t + 1) * TT], gate_rows[:, t, :], ident[0:TT, 0:TT], start=True,
                             stop=True)
                ins.then_inc(gate_in_psum, 1)

            def ternary_to_F(parts):
                pe.wait_ge(u_pos_done, 4)
                if parts[0] > 0:
                    pe.wait_ge(z_rest, 1)
                pe.wait_ge(consts_done, 5)
                for n in parts:
                    b = P67[:, n % 2, :].bitcast(F16)
                    pe.wait_ge(tern_done, n // 2 + 1)
                    if n >= 2:
                        pe.wait_ge(ternT_done, n - 1)
                    for q in range(8):
                        if n < DH:
                            src = up_t[:, q * D + n * 128:q * D + (n + 1) * 128]
                        else:
                            f, m = (n - DH) * 4 + q // 2, q % 2
                            src = dn_t[:, m * F + f * 128:m * F + (f + 1) * 128]
                        ins = nc.tensor.transpose(b[:, q * 128:(q + 1) * 128], src, ident16[:, :])
                    ins.then_inc(ternT_in_psum, 1)

            def pos_to_T(g):
                pe.wait_ge(pos_ret_done, g + 1)
                pe.wait_ge(th_done, g + 1)
                if g == 0:
                    pe.wait_ge(gh_done, 2)
                if g == G - 1:
                    pe.wait_ge(h2_done, g)
                elif g >= 2:
                    pe.wait_ge(out_done, 2 * (g - 1))
                to_T(lambda m, t: m_pc[:, m * TG + t * TT:m * TG + (t + 1) * TT], pos_in(g)).then_inc(posT_in_psum, 1)

            def kv_to_T(g):
                after = last_group(g + 1) + 1
                pe.wait_ge(kv_ret_done, g + 1)
                pe.wait_ge(gc_done, after)
                pe.wait_ge(gate_done, after)
                if g >= 2:
                    pe.wait_ge(ss_done, g - 1)
                to_T(lambda m, t: m_kc[:, m * TG + t * TT:m * TG + (t + 1) * TT], P45).then_inc(kvT_in_psum, 1)

            def z_to_F(g):
                pe.wait_ge(zT_done, g + 1)
                pe.wait_ge(u_pos_done, 2 * (last_group(g + 1) + 1))
                if g == 0:
                    pe.wait_ge(ternT_done, 2)
                else:
                    pe.wait_ge(x2_rest, g)
                to_F(ring_T[0], P67).then_inc(zF_in_psum, 1)

            def attention_out(g):
                pe.wait_ge(z_rest, g + 1)
                pe.wait_ge(aw_done, NSLOT)
                pe.wait_ge(gh_done, last_group(g + 2) + 1)
                pe.wait_ge(kvg_done, last_group(g + 1) + 1)
                for t in range(NT):
                    n = 0
                    for k in range(DH):
                        for v, w in ((z_h, aw_h), (z_l, aw_h), (z_h, aw_l)):
                            ins = mm(tiles(P01)[:, t, :], v[:, k, t * TT:(t + 1) * TT], slot(w, WO, k), start=(n == 0),
                                     stop=(n == 3 * DH - 1))
                            n += 1
                ins.then_inc(wo_in_psum, 1)

            def x2_to_F(g):
                pe.wait_ge(x2T_done, g + 1)
                pe.wait_ge(z_rest, g + 1)
                if g == 0:
                    pe.wait_ge(u_pos_done, 6)
                to_F(ring_T[1], P67).then_inc(x2F_in_psum, 1)

            def ffn_up(g, chunks):
                pe.wait_ge(x2_rest, g + 1)
                pe.wait_ge(ternT_done, 4)
                pe.wait_ge(th_done, last_group(g + 2) + 1)
                pe.wait_ge(pos_scaled, last_group(g + 1) + 1)
                if g == G - 1:
                    pe.wait_ge(h2_done, G)
                elif g >= 1:
                    pe.wait_ge(out_done, 2 * g)
                ring = 2 * len(up_banks(g))
                for f in chunks:
                    n = FC * g + f
                    if f >= ring:
                        pe.wait_ge(gelu_done, n - ring + 1)
                    i = 0
                    for k in range(DH):
                        for v in (x2_h[g], x2_l[g]):
                            ins = mm(up_bank(g, f), upT[:, k, f * 128:(f + 1) * 128], v[:, k, :], start=(i == 0),
                                     stop=(i == 2 * DH - 1))
                            i += 1
                    ins.then_inc(up_in_psum, 1)

            def gram(g):
                pe.wait_ge(g_rest, FC * (g + 1))
                pe.wait_ge(blend_done, last_group(g + 1) + 1)
                pe.wait_ge(logit_done, last_group(g + 3) + 1)
                pe.wait_ge(ss_done, g)
                for t in range(NT):
                    o = P45[0:TT, t // 2, (t % 2) * 2 * TT:(t % 2 + 1) * 2 * TT].rearrange("p (a t) -> p a t", a=2)
                    for f in range(FC):
                        ins = mm(o, ghl[:, f, 0, t * TT:(t + 1) * TT], ghl[:, f, :, t * TT:(t + 1) * TT],
                                 start=(f == 0), stop=(f == FC - 1))
                ins.then_inc(gram_in_psum, 1)

            def ffn_down(g, its_tiles):
                pe.wait_ge(gelu_done, FC * (g + 1))
                pe.wait_ge(out_done, 2 * g)
                for t in its_tiles:
                    for f in range(FC):
                        if g == G - 1 and t == 0:
                            pe.wait_ge(g_rest, FC * g + f + 1)
                        for a in range(2):
                            ins = mm(tiles(P23)[:, t, :], ghl[:, f, a, t * TT:(t + 1) * TT], dnT[:, f, :],
                                     start=(f == 0 and a == 0), stop=(f == FC - 1 and a == 1))
                    if t % 2 == 1:
                        ins.then_inc(down_in_psum, 1)

            ahead = {0: (), 1: (2,), 2: (3,), 3: (4,), 4: (5,), 5: (6, 7), 6: (8, 9)}
            x_transposes(0, 0)
            x_transposes(0, 1)
            for g in range(G):
                for j in range(KC):
                    n = g * KC + j
                    for k in ahead.get(n, (n + AHEAD,)):
                        if k < KC * G:
                            x_transposes(k // KC, k % KC)
                    embed(g, j)
                    if g == 0 and j == 3:
                        vector_columns()
                    if j == 3 and g >= 2:
                        x1_to_F(g - 2)
                    if j == 4 and g >= 1:
                        h_to_T(g - 1)

            for i in range(G + 2):
                a, t, f = i, i - 1, i - 2
                if a == 0:
                    gate_hidden(0)
                    setup()
                    x1_to_F(G - 2)
                    pos_values(0)
                    h_to_T(G - 1)
                    key_phases(0)
                    blend_hidden(0)
                    kv_values(0)
                    token_logits(0, range(NT))
                    gate_hidden(1)
                    x1_to_F(G - 1)
                    spread_gates(0)
                    blend_hidden(1)
                    kv_values(1)
                    token_logits(1, range(NT))
                    pos_values(1)
                    continue
                if i == 2:
                    spread_gates(2)
                    pos_to_T(1)
                if 2 <= a < G:
                    kv_values(a)
                    if i == 3:
                        spread_gates(a)
                if 0 <= f < G - 1 and i != 2:
                    x2_to_F(f)
                if 0 <= t < G - 1 and i != 2:
                    pos_to_T(t)
                if i == 1:
                    spread_gates(1)
                if 2 <= a < G:
                    pos_values(a)
                if a < G:
                    key_phases(a)
                if 0 <= t < G - 1:
                    kv_to_T(t)
                if i == 1:
                    ternary_to_F(range(0, 2))
                if i == 2:
                    x2_to_F(0)
                if i < 3:
                    gate_hidden(a + 1)
                if 0 <= f < G:
                    ffn_up(f, range(0, split(i)))
                if 0 <= t < G:
                    z_to_F(t)
                if a + 1 < G:
                    blend_hidden(a + 1)
                for k in range(split(i), FC):
                    if 0 <= f < G:
                        ffn_up(f, range(k, k + 1))
                    if a + 1 < G:
                        token_logits(a + 1, range(k - split(i), k - split(i) + 1))
                if 0 <= t < G:
                    attention_out(t)
                if i == 1:
                    ternary_to_F(range(2, 4))
                if i == G + 1:
                    ffn_down(f, range(0, 1))
                if 0 <= f < G:
                    gram(f)
                if i == G - 1:
                    pos_to_T(G - 1)
                if 0 <= f < G:
                    ffn_down(f, range(0 if i <= G else 1, NT // 2))
                if i == G - 1:
                    kv_to_T(G - 1)
                if i == G:
                    x2_to_F(G - 1)
                if 0 <= f < G:
                    ffn_down(f, range(NT // 2, NT))


_INS = ["x", "L0_tok_W", "L0_tok_b", "L0_attn_pos_phases", "L0_attn_Wpv", "L0_attn_bpv", "L0_attn_Wk", "L0_attn_bk",
        "L0_attn_Wkv", "L0_attn_bkv", "L0_attn_Wg1", "L0_attn_bg1", "L0_attn_Wg2", "L0_attn_bg2", "L0_attn_Wb1",
        "L0_attn_bb1", "L0_attn_Wb2", "L0_attn_bb2", "L0_attn_ln_g", "L0_attn_ln_b", "L0_attn_Wo", "L0_attn_bo",
        "L0_ffn_w_up", "L0_ffn_w_down"]
_OUTS = [((32, 49, 256), "float32")]


def kernel(**inputs):
    import numpy as _np
    import concourse.bacc as _bacc
    from concourse import mybir as _mybir
    from concourse.bass_utils import run_bass_kernel_spmd as _run

    nc = _bacc.Bacc("TRN2", target_bir_lowering=False, num_devices=1)
    arrays, args = {}, []
    for name in _INS:
        a = _np.ascontiguousarray(inputs[name])
        arrays[f"in_{name}_dram"] = a
        args.append(nc.dram_tensor(f"in_{name}_dram", a.shape, _mybir.dt.from_np(a.dtype), kind="ExternalInput").ap())
    for i, (shape, dtype) in enumerate(_OUTS):
        dt = _mybir.dt.from_np(_np.dtype(dtype))
        args.append(nc.dram_tensor(f"out_{i}_dram", shape, dt, kind="ExternalOutput").ap())
    vit_block_program(nc, *args)
    r = _run(nc, [arrays], core_ids=[0])
    return r.results[0]["out_0_dram"]
```
